# Optimizing a Trainium2 kernel written in Bass

```python
import numpy as np
import jax
import jax.numpy as jnp

def _softmax(x, axis=-1):
    return jax.nn.softmax(x, axis=axis)

def _gelu(x):
    return jax.nn.gelu(x, approximate=True)

def _silu(x):
    return jax.nn.silu(x)

def _sigmoid(x):
    return jax.nn.sigmoid(x)

def _layernorm(x, axis=-1, eps=1e-05):
    m = jnp.mean(x, axis=axis, keepdims=True)
    v = jnp.var(x, axis=axis, keepdims=True)
    return (x - m) / jnp.sqrt(v + eps)

def _scatter_add(tgt, idx, src, axis=0):
    return tgt.at[idx].add(src)

def _segment_sum(src, seg, n):
    return jax.ops.segment_sum(src, seg, n)
kernel_name = 'mk_decoder_preln_d4_seqx_r8_79ee2e'

def setup_inputs(seed: int=0):
    np.random.seed(seed)
    _w = jnp.asarray

    def _rec_inputs():
        import jax
        import jax.numpy as jnp
        _rk = jax.random.key(seed)
        x = 7.22e-05 + 1 * jax.random.normal(jax.random.fold_in(_rk, 1), (16, 128, 256), jnp.float32)
        _lenS = 128 - jax.random.randint(jax.random.fold_in(_rk, 7), (16,), 0, max(1, 128 // 4) + 1, jnp.int32)
        _lenS2 = 128 - jax.random.randint(jax.random.fold_in(_rk, 8), (16,), 0, max(1, 128 // 4) + 1, jnp.int32)
        _ctx_1024P = jax.random.normal(jax.random.fold_in(_rk, 11), (16, 16, 128), jnp.float32)
        _ctx_1024c = jax.random.dirichlet(jax.random.fold_in(_rk, 511), 0.3 * jnp.ones((16,), jnp.float32), (16, 128))
        _ctx_1024t = jnp.einsum('bsk,bkd->bsd', _ctx_1024c, _ctx_1024P)
        _ctx_1024t = _ctx_1024t * jax.lax.rsqrt(jnp.mean(jnp.square(_ctx_1024t)) + 1e-12) * 0.953939
        ctx_1024 = -1.39393e-06 + 0.999914 * (_ctx_1024t + 0.3 * jax.random.normal(jax.random.fold_in(_rk, 611), (16, 128, 128), jnp.float32))
        fside_BxSx2_0 = jax.random.uniform(jax.random.fold_in(_rk, 12), (16, 128, 2), jnp.float32, 0.0, 0.999707)
        _validS = jnp.arange(128)[None, :] < _lenS[:, None]
        _validS2 = jnp.arange(128)[None, :] < _lenS2[:, None]
        _causal = jnp.tril(jnp.ones((128, 128), dtype=bool))
        mask_BxS2_bf1 = jnp.ones((16, 128), dtype=bool)
        return (x, ctx_1024, fside_BxSx2_0, mask_BxS2_bf1)
    x, ctx_1024, fside_BxSx2_0, mask_BxS2_bf1 = _rec_inputs()

    def _L0_attn_setup():
        import jax, jax.numpy as jnp
        import numpy as np
        HID = 256
        HEADS = 16
        HD = HID // HEADS
        EPS = 1e-06

        def _heads(x, b, s):
            return x.reshape(b, s, HEADS, HD).transpose(0, 2, 1, 3)
        key = jax.random.key(seed)
        ks = jax.random.split(key, 9)
        s = 1.0 / np.sqrt(HID)
        return {'hidden_states': jax.random.normal(ks[0], (4, 512, HID), jnp.float32), 'q_w': jax.random.normal(ks[1], (HID, HID), jnp.float32) * s, 'q_b': jnp.zeros((HID,), jnp.float32), 'k_w': jax.random.normal(ks[2], (HID, HID), jnp.float32) * s, 'k_b': jnp.zeros((HID,), jnp.float32), 'v_w': jax.random.normal(ks[3], (HID, HID), jnp.float32) * s, 'v_b': jnp.zeros((HID,), jnp.float32), 'o_w': jax.random.normal(ks[4], (HID, HID), jnp.float32) * s, 'o_b': jnp.zeros((HID,), jnp.float32)}
    _L0_attn_all = _L0_attn_setup()
    _L0_attn_in = {k: v for k, v in _L0_attn_all.items() if k in ('q_w', 'q_b', 'k_w', 'k_b', 'v_w', 'v_b', 'o_w', 'o_b')}
    del _L0_attn_all

    def _L0_xattn_setup():
        import jax, jax.numpy as jnp
        import numpy as np
        DIM = 256
        CTX_DIM = 128
        N_HEADS = 32
        HEAD_DIM = DIM // N_HEADS
        POS_DIM = 2
        B, N, CTXN = (2, 256, 256)
        ROPE_BASE = 10000.0

        def apply_axial_rope(x, pos):
            b, n, h, d = x.shape
            p = pos.shape[-1]
            dpa = d // p
            half = dpa // 2
            freqs = ROPE_BASE ** (-jnp.arange(half, dtype=x.dtype) / half)
            ang = pos[..., :, None] * freqs
            cos = jnp.cos(ang)[:, :, None, :, :]
            sin = jnp.sin(ang)[:, :, None, :, :]
            xr = x.reshape(b, n, h, p, half, 2)
            x1, x2 = (xr[..., 0], xr[..., 1])
            out = jnp.stack([x1 * cos - x2 * sin, x1 * sin + x2 * cos], axis=-1)
            return out.reshape(b, n, h, d)
        key = jax.random.key(seed)
        ks = jax.random.split(key, 8)
        x = jax.random.normal(ks[0], (B, N, DIM), jnp.float32)
        ctx = jax.random.normal(ks[1], (B, CTXN, CTX_DIM), jnp.float32)
        pos_map = jax.random.uniform(ks[2], (B, N, POS_DIM), jnp.float32)
        ctx_pos_map = jax.random.uniform(ks[3], (B, CTXN, POS_DIM), jnp.float32)
        Wq = jax.random.normal(ks[4], (DIM, DIM), jnp.float32) / np.sqrt(DIM)
        Wkv = jax.random.normal(ks[5], (CTX_DIM, 2 * DIM), jnp.float32) / np.sqrt(CTX_DIM)
        Wout = jax.random.normal(ks[6], (DIM, DIM), jnp.float32) / np.sqrt(DIM)
        bout = jnp.zeros((DIM,), jnp.float32)
        return {'x': x, 'ctx': ctx, 'pos_map': pos_map, 'ctx_pos_map': ctx_pos_map, 'Wq': Wq, 'Wkv': Wkv, 'Wout': Wout, 'bout': bout}
    _L0_xattn_all = _L0_xattn_setup()
    _L0_xattn_in = {k: v for k, v in _L0_xattn_all.items() if k in ('Wq', 'Wkv', 'Wout', 'bout')}
    del _L0_xattn_all

    def _L0_ffn_setup():
        import jax, jax.numpy as jnp
        import numpy as np
        HIDDEN = 256
        INTER = 688
        LUT_SIZE = 16

        def _ghost_linear(x, idx, lut):
            w = lut[idx]
            return jnp.einsum('bsh,oh->bso', x, w)
        key = jax.random.key(seed)
        k_x, k_lut, k_g, k_u, k_d = jax.random.split(key, 5)
        x = jax.random.normal(k_x, (2, 512, HIDDEN), dtype=jnp.float32)
        lut = jax.random.normal(k_lut, (LUT_SIZE,), dtype=jnp.float32) * 0.02
        gate_idx = jax.random.randint(k_g, (INTER, HIDDEN), 0, LUT_SIZE, dtype=jnp.int32)
        up_idx = jax.random.randint(k_u, (INTER, HIDDEN), 0, LUT_SIZE, dtype=jnp.int32)
        down_idx = jax.random.randint(k_d, (HIDDEN, INTER), 0, LUT_SIZE, dtype=jnp.int32)
        return {'x': x, 'lut': lut, 'gate_idx': gate_idx, 'up_idx': up_idx, 'down_idx': down_idx}
    _L0_ffn_all = _L0_ffn_setup()
    _L0_ffn_in = {k: v for k, v in _L0_ffn_all.items() if k in ('lut', 'gate_idx', 'up_idx', 'down_idx')}
    del _L0_ffn_all

    def _L1_attn_setup():
        import jax, jax.numpy as jnp
        import numpy as np
        N_Q, N_KV = (16, 4)

        def _rope(x):
            d = x.shape[-1]
            T = x.shape[-2]
            inv_freq = 1.0 / 10000.0 ** (jnp.arange(d // 2, dtype=jnp.float32) * 2.0 / d)
            emb = jnp.arange(T, dtype=jnp.float32)[:, None] * inv_freq[None, :]
            cos, sin = (jnp.cos(emb), jnp.sin(emb))
            x1, x2 = (x[..., 0::2], x[..., 1::2])
            return jnp.concatenate([x1 * cos - x2 * sin, x1 * sin + x2 * cos], axis=-1)
        key = jax.random.key(seed)
        ks = jax.random.split(key, 5)
        B, T, C = (4, 256, 256)
        g = N_Q // N_KV
        Ckv = C // g
        s = 0.02
        return {'x': jax.random.normal(ks[0], (B, T, C), dtype=jnp.float32), 'Wq': jax.random.normal(ks[1], (C, C), dtype=jnp.float32) * s, 'bq': jnp.zeros((C,), dtype=jnp.float32), 'Wk': jax.random.normal(ks[2], (C, Ckv), dtype=jnp.float32) * s, 'bk': jnp.zeros((Ckv,), dtype=jnp.float32), 'Wv': jax.random.normal(ks[3], (C, Ckv), dtype=jnp.float32) * s, 'bv': jnp.zeros((Ckv,), dtype=jnp.float32), 'Wo': jax.random.normal(ks[4], (Ckv, C), dtype=jnp.float32) * s, 'bo': jnp.zeros((C,), dtype=jnp.float32)}
    _L1_attn_all = _L1_attn_setup()
    _L1_attn_in = {k: v for k, v in _L1_attn_all.items() if k in ('Wq', 'bq', 'Wk', 'bk', 'Wv', 'bv', 'Wo', 'bo')}
    del _L1_attn_all

    def _L1_xattn_setup():
        import jax, jax.numpy as jnp
        import numpy as np
        N_HEADS = 16
        N_KV_HEADS = 8
        HEAD_DIM = 128
        D_TEXT = 256
        D_VISION = 128
        GROUPS = N_HEADS // N_KV_HEADS
        key = jax.random.key(seed)
        ks = jax.random.split(key, 6)
        B, T_text, T_vis = (4, 256, 72)
        text_hidden = jax.random.normal(ks[0], (B, T_text, D_TEXT), dtype=jnp.float32)
        vision_tokens = jax.random.normal(ks[1], (B, T_vis, D_VISION), dtype=jnp.float32)
        vision_mask = jnp.ones((B, T_vis), dtype=bool)
        s = 0.02
        Wq = jax.random.normal(ks[2], (D_TEXT, N_HEADS * HEAD_DIM), dtype=jnp.float32) * s
        Wk = jax.random.normal(ks[3], (D_VISION, N_KV_HEADS * HEAD_DIM), dtype=jnp.float32) * s
        Wv = jax.random.normal(ks[4], (D_VISION, N_KV_HEADS * HEAD_DIM), dtype=jnp.float32) * s
        Wo = jax.random.normal(ks[5], (N_HEADS * HEAD_DIM, D_TEXT), dtype=jnp.float32) * s
        return {'text_hidden': text_hidden, 'vision_tokens': vision_tokens, 'vision_mask': vision_mask, 'Wq': Wq, 'Wk': Wk, 'Wv': Wv, 'Wo': Wo}
    _L1_xattn_all = _L1_xattn_setup()
    _L1_xattn_in = {k: v for k, v in _L1_xattn_all.items() if k in ('Wq', 'Wk', 'Wv', 'Wo')}
    del _L1_xattn_all

    def _L1_ffn_setup():
        import math
        import jax, jax.numpy as jnp
        import numpy as np
        from jax import lax
        D = 256
        I = 128
        E = 32
        K = 4
        NG = 8
        TKG = 3
        NSH = 2
        SCALE = 2.5
        CF = 1.25
        B, S = (2, 256)

        def _router(x, router_w, e_bias):
            scores = jax.nn.sigmoid(x @ router_w.T)
            sc = scores + e_bias[None, :]
            T = x.shape[0]
            gs = sc.reshape(T, NG, E // NG)
            group_scores = lax.top_k(gs, 2)[0].sum(-1)
            _, gidx = lax.top_k(group_scores, TKG)
            gmask = jnp.zeros((T, NG), sc.dtype).at[jnp.arange(T)[:, None], gidx].set(1.0)
            smask = jnp.repeat(gmask, E // NG, axis=1)
            masked = jnp.where(smask > 0, sc, 0.0)
            _, topk_idx = lax.top_k(masked, K)
            topk_w = jnp.take_along_axis(scores, topk_idx, axis=1)
            topk_w = topk_w / (topk_w.sum(-1, keepdims=True) + 1e-20)
            topk_w = topk_w * SCALE
            return (topk_idx.astype(jnp.int32), topk_w)

        def _moe_forward(hidden_states, router_w, e_bias, W_gate, W_up, W_down, shared_gate, shared_up, shared_down):
            b, s, d = hidden_states.shape
            T = b * s
            C = int(math.ceil(CF * T / E))
            EC = E * C
            x = hidden_states.reshape(T, d)
            topk_idx, topk_w = _router(x, router_w, e_bias)
            expert_flat = topk_idx.reshape(-1)
            w_flat = topk_w.reshape(-1)
            tok_flat = jnp.repeat(jnp.arange(T, dtype=jnp.int32), K)
            sort_ix = jnp.argsort(expert_flat)
            e_sorted = expert_flat[sort_ix]
            tok_s = tok_flat[sort_ix]
            w_s = w_flat[sort_ix]
            counts = jnp.zeros(E, jnp.int32).at[e_sorted].add(1)
            group_start = jnp.concatenate([jnp.zeros(1, jnp.int32), jnp.cumsum(counts)[:-1].astype(jnp.int32)])
            pos = jnp.arange(T * K, dtype=jnp.int32) - group_start[e_sorted]
            valid = pos < C
            dest = e_sorted * C + jnp.where(valid, pos, 0)
            slots_token = jnp.zeros(EC, jnp.int32).at[dest].add(jnp.where(valid, tok_s, 0))
            slots_w = jnp.zeros(EC, w_s.dtype).at[dest].add(jnp.where(valid, w_s, 0.0))
            Xp = x[slots_token].reshape(E, C, d)
            G = jnp.einsum('ecd,edi->eci', Xp, W_gate)
            U = jnp.einsum('ecd,edi->eci', Xp, W_up)
            Y = jnp.einsum('eci,eid->ecd', jax.nn.silu(G) * U, W_down)
            Yf = Y.reshape(EC, d) * slots_w[:, None]
            out = jnp.zeros((T, d), x.dtype).at[slots_token].add(Yf)
            shared = jax.nn.silu(x @ shared_gate.T) * (x @ shared_up.T) @ shared_down.T
            return (out + shared).reshape(b, s, d)
        key = jax.random.key(seed)
        ks = jax.random.split(key, 8)

        def rn(k, shape, scale=0.02):
            return jax.random.normal(k, shape, jnp.float32) * scale
        return {'hidden_states': jax.random.normal(ks[0], (B, S, D), jnp.float32), 'router_w': rn(ks[1], (E, D)), 'e_bias': jnp.zeros((E,), jnp.float32), 'W_gate': rn(ks[2], (E, D, I)), 'W_up': rn(ks[3], (E, D, I)), 'W_down': rn(ks[4], (E, I, D)), 'shared_gate': rn(ks[5], (I * NSH, D)), 'shared_up': rn(ks[6], (I * NSH, D)), 'shared_down': rn(ks[7], (D, I * NSH))}
    _L1_ffn_all = _L1_ffn_setup()
    _L1_ffn_in = {k: v for k, v in _L1_ffn_all.items() if k in ('router_w', 'e_bias', 'W_gate', 'W_up', 'W_down', 'shared_gate', 'shared_up', 'shared_down')}
    del _L1_ffn_all

    def _L2_attn_setup():
        import jax, jax.numpy as jnp
        import numpy as np
        B, S, D = (2, 256, 256)
        H, KVH = (16, 4)
        HD = D // H
        KVD = KVH * HD
        BASE = 10000.0
        EPS = 1.1920929e-07

        def _rms_norm(t):
            return t * jax.lax.rsqrt(jnp.mean(t * t, axis=-1, keepdims=True) + EPS)

        def _rope_tables(s, dtype):
            inv_freq = 1.0 / BASE ** (jnp.arange(0, HD, 2, dtype=jnp.float32) / HD)
            t = jnp.arange(s, dtype=jnp.float32)
            freqs = jnp.outer(t, inv_freq)
            cos = jnp.cos(freqs)[None, None].astype(dtype)
            sin = jnp.sin(freqs)[None, None].astype(dtype)
            return (cos, sin)

        def _apply_rope(t, cos, sin):
            half = t.shape[-1] // 2
            t1, t2 = (t[..., :half], t[..., half:])
            return jnp.concatenate([t1 * cos + t2 * sin, -t1 * sin + t2 * cos], axis=-1)
        key = jax.random.key(seed)
        ks = jax.random.split(key, 9)
        sd = 1.0 / np.sqrt(D)
        x = jax.random.normal(ks[0], (B, S, D), jnp.float32)
        Wq = jax.random.normal(ks[1], (D, D), jnp.float32) * sd
        bq = jnp.zeros((D,), jnp.float32)
        Wk = jax.random.normal(ks[2], (KVD, D), jnp.float32) * sd
        bk = jnp.zeros((KVD,), jnp.float32)
        Wv = jax.random.normal(ks[3], (KVD, D), jnp.float32) * sd
        bv = jnp.zeros((KVD,), jnp.float32)
        Wo = jax.random.normal(ks[4], (D, D), jnp.float32) * sd
        bo = jnp.zeros((D,), jnp.float32)
        q_gain = jnp.ones((H,), jnp.float32)
        return {'x': x, 'Wq': Wq, 'bq': bq, 'Wk': Wk, 'bk': bk, 'Wv': Wv, 'bv': bv, 'Wo': Wo, 'bo': bo, 'q_gain': q_gain}
    _L2_attn_all = _L2_attn_setup()
    _L2_attn_in = {k: v for k, v in _L2_attn_all.items() if k in ('Wq', 'bq', 'Wk', 'bk', 'Wv', 'bv', 'Wo', 'bo', 'q_gain')}
    del _L2_attn_all

    def _L2_xattn_setup():
        import jax, jax.numpy as jnp
        import numpy as np
        B, S1, S2, DCA = (2, 256, 128, 16)
        QDIM, KDIM, H = (256, 128, 16)
        HD = QDIM // H
        SCALE = HD ** (-0.5)
        EPS = 1e-06
        DCA_WEIGHT = 1.0

        def _ln(t, w, b):
            m = jnp.mean(t, axis=-1, keepdims=True)
            v = jnp.var(t, axis=-1, keepdims=True)
            return (t - m) * jax.lax.rsqrt(v + EPS) * w + b

        def _attn(q, k, v):
            s = jnp.einsum('bhqd,bhkd->bhqk', q, k) * SCALE
            p = jax.nn.softmax(s, axis=-1)
            return jnp.einsum('bhqk,bhkd->bhqd', p, v)
        key = jax.random.key(seed)
        ks = jax.random.split(key, 8)
        w = lambda k, shape: jax.random.normal(k, shape, jnp.float32) * 0.02
        return {'x': jax.random.normal(ks[0], (B, S1, QDIM), jnp.float32), 'y': jax.random.normal(ks[1], (B, S2 + DCA, KDIM), jnp.float32), 'Wq': w(ks[2], (QDIM, QDIM)), 'bq': jnp.zeros((QDIM,), jnp.float32), 'Wk': w(ks[3], (KDIM, QDIM)), 'bk': jnp.zeros((QDIM,), jnp.float32), 'Wv': w(ks[4], (KDIM, QDIM)), 'bv': jnp.zeros((QDIM,), jnp.float32), 'Wkv_dca': w(ks[5], (KDIM, 2 * QDIM)), 'bkv_dca': jnp.zeros((2 * QDIM,), jnp.float32), 'qn_w': jnp.ones((HD,), jnp.float32), 'qn_b': jnp.zeros((HD,), jnp.float32), 'kn_w': jnp.ones((HD,), jnp.float32), 'kn_b': jnp.zeros((HD,), jnp.float32), 'kn_dca_w': jnp.ones((HD,), jnp.float32), 'kn_dca_b': jnp.zeros((HD,), jnp.float32), 'Wo': w(ks[6], (QDIM, QDIM)), 'bo': jnp.zeros((QDIM,), jnp.float32)}
    _L2_xattn_all = _L2_xattn_setup()
    _L2_xattn_in = {k: v for k, v in _L2_xattn_all.items() if k in ('Wq', 'bq', 'Wk', 'bk', 'Wv', 'bv', 'Wkv_dca', 'bkv_dca', 'qn_w', 'qn_b', 'kn_w', 'kn_b', 'kn_dca_w', 'kn_dca_b', 'Wo', 'bo')}
    del _L2_xattn_all

    def _L2_ffn_setup():
        import jax, jax.numpy as jnp
        import numpy as np
        B, S, D = (4, 256, 256)
        E, F = (8, 176)
        FS = 352
        TOP_K = 2
        INIT = 0.02
        key = jax.random.key(seed)
        ks = jax.random.split(key, 8)
        return {'x': jax.random.normal(ks[0], (B, S, D), dtype=jnp.float32), 'w_router': jax.random.normal(ks[1], (D, E), dtype=jnp.float32) * INIT, 'w1': jax.random.normal(ks[2], (E, D, F), dtype=jnp.float32) * INIT, 'w2': jax.random.normal(ks[3], (E, F, D), dtype=jnp.float32) * INIT, 'w3': jax.random.normal(ks[4], (E, D, F), dtype=jnp.float32) * INIT, 'ws1': jax.random.normal(ks[5], (D, FS), dtype=jnp.float32) * INIT, 'ws2': jax.random.normal(ks[6], (FS, D), dtype=jnp.float32) * INIT, 'ws3': jax.random.normal(ks[7], (D, FS), dtype=jnp.float32) * INIT}
    _L2_ffn_all = _L2_ffn_setup()
    _L2_ffn_in = {k: v for k, v in _L2_ffn_all.items() if k in ('w_router', 'w1', 'w2', 'w3', 'ws1', 'ws2', 'ws3')}
    del _L2_ffn_all

    def _L3_attn_setup():
        import math
        import jax, jax.numpy as jnp
        import numpy as np
        HEAD_DIM = 128
        NUM_HEADS = 16
        ROPE_BASE = 10000.0

        def _rope_tables(seq_len, dim, dtype):
            inv_freq = 1.0 / ROPE_BASE ** (jnp.arange(0, dim, 2, dtype=jnp.float32) / dim)
            t = jnp.arange(seq_len, dtype=jnp.float32)
            freqs = jnp.einsum('i,j->ij', t, inv_freq)
            emb = jnp.concatenate([freqs, freqs], axis=-1)
            return (jnp.cos(emb).astype(dtype), jnp.sin(emb).astype(dtype))

        def _rotate_half(x):
            x1, x2 = jnp.split(x, 2, axis=-1)
            return jnp.concatenate([-x2, x1], axis=-1)

        def _apply_rope(x, cos, sin):
            return x * cos[None, :, None, :] + _rotate_half(x) * sin[None, :, None, :]
        key = jax.random.key(seed)
        k1, k2, k3 = jax.random.split(key, 3)
        B, S, dim = (2, 256, 256)
        out_dim = (NUM_HEADS + 2 * NUM_HEADS) * HEAD_DIM
        x = jax.random.normal(k1, (B, S, dim), dtype=jnp.float32)
        w_qkv = jax.random.normal(k2, (out_dim, dim), dtype=jnp.float32) * 0.02
        w_out = jax.random.normal(k3, (dim, NUM_HEADS * HEAD_DIM), dtype=jnp.float32) * 0.02
        return {'x': x, 'w_qkv': w_qkv, 'w_out': w_out}
    _L3_attn_all = _L3_attn_setup()
    _L3_attn_in = {k: v for k, v in _L3_attn_all.items() if k in ('w_qkv', 'w_out')}
    del _L3_attn_all

    def _L3_xattn_setup():
        import jax, jax.numpy as jnp
        import numpy as np
        EPS = 1e-05

        def rmsnorm(x, g, eps=EPS):
            var = jnp.mean(jnp.square(x), axis=-1, keepdims=True)
            return x * jax.lax.rsqrt(var + eps) * g
        key = jax.random.key(seed)
        ks = jax.random.split(key, 8)
        B, Sq, Skv = (2, 512, 64)
        dim, cdim, H, D = (256, 128, 16, 128)
        inner = H * D
        s = lambda f: 1.0 / np.sqrt(f)
        return {'hidden_states': jax.random.normal(ks[0], (B, Sq, dim), jnp.float32), 'encoder_hidden_states': jax.random.normal(ks[1], (B, Skv, cdim), jnp.float32), 'Wq': jax.random.normal(ks[2], (dim, inner), jnp.float32) * s(dim), 'Wk': jax.random.normal(ks[3], (cdim, inner), jnp.float32) * s(cdim), 'Wv': jax.random.normal(ks[4], (cdim, inner), jnp.float32) * s(cdim), 'Wo': jax.random.normal(ks[5], (inner, dim), jnp.float32) * s(inner), 'gq': jnp.ones((D,), jnp.float32), 'gk': jnp.ones((D,), jnp.float32)}
    _L3_xattn_all = _L3_xattn_setup()
    _L3_xattn_in = {k: v for k, v in _L3_xattn_all.items() if k in ('Wq', 'Wk', 'Wv', 'Wo', 'gq', 'gk')}
    del _L3_xattn_all

    def _L3_ffn_setup():
        import jax, jax.numpy as jnp
        import numpy as np
        HIDDEN = 256
        MOE_INTER = 128
        SHARED_INTER = 512
        N_EXPERTS = 16
        TOP_K = 2
        N_GROUP = 4
        TOPK_GROUP = 2
        NORM_TOPK_PROB = True
        ROUTED_SCALING = 1.0

        def relu2(x):
            r = jax.nn.relu(x)
            return r * r

        def _get_topk_indices(scores, e_bias):
            T, E = scores.shape
            s = scores + e_bias[None, :]
            gsz = E // N_GROUP
            group_scores = jax.lax.top_k(s.reshape(T, N_GROUP, gsz), 2)[0].sum(-1)
            group_idx = jax.lax.top_k(group_scores, TOPK_GROUP)[1]
            group_mask = jnp.zeros((T, N_GROUP), dtype=bool).at[jnp.arange(T)[:, None], group_idx].set(True)
            score_mask = jnp.repeat(group_mask, gsz, axis=1)
            masked = jnp.where(score_mask, s, 0.0)
            topk_indices = jax.lax.top_k(masked, TOP_K)[1]
            return jax.lax.stop_gradient(topk_indices)

        def _router(x_flat, router_weight, e_bias):
            logits = jnp.einsum('th,eh->te', x_flat.astype(jnp.float32), router_weight.astype(jnp.float32))
            scores = jax.nn.sigmoid(logits)
            topk_indices = _get_topk_indices(scores, e_bias)
            topk_weights = jnp.take_along_axis(scores, topk_indices, axis=1)
            if NORM_TOPK_PROB:
                topk_weights = topk_weights / (topk_weights.sum(-1, keepdims=True) + 1e-20)
            return (topk_indices, topk_weights * ROUTED_SCALING)
        key = jax.random.key(seed)
        ks = jax.random.split(key, 6)
        s = 0.02
        hidden_states = jax.random.normal(ks[0], (1, 256, HIDDEN), dtype=jnp.float32)
        router_weight = jax.random.normal(ks[1], (N_EXPERTS, HIDDEN), dtype=jnp.float32) * s
        e_bias = jnp.zeros((N_EXPERTS,), dtype=jnp.float32)
        w_up = jax.random.normal(ks[2], (N_EXPERTS, HIDDEN, MOE_INTER), dtype=jnp.float32) * s
        w_down = jax.random.normal(ks[3], (N_EXPERTS, MOE_INTER, HIDDEN), dtype=jnp.float32) * s
        shared_up = jax.random.normal(ks[4], (HIDDEN, SHARED_INTER), dtype=jnp.float32) * s
        shared_down = jax.random.normal(ks[5], (SHARED_INTER, HIDDEN), dtype=jnp.float32) * s
        return {'hidden_states': hidden_states, 'router_weight': router_weight, 'e_bias': e_bias, 'w_up': w_up, 'w_down': w_down, 'shared_up': shared_up, 'shared_down': shared_down}
    _L3_ffn_all = _L3_ffn_setup()
    _L3_ffn_in = {k: v for k, v in _L3_ffn_all.items() if k in ('router_weight', 'e_bias', 'w_up', 'w_down', 'shared_up', 'shared_down')}
    del _L3_ffn_all
    return {'x': x, 'ctx_1024': ctx_1024, 'fside_BxSx2_0': fside_BxSx2_0, 'mask_BxS2_bf1': mask_BxS2_bf1, 'L0_attn_q_w': _L0_attn_in['q_w'], 'L0_attn_q_b': _L0_attn_in['q_b'], 'L0_attn_k_w': _L0_attn_in['k_w'], 'L0_attn_k_b': _L0_attn_in['k_b'], 'L0_attn_v_w': _L0_attn_in['v_w'], 'L0_attn_v_b': _L0_attn_in['v_b'], 'L0_attn_o_w': _L0_attn_in['o_w'], 'L0_attn_o_b': _L0_attn_in['o_b'], 'L0_xattn_Wq': _L0_xattn_in['Wq'], 'L0_xattn_Wkv': _L0_xattn_in['Wkv'], 'L0_xattn_Wout': _L0_xattn_in['Wout'], 'L0_xattn_bout': _L0_xattn_in['bout'], 'L0_ffn_lut': _L0_ffn_in['lut'], 'L0_ffn_gate_idx': _L0_ffn_in['gate_idx'], 'L0_ffn_up_idx': _L0_ffn_in['up_idx'], 'L0_ffn_down_idx': _L0_ffn_in['down_idx'], 'L1_attn_Wq': _L1_attn_in['Wq'], 'L1_attn_bq': _L1_attn_in['bq'], 'L1_attn_Wk': _L1_attn_in['Wk'], 'L1_attn_bk': _L1_attn_in['bk'], 'L1_attn_Wv': _L1_attn_in['Wv'], 'L1_attn_bv': _L1_attn_in['bv'], 'L1_attn_Wo': _L1_attn_in['Wo'], 'L1_attn_bo': _L1_attn_in['bo'], 'L1_xattn_Wq': _L1_xattn_in['Wq'], 'L1_xattn_Wk': _L1_xattn_in['Wk'], 'L1_xattn_Wv': _L1_xattn_in['Wv'], 'L1_xattn_Wo': _L1_xattn_in['Wo'], 'L1_ffn_router_w': _L1_ffn_in['router_w'], 'L1_ffn_e_bias': _L1_ffn_in['e_bias'], 'L1_ffn_W_gate': _L1_ffn_in['W_gate'], 'L1_ffn_W_up': _L1_ffn_in['W_up'], 'L1_ffn_W_down': _L1_ffn_in['W_down'], 'L1_ffn_shared_gate': _L1_ffn_in['shared_gate'], 'L1_ffn_shared_up': _L1_ffn_in['shared_up'], 'L1_ffn_shared_down': _L1_ffn_in['shared_down'], 'L2_attn_Wq': _L2_attn_in['Wq'], 'L2_attn_bq': _L2_attn_in['bq'], 'L2_attn_Wk': _L2_attn_in['Wk'], 'L2_attn_bk': _L2_attn_in['bk'], 'L2_attn_Wv': _L2_attn_in['Wv'], 'L2_attn_bv': _L2_attn_in['bv'], 'L2_attn_Wo': _L2_attn_in['Wo'], 'L2_attn_bo': _L2_attn_in['bo'], 'L2_attn_q_gain': _L2_attn_in['q_gain'], 'L2_xattn_Wq': _L2_xattn_in['Wq'], 'L2_xattn_bq': _L2_xattn_in['bq'], 'L2_xattn_Wk': _L2_xattn_in['Wk'], 'L2_xattn_bk': _L2_xattn_in['bk'], 'L2_xattn_Wv': _L2_xattn_in['Wv'], 'L2_xattn_bv': _L2_xattn_in['bv'], 'L2_xattn_Wkv_dca': _L2_xattn_in['Wkv_dca'], 'L2_xattn_bkv_dca': _L2_xattn_in['bkv_dca'], 'L2_xattn_qn_w': _L2_xattn_in['qn_w'], 'L2_xattn_qn_b': _L2_xattn_in['qn_b'], 'L2_xattn_kn_w': _L2_xattn_in['kn_w'], 'L2_xattn_kn_b': _L2_xattn_in['kn_b'], 'L2_xattn_kn_dca_w': _L2_xattn_in['kn_dca_w'], 'L2_xattn_kn_dca_b': _L2_xattn_in['kn_dca_b'], 'L2_xattn_Wo': _L2_xattn_in['Wo'], 'L2_xattn_bo': _L2_xattn_in['bo'], 'L2_ffn_w_router': _L2_ffn_in['w_router'], 'L2_ffn_w1': _L2_ffn_in['w1'], 'L2_ffn_w2': _L2_ffn_in['w2'], 'L2_ffn_w3': _L2_ffn_in['w3'], 'L2_ffn_ws1': _L2_ffn_in['ws1'], 'L2_ffn_ws2': _L2_ffn_in['ws2'], 'L2_ffn_ws3': _L2_ffn_in['ws3'], 'L3_attn_w_qkv': _L3_attn_in['w_qkv'], 'L3_attn_w_out': _L3_attn_in['w_out'], 'L3_xattn_Wq': _L3_xattn_in['Wq'], 'L3_xattn_Wk': _L3_xattn_in['Wk'], 'L3_xattn_Wv': _L3_xattn_in['Wv'], 'L3_xattn_Wo': _L3_xattn_in['Wo'], 'L3_xattn_gq': _L3_xattn_in['gq'], 'L3_xattn_gk': _L3_xattn_in['gk'], 'L3_ffn_router_weight': _L3_ffn_in['router_weight'], 'L3_ffn_e_bias': _L3_ffn_in['e_bias'], 'L3_ffn_w_up': _L3_ffn_in['w_up'], 'L3_ffn_w_down': _L3_ffn_in['w_down'], 'L3_ffn_shared_up': _L3_ffn_in['shared_up'], 'L3_ffn_shared_down': _L3_ffn_in['shared_down']}

def reference(x, ctx_1024, fside_BxSx2_0, mask_BxS2_bf1, L0_attn_q_w, L0_attn_q_b, L0_attn_k_w, L0_attn_k_b, L0_attn_v_w, L0_attn_v_b, L0_attn_o_w, L0_attn_o_b, L0_xattn_Wq, L0_xattn_Wkv, L0_xattn_Wout, L0_xattn_bout, L0_ffn_lut, L0_ffn_gate_idx, L0_ffn_up_idx, L0_ffn_down_idx, L1_attn_Wq, L1_attn_bq, L1_attn_Wk, L1_attn_bk, L1_attn_Wv, L1_attn_bv, L1_attn_Wo, L1_attn_bo, L1_xattn_Wq, L1_xattn_Wk, L1_xattn_Wv, L1_xattn_Wo, L1_ffn_router_w, L1_ffn_e_bias, L1_ffn_W_gate, L1_ffn_W_up, L1_ffn_W_down, L1_ffn_shared_gate, L1_ffn_shared_up, L1_ffn_shared_down, L2_attn_Wq, L2_attn_bq, L2_attn_Wk, L2_attn_bk, L2_attn_Wv, L2_attn_bv, L2_attn_Wo, L2_attn_bo, L2_attn_q_gain, L2_xattn_Wq, L2_xattn_bq, L2_xattn_Wk, L2_xattn_bk, L2_xattn_Wv, L2_xattn_bv, L2_xattn_Wkv_dca, L2_xattn_bkv_dca, L2_xattn_qn_w, L2_xattn_qn_b, L2_xattn_kn_w, L2_xattn_kn_b, L2_xattn_kn_dca_w, L2_xattn_kn_dca_b, L2_xattn_Wo, L2_xattn_bo, L2_ffn_w_router, L2_ffn_w1, L2_ffn_w2, L2_ffn_w3, L2_ffn_ws1, L2_ffn_ws2, L2_ffn_ws3, L3_attn_w_qkv, L3_attn_w_out, L3_xattn_Wq, L3_xattn_Wk, L3_xattn_Wv, L3_xattn_Wo, L3_xattn_gq, L3_xattn_gk, L3_ffn_router_weight, L3_ffn_e_bias, L3_ffn_w_up, L3_ffn_w_down, L3_ffn_shared_up, L3_ffn_shared_down):
    import jax
    import jax.numpy as jnp

    def _L0_attn_ref(hidden_states, q_w, q_b, k_w, k_b, v_w, v_b, o_w, o_b):
        import jax, jax.numpy as jnp
        import numpy as np
        HID = 256
        HEADS = 16
        HD = HID // HEADS
        EPS = 1e-06

        def _heads(x, b, s):
            return x.reshape(b, s, HEADS, HD).transpose(0, 2, 1, 3)
        b, s, _ = hidden_states.shape
        q = _heads(hidden_states @ q_w.T + q_b, b, s)
        k = _heads(hidden_states @ k_w.T + k_b, b, s)
        v = _heads(hidden_states @ v_w.T + v_b, b, s)
        qp = jax.nn.elu(q) + 1.0
        kp = jax.nn.elu(k) + 1.0
        kv = jnp.einsum('bhsd,bhse->bhde', kp, v)
        z = jnp.einsum('bhsd,bhd->bhs', qp, kp.sum(axis=2))[..., None]
        attn = jnp.einsum('bhsd,bhde->bhse', qp, kv) / (z + EPS)
        out = attn.transpose(0, 2, 1, 3).reshape(b, s, HID)
        return out @ o_w.T + o_b

    def _L0_xattn_ref(x, ctx, pos_map, ctx_pos_map, Wq, Wkv, Wout, bout):
        import jax, jax.numpy as jnp
        import numpy as np
        DIM = 256
        CTX_DIM = 128
        N_HEADS = 32
        HEAD_DIM = DIM // N_HEADS
        POS_DIM = 2
        B, N, CTXN = (2, 256, 256)
        ROPE_BASE = 10000.0

        def apply_axial_rope(x, pos):
            b, n, h, d = x.shape
            p = pos.shape[-1]
            dpa = d // p
            half = dpa // 2
            freqs = ROPE_BASE ** (-jnp.arange(half, dtype=x.dtype) / half)
            ang = pos[..., :, None] * freqs
            cos = jnp.cos(ang)[:, :, None, :, :]
            sin = jnp.sin(ang)[:, :, None, :, :]
            xr = x.reshape(b, n, h, p, half, 2)
            x1, x2 = (xr[..., 0], xr[..., 1])
            out = jnp.stack([x1 * cos - x2 * sin, x1 * sin + x2 * cos], axis=-1)
            return out.reshape(b, n, h, d)
        b, n, _ = x.shape
        ctx_n = ctx.shape[1]
        q = (x @ Wq).reshape(b, n, N_HEADS, HEAD_DIM)
        k, v = jnp.split(ctx @ Wkv, 2, axis=-1)
        k = k.reshape(b, ctx_n, N_HEADS, HEAD_DIM)
        v = v.reshape(b, ctx_n, N_HEADS, HEAD_DIM)
        q = apply_axial_rope(q, pos_map)
        k = apply_axial_rope(k, ctx_pos_map)
        scale = 1.0 / np.sqrt(HEAD_DIM).astype(np.float32)
        logits = jnp.einsum('bqhd,bkhd->bhqk', q, k) * scale
        w = jax.nn.softmax(logits, axis=-1)
        attn = jnp.einsum('bhqk,bkhd->bqhd', w, v)
        attn = attn.reshape(b, n, N_HEADS * HEAD_DIM)
        return attn @ Wout + bout

    def _L0_ffn_ref(x, lut, gate_idx, up_idx, down_idx):
        import jax, jax.numpy as jnp
        import numpy as np
        HIDDEN = 256
        INTER = 688
        LUT_SIZE = 16

        def _ghost_linear(x, idx, lut):
            w = lut[idx]
            return jnp.einsum('bsh,oh->bso', x, w)
        gate = _ghost_linear(x, gate_idx, lut)
        up = _ghost_linear(x, up_idx, lut)
        h = jax.nn.silu(gate) * up
        return _ghost_linear(h, down_idx, lut)

    def _L1_attn_ref(x, Wq, bq, Wk, bk, Wv, bv, Wo, bo):
        import jax, jax.numpy as jnp
        import numpy as np
        N_Q, N_KV = (16, 4)

        def _rope(x):
            d = x.shape[-1]
            T = x.shape[-2]
            inv_freq = 1.0 / 10000.0 ** (jnp.arange(d // 2, dtype=jnp.float32) * 2.0 / d)
            emb = jnp.arange(T, dtype=jnp.float32)[:, None] * inv_freq[None, :]
            cos, sin = (jnp.cos(emb), jnp.sin(emb))
            x1, x2 = (x[..., 0::2], x[..., 1::2])
            return jnp.concatenate([x1 * cos - x2 * sin, x1 * sin + x2 * cos], axis=-1)
        B, T, C = x.shape
        g = N_Q // N_KV
        d = C // N_Q
        q = (x @ Wq + bq).reshape(B, T, N_Q, d).transpose(0, 2, 1, 3)
        k = (x @ Wk + bk).reshape(B, T, N_KV, d).transpose(0, 2, 1, 3)
        v = (x @ Wv + bv).reshape(B, T, N_KV, d).transpose(0, 2, 1, 3)
        q = _rope(q)
        k = _rope(k)
        qg = q.reshape(B, N_KV, g, T, d)
        scores = jnp.einsum('bhgnd,bhsd->bhns', qg, k) * (1.0 / jnp.sqrt(jnp.float32(d)))
        mask = jnp.tril(jnp.ones((T, T), dtype=bool))
        att = jax.nn.softmax(jnp.where(mask, scores, -jnp.inf), axis=-1)
        y = jnp.einsum('bhns,bhsd->bhnd', att, v)
        y = y.transpose(0, 2, 1, 3).reshape(B, T, C // g)
        return y @ Wo + bo

    def _L1_xattn_ref(text_hidden, vision_tokens, vision_mask, Wq, Wk, Wv, Wo):
        import jax, jax.numpy as jnp
        import numpy as np
        N_HEADS = 16
        N_KV_HEADS = 8
        HEAD_DIM = 128
        D_TEXT = 256
        D_VISION = 128
        GROUPS = N_HEADS // N_KV_HEADS
        B, T_text, _ = text_hidden.shape
        T_vis = vision_tokens.shape[1]
        scale = jnp.float32(np.sqrt(HEAD_DIM))
        q = (text_hidden @ Wq).reshape(B, T_text, N_HEADS, HEAD_DIM).transpose(0, 2, 1, 3)
        k = (vision_tokens @ Wk).reshape(B, T_vis, N_KV_HEADS, HEAD_DIM).transpose(0, 2, 1, 3)
        v = (vision_tokens @ Wv).reshape(B, T_vis, N_KV_HEADS, HEAD_DIM).transpose(0, 2, 1, 3)
        k = jnp.repeat(k, GROUPS, axis=1)
        v = jnp.repeat(v, GROUPS, axis=1)
        scores = jnp.einsum('bhtd,bhsd->bhts', q, k) / scale
        mask = vision_mask[:, None, None, :]
        scores = jnp.where(mask, scores, -jnp.inf)
        attn = jax.nn.softmax(scores, axis=-1)
        attn = jnp.nan_to_num(attn, nan=0.0)
        out = jnp.einsum('bhts,bhsd->bhtd', attn, v)
        out = out.transpose(0, 2, 1, 3).reshape(B, T_text, N_HEADS * HEAD_DIM)
        return out @ Wo

    def _L1_ffn_ref(hidden_states, router_w, e_bias, W_gate, W_up, W_down, shared_gate, shared_up, shared_down):
        import math
        import jax, jax.numpy as jnp
        import numpy as np
        from jax import lax
        D = 256
        I = 128
        E = 32
        K = 4
        NG = 8
        TKG = 3
        NSH = 2
        SCALE = 2.5
        CF = 1.25
        B, S = (2, 256)

        def _router(x, router_w, e_bias):
            scores = jax.nn.sigmoid(x @ router_w.T)
            sc = scores + e_bias[None, :]
            T = x.shape[0]
            gs = sc.reshape(T, NG, E // NG)
            group_scores = lax.top_k(gs, 2)[0].sum(-1)
            _, gidx = lax.top_k(group_scores, TKG)
            gmask = jnp.zeros((T, NG), sc.dtype).at[jnp.arange(T)[:, None], gidx].set(1.0)
            smask = jnp.repeat(gmask, E // NG, axis=1)
            masked = jnp.where(smask > 0, sc, 0.0)
            _, topk_idx = lax.top_k(masked, K)
            topk_w = jnp.take_along_axis(scores, topk_idx, axis=1)
            topk_w = topk_w / (topk_w.sum(-1, keepdims=True) + 1e-20)
            topk_w = topk_w * SCALE
            return (topk_idx.astype(jnp.int32), topk_w)

        def _moe_forward(hidden_states, router_w, e_bias, W_gate, W_up, W_down, shared_gate, shared_up, shared_down):
            b, s, d = hidden_states.shape
            T = b * s
            C = int(math.ceil(CF * T / E))
            EC = E * C
            x = hidden_states.reshape(T, d)
            topk_idx, topk_w = _router(x, router_w, e_bias)
            expert_flat = topk_idx.reshape(-1)
            w_flat = topk_w.reshape(-1)
            tok_flat = jnp.repeat(jnp.arange(T, dtype=jnp.int32), K)
            sort_ix = jnp.argsort(expert_flat)
            e_sorted = expert_flat[sort_ix]
            tok_s = tok_flat[sort_ix]
            w_s = w_flat[sort_ix]
            counts = jnp.zeros(E, jnp.int32).at[e_sorted].add(1)
            group_start = jnp.concatenate([jnp.zeros(1, jnp.int32), jnp.cumsum(counts)[:-1].astype(jnp.int32)])
            pos = jnp.arange(T * K, dtype=jnp.int32) - group_start[e_sorted]
            valid = pos < C
            dest = e_sorted * C + jnp.where(valid, pos, 0)
            slots_token = jnp.zeros(EC, jnp.int32).at[dest].add(jnp.where(valid, tok_s, 0))
            slots_w = jnp.zeros(EC, w_s.dtype).at[dest].add(jnp.where(valid, w_s, 0.0))
            Xp = x[slots_token].reshape(E, C, d)
            G = jnp.einsum('ecd,edi->eci', Xp, W_gate)
            U = jnp.einsum('ecd,edi->eci', Xp, W_up)
            Y = jnp.einsum('eci,eid->ecd', jax.nn.silu(G) * U, W_down)
            Yf = Y.reshape(EC, d) * slots_w[:, None]
            out = jnp.zeros((T, d), x.dtype).at[slots_token].add(Yf)
            shared = jax.nn.silu(x @ shared_gate.T) * (x @ shared_up.T) @ shared_down.T
            return (out + shared).reshape(b, s, d)
        return _moe_forward(hidden_states, router_w, e_bias, W_gate, W_up, W_down, shared_gate, shared_up, shared_down)

    def _L2_attn_ref(x, Wq, bq, Wk, bk, Wv, bv, Wo, bo, q_gain):
        import jax, jax.numpy as jnp
        import numpy as np
        B, S, D = (2, 256, 256)
        H, KVH = (16, 4)
        HD = D // H
        KVD = KVH * HD
        BASE = 10000.0
        EPS = 1.1920929e-07

        def _rms_norm(t):
            return t * jax.lax.rsqrt(jnp.mean(t * t, axis=-1, keepdims=True) + EPS)

        def _rope_tables(s, dtype):
            inv_freq = 1.0 / BASE ** (jnp.arange(0, HD, 2, dtype=jnp.float32) / HD)
            t = jnp.arange(s, dtype=jnp.float32)
            freqs = jnp.outer(t, inv_freq)
            cos = jnp.cos(freqs)[None, None].astype(dtype)
            sin = jnp.sin(freqs)[None, None].astype(dtype)
            return (cos, sin)

        def _apply_rope(t, cos, sin):
            half = t.shape[-1] // 2
            t1, t2 = (t[..., :half], t[..., half:])
            return jnp.concatenate([t1 * cos + t2 * sin, -t1 * sin + t2 * cos], axis=-1)
        b, s, d = x.shape
        q = (jnp.einsum('bsd,ed->bse', x, Wq) + bq).reshape(b, s, H, HD).transpose(0, 2, 1, 3)
        k = (jnp.einsum('bsd,ed->bse', x, Wk) + bk).reshape(b, s, KVH, HD).transpose(0, 2, 1, 3)
        v = (jnp.einsum('bsd,ed->bse', x, Wv) + bv).reshape(b, s, KVH, HD).transpose(0, 2, 1, 3)
        q = _rms_norm(q)
        k = _rms_norm(k)
        cos, sin = _rope_tables(s, q.dtype)
        q = _apply_rope(q, cos, sin)
        k = _apply_rope(k, cos, sin)
        q = q * q_gain[None, :, None, None]
        rep = H // KVH
        k = jnp.repeat(k, rep, axis=1)
        v = jnp.repeat(v, rep, axis=1)
        scale = HD ** (-0.5)
        attn = jnp.einsum('bhqd,bhkd->bhqk', q * scale, k)
        causal = jnp.tril(jnp.ones((s, s), dtype=bool))
        attn = jnp.where(causal[None, None], attn, -jnp.inf)
        attn = jax.nn.softmax(attn, axis=-1)
        out = jnp.einsum('bhqk,bhkd->bqhd', attn, v).reshape(b, s, d)
        return jnp.einsum('bsd,ed->bse', out, Wo) + bo

    def _L2_xattn_ref(x, y, Wq, bq, Wk, bk, Wv, bv, Wkv_dca, bkv_dca, qn_w, qn_b, kn_w, kn_b, kn_dca_w, kn_dca_b, Wo, bo):
        import jax, jax.numpy as jnp
        import numpy as np
        B, S1, S2, DCA = (2, 256, 128, 16)
        QDIM, KDIM, H = (256, 128, 16)
        HD = QDIM // H
        SCALE = HD ** (-0.5)
        EPS = 1e-06
        DCA_WEIGHT = 1.0

        def _ln(t, w, b):
            m = jnp.mean(t, axis=-1, keepdims=True)
            v = jnp.var(t, axis=-1, keepdims=True)
            return (t - m) * jax.lax.rsqrt(v + EPS) * w + b

        def _attn(q, k, v):
            s = jnp.einsum('bhqd,bhkd->bhqk', q, k) * SCALE
            p = jax.nn.softmax(s, axis=-1)
            return jnp.einsum('bhqk,bhkd->bhqd', p, v)
        b, s1, _ = x.shape
        y_dca = y[:, -DCA:, :]
        y_main = y[:, :-DCA, :]
        kv_dca = (y_dca @ Wkv_dca + bkv_dca).reshape(b, DCA, 2, H, HD)
        k_dca = _ln(kv_dca[:, :, 0], kn_dca_w, kn_dca_b)
        v_dca = kv_dca[:, :, 1]
        s2 = y_main.shape[1]
        q = _ln((x @ Wq + bq).reshape(b, s1, H, HD), qn_w, qn_b)
        kv = jnp.concatenate([y_main @ Wk + bk, y_main @ Wv + bv], axis=-1)
        kv = kv.reshape(b, s2, H, 2 * HD)
        k = _ln(kv[..., :HD], kn_w, kn_b)
        v = kv[..., HD:]
        qT = q.transpose(0, 2, 1, 3)
        ctx = _attn(qT, k.transpose(0, 2, 1, 3), v.transpose(0, 2, 1, 3))
        ctx = ctx.transpose(0, 2, 1, 3).reshape(b, s1, QDIM)
        ctx_dca = _attn(qT, k_dca.transpose(0, 2, 1, 3), v_dca.transpose(0, 2, 1, 3))
        ctx_dca = ctx_dca.transpose(0, 2, 1, 3).reshape(b, s1, QDIM)
        ctx = ctx + DCA_WEIGHT * ctx_dca
        return ctx @ Wo + bo

    def _L2_ffn_ref(x, w_router, w1, w2, w3, ws1, ws2, ws3):
        import jax, jax.numpy as jnp
        import numpy as np
        B, S, D = (4, 256, 256)
        E, F = (8, 176)
        FS = 352
        TOP_K = 2
        INIT = 0.02
        b, s, h = x.shape
        xf = x.reshape(-1, h)
        T = xf.shape[0]
        n_experts = w1.shape[0]
        scores = jax.nn.sigmoid(xf @ w_router)
        top_vals, top_idx = jax.lax.top_k(scores, TOP_K)
        top_vals = top_vals / jnp.sum(top_vals, axis=-1, keepdims=True)
        combine = jnp.zeros((T, n_experts), dtype=x.dtype)
        combine = combine.at[jnp.arange(T)[:, None], top_idx].add(top_vals)
        out = jnp.zeros_like(xf)
        for e in range(n_experts):
            he = jax.nn.silu(xf @ w1[e]) * (xf @ w3[e])
            out = out + combine[:, e:e + 1] * (he @ w2[e])
        shared = jax.nn.silu(xf @ ws1) * (xf @ ws3) @ ws2
        return (out + shared).reshape(b, s, h)

    def _L3_attn_ref(x, w_qkv, w_out):
        import math
        import jax, jax.numpy as jnp
        import numpy as np
        HEAD_DIM = 128
        NUM_HEADS = 16
        ROPE_BASE = 10000.0

        def _rope_tables(seq_len, dim, dtype):
            inv_freq = 1.0 / ROPE_BASE ** (jnp.arange(0, dim, 2, dtype=jnp.float32) / dim)
            t = jnp.arange(seq_len, dtype=jnp.float32)
            freqs = jnp.einsum('i,j->ij', t, inv_freq)
            emb = jnp.concatenate([freqs, freqs], axis=-1)
            return (jnp.cos(emb).astype(dtype), jnp.sin(emb).astype(dtype))

        def _rotate_half(x):
            x1, x2 = jnp.split(x, 2, axis=-1)
            return jnp.concatenate([-x2, x1], axis=-1)

        def _apply_rope(x, cos, sin):
            return x * cos[None, :, None, :] + _rotate_half(x) * sin[None, :, None, :]
        B, S, _ = x.shape
        H, D = (NUM_HEADS, HEAD_DIM)
        qkv = jnp.einsum('bsd,od->bso', x, w_qkv)
        qkv = qkv.reshape(B, S, 3 * H, D)
        q = qkv[:, :, :H, :]
        k = qkv[:, :, H:2 * H, :]
        v = qkv[:, :, 2 * H:, :]
        cos, sin = _rope_tables(S, D, x.dtype)
        q = _apply_rope(q, cos, sin)
        k = _apply_rope(k, cos, sin)
        scale = 1.0 / math.sqrt(D)
        logits = jnp.einsum('bqhd,bkhd->bhqk', q, k) * scale
        attn = jax.nn.softmax(logits.astype(jnp.float32), axis=-1).astype(logits.dtype)
        out = jnp.einsum('bhqk,bkhd->bqhd', attn, v)
        out = out.reshape(B, S, H * D)
        return jnp.einsum('bso,do->bsd', out, w_out)

    def _L3_xattn_ref(hidden_states, encoder_hidden_states, Wq, Wk, Wv, Wo, gq, gk):
        import jax, jax.numpy as jnp
        import numpy as np
        EPS = 1e-05

        def rmsnorm(x, g, eps=EPS):
            var = jnp.mean(jnp.square(x), axis=-1, keepdims=True)
            return x * jax.lax.rsqrt(var + eps) * g
        B, Sq, _ = hidden_states.shape
        Skv = encoder_hidden_states.shape[1]
        D = gq.shape[0]
        H = Wq.shape[1] // D
        scale = 1.0 / np.sqrt(D)
        q = (hidden_states @ Wq).reshape(B, Sq, H, D)
        k = (encoder_hidden_states @ Wk).reshape(B, Skv, H, D)
        v = (encoder_hidden_states @ Wv).reshape(B, Skv, H, D)
        q = rmsnorm(q, gq)
        k = rmsnorm(k, gk)
        scores = jnp.einsum('bqhd,bkhd->bhqk', q, k) * scale
        attn = jax.nn.softmax(scores, axis=-1)
        out = jnp.einsum('bhqk,bkhd->bqhd', attn, v)
        out = out.reshape(B, Sq, H * D)
        return out @ Wo

    def _L3_ffn_ref(hidden_states, router_weight, e_bias, w_up, w_down, shared_up, shared_down):
        import jax, jax.numpy as jnp
        import numpy as np
        HIDDEN = 256
        MOE_INTER = 128
        SHARED_INTER = 512
        N_EXPERTS = 16
        TOP_K = 2
        N_GROUP = 4
        TOPK_GROUP = 2
        NORM_TOPK_PROB = True
        ROUTED_SCALING = 1.0

        def relu2(x):
            r = jax.nn.relu(x)
            return r * r

        def _get_topk_indices(scores, e_bias):
            T, E = scores.shape
            s = scores + e_bias[None, :]
            gsz = E // N_GROUP
            group_scores = jax.lax.top_k(s.reshape(T, N_GROUP, gsz), 2)[0].sum(-1)
            group_idx = jax.lax.top_k(group_scores, TOPK_GROUP)[1]
            group_mask = jnp.zeros((T, N_GROUP), dtype=bool).at[jnp.arange(T)[:, None], group_idx].set(True)
            score_mask = jnp.repeat(group_mask, gsz, axis=1)
            masked = jnp.where(score_mask, s, 0.0)
            topk_indices = jax.lax.top_k(masked, TOP_K)[1]
            return jax.lax.stop_gradient(topk_indices)

        def _router(x_flat, router_weight, e_bias):
            logits = jnp.einsum('th,eh->te', x_flat.astype(jnp.float32), router_weight.astype(jnp.float32))
            scores = jax.nn.sigmoid(logits)
            topk_indices = _get_topk_indices(scores, e_bias)
            topk_weights = jnp.take_along_axis(scores, topk_indices, axis=1)
            if NORM_TOPK_PROB:
                topk_weights = topk_weights / (topk_weights.sum(-1, keepdims=True) + 1e-20)
            return (topk_indices, topk_weights * ROUTED_SCALING)
        orig_shape = hidden_states.shape
        x = hidden_states.reshape(-1, HIDDEN)
        T = x.shape[0]
        topk_indices, topk_weights = _router(x, router_weight, e_bias)
        combine = jnp.zeros((T, N_EXPERTS), dtype=topk_weights.dtype).at[jnp.arange(T)[:, None], topk_indices].add(topk_weights)
        h1 = jnp.einsum('th,ehi->tei', x, w_up)
        a = relu2(h1) * combine[:, :, None]
        routed = jnp.einsum('tei,eih->th', a, w_down)
        shared = relu2(hidden_states @ shared_up) @ shared_down
        return routed.reshape(orig_shape) + shared
    x = x + _L0_attn_ref(_layernorm(x, axis=-1), L0_attn_q_w, L0_attn_q_b, L0_attn_k_w, L0_attn_k_b, L0_attn_v_w, L0_attn_v_b, L0_attn_o_w, L0_attn_o_b)
    x = x + _L0_xattn_ref(_layernorm(x, axis=-1), ctx_1024, fside_BxSx2_0, fside_BxSx2_0, L0_xattn_Wq, L0_xattn_Wkv, L0_xattn_Wout, L0_xattn_bout)
    x = x + _L0_ffn_ref(_layernorm(x, axis=-1), L0_ffn_lut, L0_ffn_gate_idx, L0_ffn_up_idx, L0_ffn_down_idx)
    x = x + _L1_attn_ref(_layernorm(x, axis=-1), L1_attn_Wq, L1_attn_bq, L1_attn_Wk, L1_attn_bk, L1_attn_Wv, L1_attn_bv, L1_attn_Wo, L1_attn_bo)
    x = x + _L1_xattn_ref(_layernorm(x, axis=-1), ctx_1024, mask_BxS2_bf1, L1_xattn_Wq, L1_xattn_Wk, L1_xattn_Wv, L1_xattn_Wo)
    x = x + _L1_ffn_ref(_layernorm(x, axis=-1), L1_ffn_router_w, L1_ffn_e_bias, L1_ffn_W_gate, L1_ffn_W_up, L1_ffn_W_down, L1_ffn_shared_gate, L1_ffn_shared_up, L1_ffn_shared_down)
    x = x + _L2_attn_ref(_layernorm(x, axis=-1), L2_attn_Wq, L2_attn_bq, L2_attn_Wk, L2_attn_bk, L2_attn_Wv, L2_attn_bv, L2_attn_Wo, L2_attn_bo, L2_attn_q_gain)
    x = x + _L2_xattn_ref(_layernorm(x, axis=-1), ctx_1024, L2_xattn_Wq, L2_xattn_bq, L2_xattn_Wk, L2_xattn_bk, L2_xattn_Wv, L2_xattn_bv, L2_xattn_Wkv_dca, L2_xattn_bkv_dca, L2_xattn_qn_w, L2_xattn_qn_b, L2_xattn_kn_w, L2_xattn_kn_b, L2_xattn_kn_dca_w, L2_xattn_kn_dca_b, L2_xattn_Wo, L2_xattn_bo)
    x = x + _L2_ffn_ref(_layernorm(x, axis=-1), L2_ffn_w_router, L2_ffn_w1, L2_ffn_w2, L2_ffn_w3, L2_ffn_ws1, L2_ffn_ws2, L2_ffn_ws3)
    x = x + _L3_attn_ref(_layernorm(x, axis=-1), L3_attn_w_qkv, L3_attn_w_out)
    x = x + _L3_xattn_ref(_layernorm(x, axis=-1), ctx_1024, L3_xattn_Wq, L3_xattn_Wk, L3_xattn_Wv, L3_xattn_Wo, L3_xattn_gq, L3_xattn_gk)
    x = x + _L3_ffn_ref(_layernorm(x, axis=-1), L3_ffn_router_weight, L3_ffn_e_bias, L3_ffn_w_up, L3_ffn_w_down, L3_ffn_shared_up, L3_ffn_shared_down)
    return x

_drawn_inputs = setup_inputs


def setup_inputs(seed=0):
    import zlib

    import numpy as np

    out = dict(_drawn_inputs(seed))
    spreads = {'L0_attn_q_b': (0.0, 0.8),
     'L0_attn_k_b': (0.0, 0.8),
     'L0_attn_v_b': (0.0, 0.1),
     'L0_attn_o_b': (0.0, 0.1),
     'L0_xattn_bout': (0.0, 0.1),
     'L1_attn_bq': (0.0, 0.8),
     'L1_attn_bk': (0.0, 0.8),
     'L1_attn_bv': (0.0, 0.448),
     'L1_attn_bo': (0.0, 0.1),
     'L1_ffn_e_bias': (0.0, 0.8),
     'L2_attn_bq': (0.0, 0.647),
     'L2_attn_bk': (0.0, 0.8),
     'L2_attn_bv': (0.0, 0.1),
     'L2_attn_bo': (0.0, 0.1),
     'L2_attn_q_gain': (1.0, 0.6),
     'L2_xattn_bq': (0.0, 0.8),
     'L2_xattn_bk': (0.0, 0.523),
     'L2_xattn_bv': (0.0, 0.489),
     'L2_xattn_bkv_dca': (0.0, 0.343),
     'L2_xattn_qn_w': (1.0, 0.6),
     'L2_xattn_qn_b': (0.0, 0.8),
     'L2_xattn_kn_w': (1.0, 0.6),
     'L2_xattn_kn_b': (0.0, 2.0),
     'L2_xattn_kn_dca_w': (1.0, 0.6),
     'L2_xattn_kn_dca_b': (0.0, 2.0),
     'L2_xattn_bo': (0.0, 0.1),
     'L3_xattn_gq': (1.0, 0.6),
     'L3_xattn_gk': (1.0, 0.6),
     'L3_ffn_e_bias': (0.0, 0.567)}
    factors = {'L0_attn_q_w': 5.909,
     'L0_attn_k_w': 2.675,
     'L1_attn_Wq': 8.0,
     'L1_attn_Wk': 8.0,
     'L1_xattn_Wq': 8.0,
     'L1_xattn_Wk': 8.0,
     'L1_ffn_router_w': 8.0,
     'L1_ffn_W_gate': 8.0,
     'L1_ffn_W_up': 8.0,
     'L1_ffn_W_down': 8.0,
     'L1_ffn_shared_gate': 3.96,
     'L1_ffn_shared_up': 4.121,
     'L1_ffn_shared_down': 3.923,
     'L2_xattn_Wq': 3.619,
     'L2_xattn_Wk': 2.833,
     'L2_xattn_Wv': 2.869,
     'L2_ffn_w_router': 8.0,
     'L2_ffn_w1': 8.0,
     'L2_ffn_w2': 8.0,
     'L2_ffn_w3': 8.0,
     'L2_ffn_ws1': 4.036,
     'L2_ffn_ws2': 3.981,
     'L2_ffn_ws3': 3.962,
     'L3_ffn_router_weight': 4.775,
     'L3_ffn_w_up': 4.5,
     'L3_ffn_w_down': 4.077,
     'L3_attn_w_qkv': 3.269,
     'L3_attn_w_out': 3.26,
     'L3_ffn_shared_up': 8.0,
     'L3_ffn_shared_down': 8.0}
    for name, (base, spread) in spreads.items():
        noise = np.random.default_rng([zlib.crc32(name.encode()), seed]).standard_normal(out[name].shape)
        drawn = base * np.exp(spread * noise) if base else spread * noise
        out[name] = jnp.asarray(drawn.astype(out[name].dtype))
    for name, factor in factors.items():
        out[name] = (out[name] * factor).astype(out[name].dtype)
    return out
```

```python
from contextlib import ExitStack

import numpy as np

import concourse.bass as bass
from concourse import mybir

ALU = mybir.AluOpType
ACT = mybir.ActivationFunctionType
AX = mybir.AxisListType
F32 = mybir.dt.float32
BF16 = mybir.dt.bfloat16
I32 = mybir.dt.int32

P = 128
NB = 16
D = 256
KD = D // P
DCTX = 128
GRP = 4
NG = NB // GRP
LN_EPS = 1e-5
PI = float(np.pi)
FREQ = (1.0, 0.01)
NEG = -1e30
SPARE = 2


def nth(k):
    return k + 1 + SPARE


def held(eng, sem, value):
    if not isinstance(value, int) or value > SPARE:
        eng.wait_ge(sem, value)


def pick(ap, i):
    return ap[:, bass.ds(i, 1)]


class Layer:

    def __init__(self, nc, name):
        self.nc, self.name, self.stack, self.sems = nc, name, ExitStack(), []

    def __enter__(self):
        return self

    def sb(self, name, shape, dtype=F32):
        return self.stack.enter_context(self.nc.sbuf_tensor(f"{self.name}_{name}", shape, dtype))

    def sem(self, name):
        s = self.nc.alloc_semaphore(f"{self.name}_{name}")
        self.sems.append(s)
        return s

    def __exit__(self, *exc):
        if exc[0] is None:
            self.nc.clear_and_free_semaphores(self.sems)
            self.nc.all_engine_barrier()
        self.stack.close()
        return False


class Core:

    def __init__(self, nc, ctx, consts):
        self.nc = nc
        sb = lambda n, s, d=F32: ctx.enter_context(nc.sbuf_tensor(n, s, d))
        self.x = sb("x_res", [P, NB, D])
        self.ident = sb("ident", [P, P])
        self.ones = sb("ones", [P, P])
        self.minus_half = sb("minus_half", [P, 32])
        self.far = sb("far", [P, 16384])
        self.near = sb("near", [P, 12288])
        self.arrived = {}
        self.bank = [ctx.enter_context(nc.psum_tensor(f"bank{i}", [P, 512], F32)) for i in range(8)]


def claim(nc, core, arena, at, name, parts):
    arrived = nc.alloc_semaphore(f"{name}_weights_in")
    views, todo = [], []
    for source, rows, shape in parts:
        n = int(np.prod(shape))
        flat = arena[0:rows, at:at + n]
        names = " ".join(f"d{i}" for i in range(len(shape)))
        sizes = {f"d{i}": s for i, s in enumerate(shape)}
        views.append(flat.rearrange(f"p ({names}) -> p {names}", **sizes))
        todo.append((flat, source))
        at += n

    def fetch(sp):
        for flat, source in todo:
            sp.dma_start(flat, source).then_inc(arrived, 16)

    return views, (arrived, 16 * len(parts)), fetch


def load_constants(nc, core, x_in, ident_in, prefetch=()):
    with Layer(nc, "begin") as L:
        loaded = L.sem("loaded")
        with nc.Block() as block:
            @block.sync
            def _(sp):
                sp.dma_start(core.x[:, :, :], x_in.rearrange("b p d -> p b d")).then_inc(loaded, 16)
                sp.dma_start(core.ident[:, :], ident_in).then_inc(loaded, 16)
                for fetch in prefetch:
                    fetch(sp)
                sp.wait_ge(loaded, 32)

            @block.vector
            def _(dve):
                nc.vector.memset(core.ones[:, :], 1.0)
                nc.vector.memset(core.minus_half[:, :], -0.5)


def store_result(nc, core, out):
    with Layer(nc, "end") as L:
        stored = L.sem("stored")
        with nc.Block() as block:
            @block.sync
            def _(sp):
                sp.dma_start(out.rearrange("b p d -> p b d"), core.x[:, :, :]).then_inc(stored, 16)
                sp.wait_ge(stored, 16)


def top_first(nc, dve, v, k, n, iota, work, sel):
    eq, top = work["eq"], work["top"]
    rows = v.shape[1]
    wide = [P, rows, n]
    for r in range(k):
        dve.drain()
        nc.vector.tensor_reduce(top, v, AX.X, ALU.max)
        dve.drain()
        nc.vector.tensor_tensor(eq, v, top.unsqueeze(2).to_broadcast(wide), ALU.is_equal)
        dve.drain()
        nc.vector.tensor_tensor(eq, eq, iota, ALU.mult)
        dve.drain()
        nc.vector.tensor_reduce(top, eq, AX.X, ALU.max)
        dve.drain()
        nc.vector.tensor_tensor(eq, eq, top.unsqueeze(2).to_broadcast(wide), ALU.is_equal)
        dve.drain()
        if r == 0:
            nc.vector.tensor_copy(sel, eq)
        else:
            nc.vector.tensor_tensor(sel, sel, eq, ALU.add)
        nc.vector.scalar_tensor_tensor(v, eq, NEG, v, ALU.mult, ALU.add)
    dve.drain()


def ffn_layer(nc, core, name, w_in, w_down, width, act, router=None, per=1, prefetch=()):
    gated = act == "silu"
    slices = w_in.shape[0]
    halves = 2 if gated else 1
    experts = router["experts"] if router else 0
    with Layer(nc, name) as L:
        sb, sem = L.sb, L.sem
        stats = sb("stats", [P, GRP, 6])
        mv = sb("mv", [P, GRP, 2])
        var = sb("var", [P, GRP])
        rstd = sb("rstd", [P, GRP])
        xn = sb("xn", [P, GRP, D])
        xnT = sb("xnT", [P, KD, NB * P])
        wi = [sb(f"wi{u}", [P, halves, KD, width]) for u in range(2)]
        wd = [sb(f"wd{u}", [width, D]) for u in range(2)]
        s = [sb(f"s{u}", [width, 512]) for u in range(2)]
        h = [sb(f"h{u}", [width, 512]) for u in range(2)]
        combine = sb("combine", [P, NB, slices])
        if router:
            wr = sb("wr", [P, KD, experts])
            xg = sb("xg", [P, KD, 512])
            logits = sb("logits", [P, NB, experts])
        b_T, b_log = core.bank[0:2], core.bank[2]
        b_g, b_u, b_y = core.bank[0:2], core.bank[2:4], core.bank[4:8]

        var_ready, rstd_ready, xn_ready = sem("var_ready"), sem("rstd_ready"), sem("xn_ready")
        turned, xnT_ready, xg_ready = sem("turned"), sem("xnT_ready"), sem("xg_ready")
        logits_made, logits_kept, scored = sem("logits_made"), sem("logits_kept"), sem("scored")
        combined, router_in = sem("combined"), sem("router_in")
        wi_loaded = [sem(f"wi_loaded{u}") for u in range(2)]
        wd_loaded = [sem(f"wd_loaded{u}") for u in range(2)]
        gu_made, act_done, h_ready, y_made, y_added = (
            sem("gu_made"), sem("act_done"), sem("h_ready"), sem("y_made"), sem("y_added"))
        picked, counted = sem("picked"), sem("counted")

        with nc.Block() as block:
            @block.sync
            def _(sp):
                def load(n, u):
                    sp.dma_start(wi[u][:, :, :, :].rearrange("p a k w -> p (a k w)"),
                                 w_in[bass.ds(n, 1), :, :].rearrange("a p w -> (a p) w")
                                 ).then_inc(wi_loaded[u], 16)
                    sp.dma_start(wd[u][:, :], w_down[bass.ds(n, 1), :, :].rearrange("a p w -> (a p) w")
                                 ).then_inc(wd_loaded[u], 16)

                if router:
                    sp.dma_start(wr[:, :, :], router["w"].rearrange("(k p) e -> p k e", k=KD)
                                 ).then_inc(router_in, 16)
                    router["load"](sp, L, router_in)
                load(0, 0)
                load(1, 1)
                for fetch in prefetch:
                    fetch(sp)
                with sp.Fori(1, slices // 2) as i:
                    for u in range(2):
                        sp.wait_ge(y_made, nth(4 * (2 * i + u - 2) + 3))
                        load(2 * i + u, u)

            @block.vector
            def _(dve):
                dve.sem_inc(h_ready, SPARE)
                dve.sem_inc(y_added, SPARE)
                dve.sem_inc(logits_kept, SPARE)
                with dve.Fori(0, NG) as g:
                    for t in range(GRP):
                        nc.vector.bn_stats(stats[:, t, :], core.x[:, bass.ds(GRP * g + t, 1), :])
                    dve.drain()
                    for t in range(GRP):
                        nc.vector.bn_aggr(mv[:, t, :], stats[:, t, :])
                    dve.drain()
                    nc.vector.tensor_scalar(var[:, :], mv[:, :, 1], LN_EPS, None, ALU.add
                                            ).then_inc(var_ready, 1)
                    dve.wait_ge(rstd_ready, g + 1)
                    dve.wait_ge(turned, nth(g - 1))
                    for t in range(GRP):
                        last = nc.vector.tensor_scalar(
                            xn[:, t, :], core.x[:, bass.ds(GRP * g + t, 1), :],
                            mv[:, t, 0:1], rstd[:, t:t + 1], ALU.subtract, ALU.mult)
                    last.then_inc(xn_ready, 1)
                    if router:
                        dve.wait_ge(logits_made, nth(g))
                        nc.vector.tensor_copy(logits[:, bass.ds(GRP * g, GRP), :],
                                              b_log[:, 0:GRP * experts].rearrange("p (t e) -> p t e", t=GRP)
                                              ).then_inc(logits_kept, 1)
                nc.vector.memset(combine[:, :, experts * per:], 1.0)
                if router:
                    router["choose"](dve, L, logits, combine, scored, picked, counted, router_in)
                dve.drain()

                def hidden(f, g):
                    dve.wait_ge(act_done, nth(f))
                    dve.wait_ge(y_made, nth(f - 2))
                    if gated:
                        nc.vector.tensor_tensor(h[g % 2][:, :], s[g % 2][:, :], b_u[g % 2][0:width, :],
                                                ALU.mult).then_inc(h_ready, 1)
                    else:
                        nc.vector.tensor_tensor(h[g % 2][:, :], s[g % 2][:, :], s[g % 2][:, :],
                                                ALU.mult).then_inc(h_ready, 1)

                def add(f, n, g):
                    dve.wait_ge(y_made, nth(f))
                    for t in range(GRP):
                        b = GRP * g + t
                        y = b_y[2 * (g % 2) + t // 2][:, 256 * (t % 2):256 * (t % 2) + 256]
                        last = nc.vector.scalar_tensor_tensor(
                            core.x[:, b, :], y, combine[:, b, bass.ds(n, 1)], core.x[:, b, :],
                            ALU.mult, ALU.add)
                    last.then_inc(y_added, 1)

                for u in range(2):
                    for g in range(NG):
                        hidden(4 * u + g, g)
                        if 4 * u + g:
                            add(4 * u + g - 1, u if g else 0, (g - 1) % NG)
                with dve.Fori(1, slices // 2) as i:
                    for u in range(2):
                        for g in range(NG):
                            hidden(8 * i + 4 * u + g, g)
                            add(8 * i + 4 * u + g - 1, 2 * i + u - (0 if g else 1), (g - 1) % NG)
                add(4 * slices - 1, slices - 1, NG - 1)

            @block.gpsimd
            def _(pool):
                with pool.Fori(0, NG) as g:
                    pool.wait_ge(var_ready, g + 1)
                    nc.gpsimd.tensor_tensor(rstd[:, :], var[:, :], core.minus_half[:, 0:GRP], ALU.pow
                                            ).then_inc(rstd_ready, 1)

            @block.scalar
            def _(act_):
                act_.sem_inc(act_done, SPARE)
                act_.sem_inc(xnT_ready, SPARE)
                with act_.Fori(0, NG) as g:
                    act_.wait_ge(turned, nth(g))
                    if router:
                        act_.wait_ge(logits_made, nth(g - 1))
                        for k in range(KD):
                            nc.scalar.copy(xg[:, k, :], b_T[k][:, :])
                    for k in range(KD):
                        last = nc.scalar.copy(xnT[:, k, bass.ds(512 * g, 512)], b_T[k][:, :])
                    act_.drain().then_inc(xnT_ready, 1)
                if router:
                    act_.wait_ge(logits_kept, nth(NG - 1))
                    nc.scalar.activation(logits[:, :, :], logits[:, :, :], ACT.Sigmoid
                                         ).then_inc(scored, 1)

                def activate(f, g):
                    act_.wait_ge(gu_made, nth(f))
                    if gated:
                        nc.scalar.activation(s[g % 2][:, :], b_g[g % 2][0:width, :], ACT.Silu
                                             ).then_inc(act_done, 1)
                    else:
                        nc.scalar.activation(s[g % 2][:, :], b_g[g % 2][0:width, :], ACT.Relu
                                             ).then_inc(act_done, 1)

                for f in range(8):
                    activate(f, f % NG)
                with act_.Fori(1, slices // 2) as i:
                    for f in range(8):
                        activate(8 * i + f, f % NG)

            @block.tensor
            def _(pe):
                pe.sem_inc(turned, SPARE)
                pe.sem_inc(logits_made, SPARE)
                pe.sem_inc(gu_made, SPARE)
                pe.sem_inc(y_made, SPARE)
                if router:
                    pe.wait_ge(router_in, router["loads"])
                with pe.Fori(0, NG) as g:
                    pe.wait_ge(xn_ready, g + 1)
                    pe.wait_ge(xnT_ready, nth(g - 1))
                    for k in range(KD):
                        for t in range(GRP):
                            last = nc.tensor.transpose(b_T[k][:, P * t:P * t + P],
                                                       xn[:, t, P * k:P * k + P], core.ident[:, :])
                    last.then_inc(turned, 1)
                    if router:
                        pe.wait_ge(xnT_ready, nth(g))
                        pe.wait_ge(logits_kept, nth(g - 1))
                        for t in range(GRP):
                            for k in range(KD):
                                last = nc.tensor.matmul(b_log[:, experts * t:experts * (t + 1)],
                                                        xg[:, k, P * t:P * t + P], wr[:, k, :],
                                                        start=(k == 0), stop=(k == KD - 1))
                        last.then_inc(logits_made, 1)
                pe.wait_ge(xnT_ready, nth(NG - 1))
                if router:
                    pe.wait_ge(logits_kept, nth(NG - 1))
                    router["count"](pe, L, picked, counted)

                def up(f, i, u, g):
                    if g == 0:
                        pe.wait_ge(wi_loaded[u], 16 * (i + 1))
                    pe.wait_ge(h_ready, nth(f - 2))
                    for a, bank in ((0, b_g), (1, b_u))[:halves]:
                        for k in range(KD):
                            last = nc.tensor.matmul(bank[g % 2][0:width, :], wi[u][:, a, k, :],
                                                    xnT[:, k, 512 * g:512 * g + 512],
                                                    start=(k == 0), stop=(k == KD - 1))
                    last.then_inc(gu_made, 1)

                def down(f, i, u, g):
                    if g == 0:
                        pe.wait_ge(wd_loaded[u], 16 * (i + 1))
                    pe.wait_ge(h_ready, nth(f))
                    pe.wait_ge(y_added, nth(f - 2))
                    for t in range(GRP):
                        last = nc.tensor.matmul(
                            b_y[2 * (g % 2) + t // 2][:, 256 * (t % 2):256 * (t % 2) + 256],
                            h[g % 2][:, P * t:P * t + P], wd[u][:, :], start=True, stop=True)
                    last.then_inc(y_made, 1)

                for u in range(2):
                    for g in range(NG):
                        up(4 * u + g, 0, u, g)
                        if 4 * u + g:
                            down(4 * u + g - 1, 0, u if g else 0, (g - 1) % NG)
                with pe.Fori(1, slices // 2) as i:
                    for u in range(2):
                        for g in range(NG):
                            up(8 * i + 4 * u + g, i, u, g)
                            if g:
                                down(8 * i + 4 * u + g - 1, i, u, g - 1)
                            else:
                                down(8 * i + 4 * u - 1, i - (1 - u), 1 - u, NG - 1)
                down(4 * slices - 1, slices // 2 - 1, 1, NG - 1)


def make_router(nc, core, w, bias, iotas, experts, groups, top_groups, top, scale, eps,
                capacity=0, below=None, per=1):
    size = experts // groups if groups else 0
    r = {"w": w, "experts": experts}
    r["loads"] = 16 * (2 + (bias is not None) + (groups > 0) + (capacity > 0))
    wide = [P, NB, experts]

    def load(sp, L, router_in):
        r["iota"] = L.sb("iota", [P, NB, experts])
        sp.dma_start(r["iota"][:, :, :].rearrange("p b e -> p (b e)"), iotas[0]).then_inc(router_in, 16)
        if bias is not None:
            r["bias"] = L.sb("bias", [P, experts])
            sp.dma_start(r["bias"][:, :], bias.partition_broadcast(P)).then_inc(router_in, 16)
        if groups:
            r["giota"] = L.sb("giota", [P, NB, groups])
            sp.dma_start(r["giota"][:, :, :].rearrange("p b e -> p (b e)"), iotas[1]).then_inc(router_in, 16)
        if capacity:
            r["below"] = L.sb("below", [P, P])
            sp.dma_start(r["below"][:, :], below).then_inc(router_in, 16)

    def spread(combine):
        return combine[:, :, 0:experts * per].rearrange("p b (e r) -> p b e r", r=per)

    def choose(dve, L, scores, combine, scored, picked, counted, router_in):
        v = L.sb("v", wide)
        sel = L.sb("sel", wide)
        eq = L.sb("eq", wide)
        top_v = L.sb("top_v", [P, NB])
        dve.wait_ge(scored, 1)
        dve.wait_ge(router_in, r["loads"])
        if bias is not None:
            nc.vector.tensor_tensor(v[:, :, :], scores[:, :, :],
                                    r["bias"][:, :].unsqueeze(1).to_broadcast(wide), ALU.add)
        else:
            nc.vector.tensor_copy(v[:, :, :], scores[:, :, :])
        if groups:
            ab = L.sb("ab", [P, 4, NB * groups])
            gs = L.sb("gs", [P, NB, groups])
            gsel = L.sb("gsel", [P, NB, groups])
            geq = L.sb("geq", [P, NB, groups])
            m = v[:, :, :].rearrange("p b (g i) -> p (b g) i", i=size)
            dve.drain()
            for i in range(2):
                nc.vector.tensor_tensor(ab[:, 2 * i, :], m[:, :, 2 * i], m[:, :, 2 * i + 1], ALU.max)
                nc.vector.tensor_tensor(ab[:, 2 * i + 1, :], m[:, :, 2 * i], m[:, :, 2 * i + 1], ALU.min)
            dve.drain()
            g1 = gs[:, :, :].rearrange("p b g -> p (b g)")
            g2 = geq[:, :, :].rearrange("p b g -> p (b g)")
            g3 = gsel[:, :, :].rearrange("p b g -> p (b g)")
            nc.vector.tensor_tensor(g1, ab[:, 0, :], ab[:, 2, :], ALU.max)
            nc.vector.tensor_tensor(g2, ab[:, 0, :], ab[:, 2, :], ALU.min)
            nc.vector.tensor_tensor(g3, ab[:, 1, :], ab[:, 3, :], ALU.max)
            dve.drain()
            nc.vector.tensor_tensor(g2, g2, g3, ALU.max)
            dve.drain()
            nc.vector.tensor_tensor(g1, g1, g2, ALU.add)
            top_first(nc, dve, gs[:, :, :], top_groups, groups, r["giota"][:, :, :],
                      {"eq": geq[:, :, :], "top": top_v[:, :]}, gsel[:, :, :])
            nc.vector.tensor_tensor(m, m, g3.unsqueeze(2).to_broadcast([P, NB * groups, size]), ALU.mult)
        top_first(nc, dve, v[:, :, :], top, experts, r["iota"][:, :, :],
                  {"eq": eq[:, :, :], "top": top_v[:, :]}, sel[:, :, :])
        nc.vector.tensor_tensor(v[:, :, :], sel[:, :, :], scores[:, :, :], ALU.mult)
        dve.drain()
        nc.vector.tensor_reduce(top_v[:, :], v[:, :, :], AX.X, ALU.add)
        dve.drain()
        if eps:
            nc.vector.tensor_scalar(top_v[:, :], top_v[:, :], eps, None, ALU.add)
            dve.drain()
        nc.vector.reciprocal(top_v[:, :], top_v[:, :])
        dve.drain()
        nc.vector.tensor_tensor(v[:, :, :], v[:, :, :],
                                top_v[:, :].unsqueeze(2).to_broadcast(wide), ALU.mult)
        dve.drain()
        if not capacity:
            for r_ in range(per):
                nc.vector.tensor_scalar(spread(combine)[:, :, :, r_], v[:, :, :], scale, None, ALU.mult)
            return
        r["sel"] = sel
        nc.vector.tensor_scalar(v[:, :, :], v[:, :, :], scale, None, ALU.mult).then_inc(picked, 1)
        dve.wait_ge(counted, 1)
        total = [eq, L.sb("total", wide)]
        nc.vector.memset(total[0][:, 0, :], 0.0)
        nc.vector.tensor_copy(total[0][:, 1:, :], core.bank[1][:, 0:(NB - 1) * experts].rearrange(
            "p (b e) -> p b e", b=NB - 1))
        at, step = 0, 1
        while step < NB:
            dve.drain()
            a, b = total[at], total[1 - at]
            nc.vector.tensor_copy(b[:, 0:step, :], a[:, 0:step, :])
            nc.vector.tensor_tensor(b[:, step:, :], a[:, step:, :], a[:, 0:NB - step, :], ALU.add)
            at, step = 1 - at, 2 * step
        dve.drain()
        nc.vector.tensor_tensor(total[at][:, :, :], total[at][:, :, :],
                                core.bank[0][:, 0:NB * experts].rearrange("p (b e) -> p b e", b=NB), ALU.add)
        dve.drain()
        nc.vector.tensor_scalar(total[at][:, :, :], total[at][:, :, :], float(capacity), None, ALU.is_lt)
        dve.drain()
        nc.vector.tensor_tensor(combine[:, :, 0:experts], total[at][:, :, :], v[:, :, :],
                                ALU.mult).then_inc(picked, 1)

    def count(pe, L, picked, counted):
        if not capacity:
            return
        pe.wait_ge(picked, 1)
        flat = r["sel"][:, :, :].rearrange("p b e -> p (b e)")
        nc.tensor.matmul(core.bank[0][:, 0:NB * experts], r["below"][:, :], flat, start=True, stop=True)
        nc.tensor.matmul(core.bank[1][:, 0:NB * experts], core.ones[:, :], flat, start=True, stop=True
                         ).then_inc(counted, 1)
        pe.wait_ge(picked, 2)

    r["load"], r["choose"], r["count"] = load, choose, count
    return r


def behind(b, u, c, k, chunks):
    db, cc = divmod(c - k, chunks)
    if isinstance(b, int) and not 0 <= b + db < NB:
        return None
    return b + db, (u + db) % 2, cc, chunks * (b + db) + cc


def run_slots(eng, slot, chunks, peeled, extra):
    for b in range(2 * peeled):
        for c in range(chunks):
            slot(b, b % 2, c)
    with eng.Fori(peeled, NB // 2) as i:
        for u in range(2):
            for c in range(chunks):
                slot(2 * i + u, u, c)
    for f in range(NB * chunks, NB * chunks + extra):
        slot(f // chunks, (f // chunks) % 2, f % chunks)


class Norm:

    def __init__(self, nc, core, L, bank):
        self.nc, self.core, self.bank = nc, core, bank
        self.stats = L.sb("ln_stats", [P, 6])
        self.mv = [L.sb(f"ln_mv{u}", [P, 2]) for u in range(2)]
        self.var = L.sb("ln_var", [P, 1])
        self.rstd = L.sb("ln_rstd", [P, 1])
        self.xn = L.sb("ln_xn", [P, D])
        self.xnT = [L.sb(f"ln_xnT{u}", [P, KD, P]) for u in range(2)]
        self.var_ready, self.rstd_ready = L.sem("ln_var_ready"), L.sem("ln_rstd_ready")
        self.xn_ready, self.turned, self.kept = L.sem("xn_ready"), L.sem("xn_turned"), L.sem("xnT_kept")

    def prime_pe(self, pe):
        pe.sem_inc(self.turned, SPARE)

    def prime_act(self, act):
        act.sem_inc(self.kept, SPARE)

    def moments(self, dve, b):
        nc = self.nc
        nc.vector.bn_stats(self.stats[:, :], pick(self.core.x[:, :, :], b))
        dve.drain()
        mv = self.mv[0]
        nc.vector.bn_aggr(mv[:, :], self.stats[:, :])
        dve.drain()
        nc.vector.tensor_scalar(self.var[:, :], mv[:, 1:2], LN_EPS, None, ALU.add
                                ).then_inc(self.var_ready, 1)

    def rsqrt(self, pool, b):
        pool.wait_ge(self.var_ready, b + 1)
        self.nc.gpsimd.tensor_tensor(self.rstd[:, :], self.var[:, :], self.core.minus_half[:, 0:1],
                                     ALU.pow).then_inc(self.rstd_ready, 1)

    def normalise(self, dve, b):
        dve.wait_ge(self.rstd_ready, b + 1)
        dve.wait_ge(self.turned, nth(b - 1))
        self.nc.vector.tensor_scalar(self.xn[:, :], pick(self.core.x[:, :, :], b), self.mv[0][:, 0:1],
                                     self.rstd[:, 0:1], ALU.subtract, ALU.mult).then_inc(self.xn_ready, 1)

    def turn(self, pe, b):
        pe.wait_ge(self.xn_ready, b + 1)
        pe.wait_ge(self.kept, nth(b - 1))
        for k in range(KD):
            last = self.nc.tensor.transpose(self.bank[:, P * k:P * k + P], self.xn[:, P * k:P * k + P],
                                            self.core.ident[:, :])
        last.then_inc(self.turned, 1)

    def keep(self, act, b, u, users):
        act.wait_ge(self.turned, nth(b))
        for sem, value in users:
            act.wait_ge(sem, value)
        self.nc.scalar.copy(self.xnT[u][:, :, :].rearrange("p k t -> p (k t)"), self.bank[:, 0:D]
                            ).then_inc(self.kept, 1)


def wide_attention_layer(nc, core, name, wq, wk, wv, wo, loaded, kv_heads, prep, scale, ctxT=None,
                         tables=None, mask=None, prefetch=()):
    HC = 4
    NC = 4
    KC = kv_heads // NC
    K_PROJ, K_S, K_P, K_O = NC, NC + 1, NC + 2, NC + 3
    with Layer(nc, name) as L:
        sb, sem = L.sb, L.sem
        b_q, b_k, b_v, b_s, b_p, b_o, b_y, b_x = core.bank
        norm = Norm(nc, core, L, b_x)
        two = lambda n, w=512: [sb(f"{n}{i}", [P, w]) for i in range(2)]
        v, qT, kT, dif, prob, oT = two("v", KC * P), two("qT"), two("kT", KC * P), two("dif"), two("prob"), two("oT")
        pT = sb("pT", [P, 512])
        smax, ssum = sb("smax", [P, HC]), sb("ssum", [P, HC])
        srec = two("srec", HC)
        if prep != "direct":
            q_tok, k_tok = sb("q_tok", [P, 512]), sb("k_tok", [P, 512])
        if prep == "rope":
            qa, qb, ka, kb = (sb(n, [P, 512]) for n in ("qa", "qb", "ka", "kb"))
            cos, sin = sb("cos", [P, P]), sb("sin", [P, P])
        if prep == "rms":
            q_sq, k_sq = sb("q_sq", [P, 512]), sb("k_sq", [P, 512])
            ss, rr = sb("ss", [P, 2 * HC]), sb("rr", [P, 2 * HC])
            gains, gain = sb("gains", [P, 2]), sb("gain", [P, 1])
        if mask is not None:
            mrow_u8, mcol_u8 = sb("mrow_u8", [1, NB * P], mybir.dt.uint8), sb("mcol_u8", [P, NB], mybir.dt.uint8)
            mrow, mcol = sb("mrow", [1, NB * P], BF16), sb("mcol", [P, NB])
            one_row = sb("one_row", [1, P], BF16)
            mrow_b = [sb(f"mrow_b{u}", [1, HC, P], BF16) for u in range(2)]
            mcol_b = [sb(f"mcol_b{u}", [P, 1]) for u in range(2)]
        if ctxT is not None:
            cT = two("cT", P)
            ctx_in = [sem(f"ctx_in{u}") for u in range(2)]
        tables_in, tables_done = sem("tables_in"), sem("tables_done")
        n_tables = 0
        (q_made, k_made, v_made, q_parts, k_parts, sq_ready, ss_ready, rr_ready, k_ready, turned,
         qT_kept, kT_kept, v_kept, s_made, d_ready, e_ready, sum_ready, p_ready, p_turned, pT_kept,
         o_made, oT_kept, y_made, y_added) = (sem(n) for n in (
             "q_made", "k_made", "v_made", "q_parts", "k_parts", "sq_ready", "ss_ready", "rr_ready",
             "k_ready", "turned", "qT_kept", "kT_kept", "v_kept", "s_made", "d_ready", "e_ready",
             "sum_ready", "p_ready", "p_turned", "pT_kept", "o_made", "oT_kept", "y_made", "y_added"))
        heads = lambda ap, n=HC: ap.rearrange("p (h w) -> p h w", h=n)
        wide = [P, HC, P]

        with nc.Block() as block:
            @block.sync
            def _(sp):
                if prep == "rope":
                    sp.dma_start(cos[:, :], tables[0]).then_inc(tables_in, 16)
                    sp.dma_start(sin[:, :], tables[1]).then_inc(tables_in, 16)
                elif prep == "rms":
                    sp.dma_start(gains[:, 0:1], tables[0].rearrange("(p o) -> p o", o=1)).then_inc(tables_in, 16)
                    sp.dma_start(gains[:, 1:2], tables[1].rearrange("(p o) -> p o", o=1)).then_inc(tables_in, 16)
                else:
                    sp.dma_start(mrow_u8[:, :], mask[0]).then_inc(tables_in, 16)
                    sp.dma_start(mcol_u8[:, :], mask[1]).then_inc(tables_in, 16)
                if ctxT is not None:
                    def load(b, u):
                        sp.dma_start(cT[u][:, :], ctxT[bass.ds(b, 1), :, :].rearrange("a p t -> (a p) t")
                                     ).then_inc(ctx_in[u], 16)
                    load(0, 0)
                    load(1, 1)
                for fetch in prefetch:
                    fetch(sp)
                if ctxT is not None:
                    with sp.Fori(1, NB // 2) as i:
                        for u in range(2):
                            sp.wait_ge(v_made, nth(NC * (2 * i + u - 2) + NC - 1))
                            load(2 * i + u, u)

            @block.tensor
            def _(pe):
                norm.prime_pe(pe)
                for s in (v_made, k_made, turned, s_made, p_turned, o_made):
                    pe.sem_inc(s, SPARE)
                pe.wait_ge(loaded[0], loaded[1])
                pe.wait_ge(tables_done, 1)

                def turn_probs(it):
                    b, u, c, f = it
                    pe.wait_ge(p_ready, f + 1)
                    pe.wait_ge(pT_kept, nth(f - 1))
                    for j in range(HC):
                        last = nc.tensor.transpose(b_p[:, P * j:P * j + P], prob[c % 2][:, P * j:P * j + P],
                                                   core.ident[:, :])
                    last.then_inc(p_turned, 1)

                def project_out(it):
                    b, u, c, f = it
                    pe.wait_ge(oT_kept, nth(f))
                    if c == 0:
                        pe.wait_ge(y_added, nth(b - 1))
                    for j in range(HC):
                        last = nc.tensor.matmul(b_y[:, 0:D], oT[c % 2][:, P * j:P * j + P],
                                                wo[:, HC * c + j, :], start=(c == 0 and j == 0),
                                                stop=(c == NC - 1 and j == HC - 1))
                    if c == NC - 1:
                        last.then_inc(y_made, 1)

                def turn_qk(it):
                    b, u, c, f = it
                    pe.wait_ge(k_ready, f + 1)
                    for src, bank in ((q_tok, b_q), (k_tok, b_k)):
                        for j in range(HC):
                            last = nc.tensor.transpose(bank[:, P * j:P * j + P], src[:, P * j:P * j + P],
                                                       core.ident[:, :])
                    last.then_inc(turned, 1)

                def heads_out(it):
                    b, u, c, f = it
                    pe.wait_ge(pT_kept, nth(f))
                    pe.wait_ge(v_kept, nth(f))
                    pe.wait_ge(oT_kept, nth(f - 1))
                    for j in range(HC):
                        at = P * (j * KC // HC)
                        last = nc.tensor.matmul(b_o[:, P * j:P * j + P], v[c % 2][:, at:at + P],
                                                pT[:, P * j:P * j + P], start=True, stop=True)
                    last.then_inc(o_made, 1)

                def scores(it):
                    b, u, c, f = it
                    pe.wait_ge(kT_kept, nth(f))
                    pe.wait_ge(qT_kept, nth(f))
                    pe.wait_ge(d_ready, nth(f - 1))
                    if mask is not None:
                        nc.tensor.matmul(b_s[:, :], one_row[:, :], mrow_b[u][:, :, :].rearrange(
                            "p h k -> p (h k)"), start=True, stop=False)
                    for j in range(HC):
                        at = P * (j * KC // HC)
                        last = nc.tensor.matmul(b_s[:, P * j:P * j + P], qT[c % 2][:, P * j:P * j + P],
                                                kT[c % 2][:, at:at + P], start=mask is None,
                                                stop=mask is None or j == HC - 1)
                    last.then_inc(s_made, 1)

                def project_q(it):
                    b, u, c, f = it
                    if c == 0:
                        pe.wait_ge(norm.kept, nth(b))
                        if ctxT is not None:
                            pe.wait_ge(ctx_in[u], ctx_turn(b))
                    pe.wait_ge(qT_kept, nth(f - 1))
                    if prep == "direct":
                        for j in range(HC):
                            for k in range(KD):
                                last = nc.tensor.matmul(b_q[:, P * j:P * j + P],
                                                        wq[:, k, 512 * c + P * j:512 * c + P * j + P],
                                                        norm.xnT[u][:, k, :], start=(k == 0), stop=(k == KD - 1))
                    else:
                        for k in range(KD):
                            last = nc.tensor.matmul(b_q[:, :], norm.xnT[u][:, k, :],
                                                    wq[:, k, 512 * c:512 * c + 512],
                                                    start=(k == 0), stop=(k == KD - 1))
                    last.then_inc(q_made, 1)

                def ctx_turn(b):
                    return 16 * (b // 2 + 1)

                def project_k(it):
                    b, u, c, f = it
                    w = KC * P
                    pe.wait_ge(kT_kept, nth(f - 1))
                    if prep == "direct":
                        for j in range(KC):
                            last = nc.tensor.matmul(b_k[:, P * j:P * j + P],
                                                    wk[:, 0, w * c + P * j:w * c + P * j + P], cT[u][:, :],
                                                    start=True, stop=True)
                    elif ctxT is not None:
                        last = nc.tensor.matmul(b_k[:, 0:w], cT[u][:, :], wk[:, 0, w * c:w * c + w],
                                                start=True, stop=True)
                    else:
                        for k in range(KD):
                            last = nc.tensor.matmul(b_k[:, 0:w], norm.xnT[u][:, k, :],
                                                    wk[:, k, w * c:w * c + w], start=(k == 0), stop=(k == KD - 1))
                    last.then_inc(k_made, 1)

                def project_v(it):
                    b, u, c, f = it
                    w = KC * P
                    pe.wait_ge(v_kept, nth(f - 1))
                    if ctxT is not None:
                        last = nc.tensor.matmul(b_v[:, 0:w], cT[u][:, :], wv[:, 0, w * c:w * c + w],
                                                start=True, stop=True)
                    else:
                        for k in range(KD):
                            last = nc.tensor.matmul(b_v[:, 0:w], norm.xnT[u][:, k, :],
                                                    wv[:, k, w * c:w * c + w], start=(k == 0), stop=(k == KD - 1))
                    last.then_inc(v_made, 1)

                def slot(b, u, c):
                    proj, sc, pr, ou = (behind(b, u, c, k, NC) for k in (K_PROJ, K_S, K_P, K_O))
                    if pr:
                        turn_probs(pr)
                    if c == 2 and behind(b, u, c, 0, NC):
                        norm.turn(pe, b)
                    if ou:
                        project_out(ou)
                    if sc and prep != "direct":
                        turn_qk(sc)
                    if pr:
                        heads_out(pr)
                    if proj:
                        project_q(proj)
                    if sc:
                        scores(sc)
                    if proj:
                        project_k(proj)
                        project_v(proj)

                run_slots(pe, slot, NC, 1, K_O)

            @block.vector
            def _(dve):
                for s in (d_ready, oT_kept, y_added, ss_ready):
                    dve.sem_inc(s, SPARE)
                dve.wait_ge(tables_in, 32)
                if prep == "rms":
                    nc.vector.tensor_tensor(gain[:, :], gains[:, 0:1], gains[:, 1:2], ALU.mult)
                if mask is not None:
                    nc.vector.memset(one_row[:, :], 1.0)
                    nc.vector.tensor_scalar(mrow[:, :], mrow_u8[:, :], -1.0, -NEG, ALU.add, ALU.mult)
                    nc.vector.tensor_copy(mcol[:, :], mcol_u8[:, :])
                dve.drain().then_inc(tables_done, 1)

                def residual(it):
                    b, u, c, f = it
                    dve.wait_ge(y_made, b + 1)
                    xb = pick(core.x[:, :, :], b).rearrange("p a d -> p (a d)")
                    nc.vector.tensor_tensor(xb, b_y[:, 0:D], xb, ALU.add).then_inc(y_added, 1)

                def keep_o(it):
                    b, u, c, f = it
                    dve.wait_ge(o_made, nth(f))
                    nc.vector.tensor_copy(oT[c % 2][:, :], b_o[:, :]).then_inc(oT_kept, 1)

                def less_max(it):
                    b, u, c, f = it
                    dve.wait_ge(s_made, nth(f))
                    nc.vector.tensor_reduce(smax[:, :], heads(b_s[:, :]), AX.X, ALU.max)
                    dve.drain()
                    nc.vector.tensor_tensor(heads(dif[c % 2][:, :]), heads(b_s[:, :]),
                                            smax[:, :].unsqueeze(2).to_broadcast(wide), ALU.subtract
                                            ).then_inc(d_ready, 1)

                def sums(it):
                    b, u, c, f = it
                    dve.wait_ge(e_ready, f + 1)
                    nc.vector.tensor_reduce(ssum[:, :], heads(prob[c % 2][:, :]), AX.X, ALU.add)
                    dve.drain()
                    nc.vector.reciprocal(srec[c % 2][:, :], ssum[:, :]).then_inc(sum_ready, 1)

                def rotate(made, bank, a, b_, parts, it):
                    b, u, c, f = it
                    dve.wait_ge(made, f + 1 if made is q_made else nth(f))
                    if not (isinstance(f, int) and f == 0):
                        dve.wait_ge(k_ready, f)
                    x, y = heads(bank[:, :]), heads(b_[:, :])
                    half = [P, HC, P // 2]
                    nc.vector.tensor_tensor(heads(a[:, :]), x, cos[:, :].unsqueeze(1).to_broadcast(wide), ALU.mult)
                    nc.vector.tensor_tensor(y[:, :, 0:64], x[:, :, 64:128],
                                            sin[:, 0:64].unsqueeze(1).to_broadcast(half), ALU.mult)
                    nc.vector.tensor_tensor(y[:, :, 64:128], x[:, :, 0:64],
                                            sin[:, 64:128].unsqueeze(1).to_broadcast(half), ALU.mult)
                    dve.drain().then_inc(parts, 1)

                def squares(it):
                    b, u, c, f = it
                    for i, sq in enumerate((q_sq, k_sq)):
                        dve.wait_ge(sq_ready, 2 * f + i + 1)
                        nc.vector.tensor_reduce(ss[:, HC * i:HC * i + HC], heads(sq[:, :]), AX.X, ALU.add)
                    dve.drain()
                    nc.vector.tensor_scalar(ss[:, :], ss[:, :], 1.0 / P, LN_EPS, ALU.mult, ALU.add
                                            ).then_inc(ss_ready, 1)

                def scale_qk(it):
                    b, u, c, f = it
                    dve.wait_ge(rr_ready, f + 1)
                    dve.wait_ge(turned, nth(f - 1))
                    for i, (bank, tok) in enumerate(((b_q, q_tok), (b_k, k_tok))):
                        nc.vector.tensor_tensor(heads(tok[:, :]), heads(bank[:, :]),
                                                rr[:, HC * i:HC * i + HC].unsqueeze(2).to_broadcast(wide),
                                                ALU.mult)
                    dve.drain().then_inc(k_ready, 1)

                def slot(b, u, c):
                    proj, sc, pr, ou = (behind(b, u, c, k, NC) for k in (K_PROJ, K_S, K_P, K_O))
                    ln = behind(b, u, c, 0, NC)
                    if ln and c == 0:
                        norm.moments(dve, b)
                    if ou and ou[2] == NC - 1:
                        residual(ou)
                    if pr:
                        keep_o(pr)
                    if ln and c == 1:
                        if mask is not None:
                            nc.vector.tensor_copy(mrow_b[u][:, :, :], mrow[:, bass.ds(P * b, P)].unsqueeze(1)
                                                  .to_broadcast([1, HC, P]))
                            nc.vector.tensor_copy(mcol_b[u][:, :], mcol[:, bass.ds(b, 1)])
                        norm.normalise(dve, b)
                    if proj and prep == "rope":
                        rotate(q_made, b_q, qa, qb, q_parts, proj)
                    if sc:
                        less_max(sc)
                    if proj and prep == "rope":
                        rotate(k_made, b_k, ka, kb, k_parts, proj)
                    if proj and prep == "rms":
                        squares(proj)
                    if sc:
                        sums(sc)
                    if proj and prep == "rms":
                        scale_qk(proj)

                run_slots(dve, slot, NC, 1, K_O)

            @block.scalar
            def _(act):
                norm.prime_act(act)
                for s in (pT_kept, qT_kept, kT_kept, v_kept):
                    act.sem_inc(s, SPARE)
                act.wait_ge(tables_done, 1)

                def keep_probs(it):
                    b, u, c, f = it
                    act.wait_ge(p_turned, nth(f))
                    act.wait_ge(o_made, nth(f - 1))
                    nc.scalar.copy(pT[:, :], b_p[:, :]).then_inc(pT_kept, 1)

                def keep_q(it, made, value):
                    b, u, c, f = it
                    act.wait_ge(made, value)
                    act.wait_ge(s_made, nth(f - 2))
                    if prep == "rms":
                        nc.scalar.activation(qT[c % 2][:, :], b_q[:, :], ACT.Copy, scale=gain[:, 0:1]
                                             ).then_inc(qT_kept, 1)
                    else:
                        nc.scalar.copy(qT[c % 2][:, :], b_q[:, :]).then_inc(qT_kept, 1)

                def keep_k(it, made):
                    b, u, c, f = it
                    act.wait_ge(made, nth(f))
                    act.wait_ge(s_made, nth(f - 2))
                    nc.scalar.copy(kT[c % 2][:, :], b_k[:, 0:KC * P]).then_inc(kT_kept, 1)

                def keep_v(it):
                    b, u, c, f = it
                    act.wait_ge(v_made, nth(f))
                    act.wait_ge(o_made, nth(f - 2))
                    if mask is not None:
                        nc.scalar.activation(v[c % 2][:, :], b_v[:, 0:KC * P], ACT.Copy,
                                             scale=mcol_b[u][:, 0:1]).then_inc(v_kept, 1)
                    else:
                        nc.scalar.copy(v[c % 2][:, :], b_v[:, 0:KC * P]).then_inc(v_kept, 1)

                def exponentials(it):
                    b, u, c, f = it
                    act.wait_ge(d_ready, nth(f))
                    act.wait_ge(p_turned, nth(f - 2))
                    nc.scalar.activation(prob[c % 2][:, :], dif[c % 2][:, :], ACT.Exp, scale=scale
                                         ).then_inc(e_ready, 1)

                def square(it):
                    b, u, c, f = it
                    act.wait_ge(q_made, f + 1)
                    act.wait_ge(ss_ready, nth(f - 1))
                    nc.scalar.activation(q_sq[:, :], b_q[:, :], ACT.Square).then_inc(sq_ready, 1)
                    act.wait_ge(k_made, nth(f))
                    nc.scalar.activation(k_sq[:, :], b_k[:, :], ACT.Square).then_inc(sq_ready, 1)

                def slot(b, u, c):
                    proj, sc, pr, ou = (behind(b, u, c, k, NC) for k in (K_PROJ, K_S, K_P, K_O))
                    if pr:
                        keep_probs(pr)
                    if c == 2 and behind(b, u, c, 0, NC):
                        norm.keep(act, b, u, ((v_made, nth(NC * (b - 2) + NC - 1)),)
                                  if not (isinstance(b, int) and b < 2) else ())
                    if sc and prep != "direct":
                        keep_q(sc, turned, nth(sc[3]))
                        keep_k(sc, turned)
                    if sc:
                        exponentials(sc)
                    if proj and prep == "rms":
                        square(proj)
                    if proj and prep == "direct":
                        keep_q(proj, q_made, proj[3] + 1)
                        keep_k(proj, k_made)
                    if proj:
                        keep_v(proj)

                run_slots(act, slot, NC, 1, K_O)

            @block.gpsimd
            def _(pool):
                def add_parts(it):
                    b, u, c, f = it
                    pool.wait_ge(turned, nth(f - 1))
                    pool.wait_ge(q_parts, f + 1)
                    nc.gpsimd.tensor_tensor(q_tok[:, :], qa[:, :], qb[:, :], ALU.add)
                    pool.wait_ge(k_parts, f + 1)
                    nc.gpsimd.tensor_tensor(k_tok[:, :], ka[:, :], kb[:, :], ALU.add)
                    pool.drain().then_inc(k_ready, 1)

                def rsqrt(it):
                    b, u, c, f = it
                    pool.wait_ge(ss_ready, nth(f))
                    nc.gpsimd.tensor_tensor(rr[:, :], ss[:, :], core.minus_half[:, 0:2 * HC], ALU.pow
                                            ).then_inc(rr_ready, 1)

                def divide(it):
                    b, u, c, f = it
                    pool.wait_ge(sum_ready, f + 1)
                    nc.gpsimd.tensor_tensor(heads(prob[c % 2][:, :]), heads(prob[c % 2][:, :]),
                                            srec[c % 2][:, :].unsqueeze(2).to_broadcast(wide), ALU.mult
                                            ).then_inc(p_ready, 1)

                def slot(b, u, c):
                    proj, sc, pr, ou = (behind(b, u, c, k, NC) for k in (K_PROJ, K_S, K_P, K_O))
                    if c == 0 and behind(b, u, c, 0, NC):
                        norm.rsqrt(pool, b)
                    if proj and prep == "rope":
                        add_parts(proj)
                    if proj and prep == "rms":
                        rsqrt(proj)
                    if sc:
                        divide(sc)

                run_slots(pool, slot, NC, 1, K_O)


def small_attention_layer(nc, core, name, weights, loaded, kind, scale, tables, ctxT=None, prefetch=()):
    HC = 4
    HD = {"axial": 8}.get(kind, 16)
    H = {"axial": 32, "summed": 4}.get(kind, 16)
    NC = H // HC
    R = HC * HD
    NF = -(-H * HD // P)
    F = H * HD // NF
    causal = kind in ("summed", "grouped")
    split = kind == "split"
    W = (HD + 1) * (2 if split else 1)
    lag = 0 if NC == 1 else 1
    K_PROJ, K_QK = NC, NC
    K_S = 2 * NC
    K_P, K_O, K_T, K_Y = K_S + lag, K_S + 2 * lag, K_S + 2 * lag + 1, K_S + 2 * lag + 2
    peeled = -(-(K_Y + 1) // (2 * NC))
    QW = 384 if kind in ("summed", "grouped") else D
    wq, wkv, wo = weights["q"], weights.get("kv"), weights["o"]
    with Layer(nc, name) as L:
        sb, sem = L.sb, L.sem
        b_s, b_p, b_q, b_kv, b_t1, b_t2, b_o = (core.bank[0:2], core.bank[2], core.bank[3], core.bank[4],
                                                core.bank[5], core.bank[6], core.bank[7])
        norm = Norm(nc, core, L, b_q)
        qT = [sb(f"qT{u}", [P, NF, P]) for u in range(2)]
        kX = [sb(f"kX{u}", [P, NF, HC, P]) for u in range(2)]
        v = [sb(f"v{u}", [P, H, W]) for u in range(2)]
        dif = [sb(f"dif{i}", [P, HC, P]) for i in range(2)]
        prob = [sb(f"prob{i}", [P, HC, P]) for i in range(2)]
        pT = [sb(f"pT{i}", [P, HC, P]) for i in range(2)]
        smax = sb("smax", [P, 2, HC])
        orec = sb("orec", [P, 2, HC])
        o_two = sb("o_two", [P, 2, HC, HD])
        o_tok = [sb(f"o_tok{u}", [P, NF * P // HD, HD]) for u in range(2)]
        oT = sb("oT", [P, NF, P])
        q_tok, k_tok = sb("q_tok", [P, NF * P]), sb("k_tok", [P, NF * P])
        yb = sb("yb", [P, D])
        if ctxT is not None:
            cT = [sb(f"cT{u}", [P, P]) for u in range(2)]
            ctx_in = [sem(f"ctx_in{u}") for u in range(2)]
            if split:
                cT2 = [sb(f"cT2{u}", [P, P]) for u in range(2)]
        consts = {n: sb(f"t_{n}", shape, dt) for n, (shape, dt, _) in tables.items()}
        masks = consts["masks"]
        if causal:
            ident_b, mask_b = sb("ident_b", [P, P], BF16), sb("mask_b", [P, HC, P], BF16)
        if kind == "axial":
            rot = sb("rot", [P, D])
            sin_t, cos_t, turns = (sb(n, [P, NB, HD]) for n in ("sin_t", "cos_t", "turns"))
            whole, angles_ready = sb("whole", [P, NB, HD], I32), sem("angles_ready")
        if kind == "summed":
            rot, raw, pair = sb("rot", [P, D]), sb("raw", [P, 384]), sb("pair", [P, 2, 4, 16])
        if kind == "grouped":
            rot, raw, turnd = sb("rot", [P, 320]), sb("raw", [P, 384]), sb("turnd", [P, 320])
        if kind == "split":
            rot, raw, v_raw = sb("rot", [P, 512]), sb("raw", [P, 512]), sb("v_raw", [P, D])

        if kind in ("grouped", "split"):
            n_rr = 20 if kind == "grouped" else 32
            ss, rr = sb("ss", [P, n_rr]), sb("rr", [P, n_rr])
        tables_in, tables_done, ctx_zeroed = sem("tables_in"), sem("tables_done"), sem("ctx_zeroed")
        (q_made, kv_made, qk_ready, qk_turned, qT_kept, kX_kept, v_kept, s_made, d_ready, e_ready, p_turned,
         pT_kept, o_made, o_kept, o_turned, oT_kept, y_made, y_kept, ss_ready, rr_ready) = (sem(n) for n in (
             "q_made", "kv_made", "qk_ready", "qk_turned", "qT_kept", "kX_kept", "v_kept", "s_made", "d_ready",
             "e_ready", "p_turned", "pT_kept", "o_made", "o_kept", "o_turned", "oT_kept", "y_made",
             "y_kept", "ss_ready", "rr_ready"))
        wide = [P, HC, P]
        MAIN = P - 16

        with nc.Block() as block:
            @block.sync
            def _(sp):
                for n, (_, _, source) in tables.items():
                    ap = consts[n][tuple(slice(None) for _ in consts[n].shape)]
                    if len(consts[n].shape) == 3:
                        ap = ap.rearrange("p a b -> p (a b)")
                    for rows, src in source:
                        sp.dma_start(ap[rows, :], src).then_inc(tables_in, 16)
                if ctxT is not None:
                    if split:
                        sp.wait_ge(ctx_zeroed, 1)

                    def load(b, u):
                        src = ctxT[bass.ds(b, 1), :, :].rearrange("a p t -> (a p) t")
                        if split:
                            sp.dma_start(cT[u][:, 0:MAIN], src[:, 0:MAIN]).then_inc(ctx_in[u], 16)
                            sp.dma_start(cT2[u][:, MAIN:], src[:, MAIN:]).then_inc(ctx_in[u], 16)
                        else:
                            sp.dma_start(cT[u][:, :], src).then_inc(ctx_in[u], 16)
                    load(0, 0)
                    load(1, 1)
                for fetch in prefetch:
                    fetch(sp)
                if ctxT is not None:
                    with sp.Fori(1, NB // 2) as i:
                        for u in range(2):
                            sp.wait_ge(kv_made, nth(2 * i + u - 2))
                            load(2 * i + u, u)

            @block.tensor
            def _(pe):
                norm.prime_pe(pe)
                for s in (kv_made, qk_turned, s_made, p_turned, o_made, o_turned, y_made):
                    pe.sem_inc(s, SPARE)
                pe.wait_ge(loaded[0], loaded[1])
                pe.wait_ge(tables_done, 1)

                def project(b, u):
                    pe.wait_ge(norm.kept, nth(b))
                    pe.wait_ge(qk_ready, nth(b - 1))
                    for k in range(KD):
                        last = nc.tensor.matmul(b_q[:, 0:QW], norm.xnT[u][:, k, :], wq[:, k, :],
                                                start=(k == 0), stop=(k == KD - 1))
                    if ctxT is not None:
                        last.then_inc(q_made, 1)
                        pe.wait_ge(ctx_in[u], (32 if split else 16) * (b // 2 + 1))
                        pe.wait_ge(v_kept, nth(b - 1))
                        last = nc.tensor.matmul(b_kv[:, :], cT[u][:, :], wkv[:, 0, :], start=True, stop=not split)
                        if split:
                            last = nc.tensor.matmul(b_kv[:, :], cT2[u][:, :], wkv[:, 1, :], start=False, stop=True)
                    last.then_inc(kv_made, 1)

                def turn_qk(b, u):
                    pe.wait_ge(qk_ready, nth(b))
                    pe.wait_ge(kX_kept, nth(b - 1))
                    pe.wait_ge(qT_kept, nth(b - 1))
                    for i, src in enumerate((q_tok, k_tok)):
                        for k in range(NF):
                            at = 2 * P * i + P * k
                            last = nc.tensor.transpose(b_t2[:, at:at + P], src[:, P * k:P * k + P],
                                                       core.ident[:, :])
                    last.then_inc(qk_turned, 1)

                def scores(it):
                    b, u, c, f = it
                    if c == 0:
                        pe.wait_ge(qT_kept, nth(b))
                        pe.wait_ge(kX_kept, nth(b))
                    pe.wait_ge(d_ready, nth(f - 2))
                    i = c % 2 if NC > 1 else u
                    if causal:
                        nc.tensor.matmul(b_s[i][:, :], ident_b[:, :], mask_b[:, :, :].rearrange(
                            "p h k -> p (h k)"), start=True, stop=False)
                    at, k = R * c % F, R * c // F
                    nc.tensor.matmul(b_s[i][:, :], qT[u][at:at + R, k, :],
                                     kX[u][at:at + R, k, :, :].rearrange("p h k -> p (h k)"),
                                     start=not causal, stop=True).then_inc(s_made, 1)

                def turn_probs(it):
                    b, u, c, f = it
                    i = c % 2 if NC > 1 else u
                    pe.wait_ge(e_ready, f + 1)
                    pe.wait_ge(pT_kept, nth(f - 1))
                    for j in range(HC):
                        last = nc.tensor.transpose(b_p[:, P * j:P * j + P], prob[i][:, j, :], core.ident[:, :])
                    last.then_inc(p_turned, 1)

                def heads_out(it):
                    b, u, c, f = it
                    i = c % 2 if NC > 1 else u
                    if c == 0:
                        pe.wait_ge(v_kept, nth(b))
                    pe.wait_ge(pT_kept, nth(f))
                    pe.wait_ge(o_kept, nth(f - 1))
                    for j in range(HC):
                        last = nc.tensor.matmul(b_o[:, W * j:W * j + W], pT[i][:, j, :],
                                                v[u][:, HC * c + j, :], start=True, stop=True)
                    last.then_inc(o_made, 1)

                def turn_out(b, u):
                    pe.wait_ge(o_kept, nth(NC * b + NC - 1))
                    pe.wait_ge(y_kept, nth(b - 1))
                    for k in range(NF):
                        last = nc.tensor.transpose(b_t1[:, P * k:P * k + P],
                                                   o_tok[u][:, :, :].rearrange("p h d -> p (h d)")[:, P * k:P * k + P],
                                                   core.ident[:, :])
                    last.then_inc(o_turned, 1)

                def project_out(b, u):
                    pe.wait_ge(oT_kept, nth(b))
                    for k in range(NF):
                        last = nc.tensor.matmul(b_t1[:, 0:D], oT[0:F, k, :], wo[0:F, k, :],
                                                start=(k == 0), stop=(k == NF - 1))
                    last.then_inc(y_made, 1)

                def slot(b, u, c):
                    pj, sc, pr, ou, tn, fin = (behind(b, u, c, k, NC) for k in (K_PROJ, K_S, K_P, K_O, K_T, K_Y))
                    if sc:
                        scores(sc)
                    if pj and c == 0:
                        project(pj[0], pj[1])
                    if fin and fin[2] == NC - 1:
                        project_out(fin[0], fin[1])
                    if pr:
                        turn_probs(pr)
                    if tn and tn[2] == NC - 1:
                        turn_out(tn[0], tn[1])
                    if ou:
                        heads_out(ou)
                    if pj and c == NC - 1:
                        turn_qk(pj[0], pj[1])
                    if c == NC - 1 and behind(b, u, c, 0, NC):
                        held(pe, qk_ready, nth(b - 1))
                        norm.turn(pe, b)

                run_slots(pe, slot, NC, peeled, K_Y)

            @block.vector
            def _(dve):
                for s in (d_ready, kX_kept, v_kept, o_kept, y_kept, qk_ready, ss_ready):
                    dve.sem_inc(s, SPARE)
                for u in range(2):
                    nc.vector.memset(v[u][:, :, :], 1.0)
                    if F < P:
                        nc.vector.memset(o_tok[u][:, :, :], 0.0)
                if F < P:
                    nc.vector.memset(q_tok[:, :], 0.0)
                    nc.vector.memset(k_tok[:, :], 0.0)
                if split:
                    for u in range(2):
                        nc.vector.memset(cT[u][:, :], 0.0)
                        nc.vector.memset(cT2[u][:, :], 0.0)
                dve.drain().then_inc(ctx_zeroed, 1)
                dve.wait_ge(tables_in, 16 * sum(len(t[2]) for t in tables.values()))
                if kind == "axial":
                    for i, angle in enumerate((sin_t, cos_t)):
                        a4 = angle[:, :, :].rearrange("p b (q h e) -> p b q h e", q=2, h=2)
                        for q in range(2):
                            for h in range(2):
                                for e in range(2):
                                    nc.vector.tensor_scalar(a4[:, :, q, h, e], consts["pos"][:, :, q],
                                                            FREQ[h], i * PI / 2, ALU.mult, ALU.add)
                        dve.drain()
                        nc.vector.tensor_scalar(turns[:, :, :], angle[:, :, :], 1 / (2 * PI), None, ALU.mult)
                        dve.drain()
                        nc.vector.tensor_copy(whole[:, :, :], turns[:, :, :])
                        dve.drain()
                        nc.vector.tensor_copy(turns[:, :, :], whole[:, :, :])
                        dve.drain()
                        nc.vector.scalar_tensor_tensor(angle[:, :, :], turns[:, :, :], -2 * PI, angle[:, :, :],
                                                       ALU.mult, ALU.add)
                        for op, bound, step in ((ALU.is_gt, PI, -2 * PI), (ALU.is_lt, -PI, 2 * PI)):
                            dve.drain()
                            nc.vector.tensor_scalar(turns[:, :, :], angle[:, :, :], bound, step, op, ALU.mult)
                            dve.drain()
                            nc.vector.tensor_tensor(angle[:, :, :], angle[:, :, :], turns[:, :, :], ALU.add)
                        dve.drain()
                        nc.vector.tensor_scalar(angle[:, :, :], angle[:, :, :], PI, -PI, ALU.min, ALU.max
                                                ).then_inc(angles_ready, 1)
                    dve.wait_ge(angles_ready, 4)
                    nc.vector.tensor_scalar(sin_t[:, :, 0::2], sin_t[:, :, 0::2], -1.0, None, ALU.mult)
                if causal:
                    nc.vector.tensor_copy(ident_b[:, :], core.ident[:, :])
                    nc.vector.tensor_copy(mask_b[:, :, :], consts["causal"][:, :].unsqueeze(1).to_broadcast(wide))
                if split:
                    for u in range(2):
                        for i in range(2):
                            at = (HD + 1) * (i + 1) - 1
                            nc.vector.tensor_copy(v[u][:, :, at], consts["part"][:, i:i + 1].to_broadcast([P, H]))
                dve.drain().then_inc(tables_done, 1)

                def prepare(b, u):
                    PREPARE[kind](b, u)

                def axial(b, u):
                    dve.wait_ge(q_made, b + 1)
                    dve.wait_ge(qk_turned, nth(b - 1))
                    cs = cos_t[:, bass.ds(b, 1), :].to_broadcast([P, H, HD])
                    for src, tok, made in ((b_q[:, 0:D], q_tok, None), (b_kv[:, 0:D], k_tok, kv_made)):
                        if made is not None:
                            dve.drain()
                            dve.wait_ge(made, nth(b))
                        x = src.rearrange("p (h d) -> p h d", h=H)
                        t = tok[:, :].rearrange("p (h d) -> p h d", h=H)
                        nc.vector.tensor_tensor(t, x, cs, ALU.mult)
                        r = rot[:, :].rearrange("p (h d) -> p h d", h=H)
                        for i in range(2):
                            sn = sin_t[:, bass.ds(b, 1), i::2].to_broadcast([P, H, HD // 2])
                            nc.vector.tensor_tensor(r[:, :, i::2], x[:, :, 1 - i::2], sn, ALU.mult)
                        dve.drain()
                        nc.vector.tensor_tensor(tok[:, :], tok[:, :], rot[:, :], ALU.add)
                    dve.drain().then_inc(qk_ready, 1)

                def values_axial(b, u):
                    dve.wait_ge(kv_made, nth(b))
                    held(dve, o_made, nth(NC * (b - 2) + NC - 1))
                    nc.vector.tensor_copy(v[u][:, :, 0:HD], b_kv[:, D:2 * D].rearrange("p (h d) -> p h d", h=H)
                                          ).then_inc(v_kept, 1)

                def summed(b, u):
                    dve.wait_ge(kv_made, nth(b))
                    dve.wait_ge(qk_turned, nth(b - 1))
                    nc.vector.tensor_tensor(raw[:, :], b_q[:, 0:384], consts["bias"][:, :], ALU.add)
                    dve.drain()
                    nc.vector.tensor_reduce(pair[:, 0, :, :], raw[:, 0:D].rearrange("p (h g d) -> p h d g", h=4, g=4),
                                            AX.X, ALU.add)
                    nc.vector.tensor_copy(pair[:, 1, :, :], raw[:, D:D + 64].rearrange("p (h d) -> p h d", h=4))
                    dve.drain()
                    x = pair[:, :, :, :].rearrange("p a h d -> p (a h) d")
                    cs = consts["cos"][:, :].unsqueeze(1).to_broadcast([P, 8, 8])
                    sn = consts["sin"][:, :].unsqueeze(1).to_broadcast([P, 8, 8])
                    parts = [rot[:, 64 * i:64 * i + 64].rearrange("p (h d) -> p h d", h=8) for i in range(4)]
                    nc.vector.tensor_tensor(parts[0], x[:, :, 0::2], cs, ALU.mult)
                    nc.vector.tensor_tensor(parts[1], x[:, :, 1::2], sn, ALU.mult)
                    nc.vector.tensor_tensor(parts[2], x[:, :, 0::2], sn, ALU.mult)
                    nc.vector.tensor_tensor(parts[3], x[:, :, 1::2], cs, ALU.mult)
                    dve.drain()
                    for i, tok in enumerate((q_tok, k_tok)):
                        t = tok[:, 0:64].rearrange("p (h d) -> p h d", h=4)
                        s = slice(4 * i, 4 * i + 4)
                        nc.vector.tensor_tensor(t[:, :, 0:8], parts[0][:, s, :], parts[1][:, s, :], ALU.subtract)
                        nc.vector.tensor_tensor(t[:, :, 8:16], parts[2][:, s, :], parts[3][:, s, :], ALU.add)
                    dve.drain().then_inc(qk_ready, 1)

                def values_raw(b, u):
                    held(dve, o_made, nth(NC * (b - 2) + NC - 1))
                    src = raw[:, D + 64:D + 128].rearrange("p (h d) -> p h d", h=4)
                    if kind == "grouped":
                        for r in range(4):
                            nc.vector.tensor_copy(v[u][:, r::4, 0:HD], src)
                    else:
                        nc.vector.tensor_copy(v[u][:, :, 0:HD], src)
                    dve.drain().then_inc(v_kept, 1)

                def grouped(b, u):
                    dve.wait_ge(kv_made, nth(b))
                    dve.wait_ge(qk_turned, nth(b - 1))
                    nc.vector.tensor_tensor(raw[:, :], b_q[:, 0:384], consts["bias"][:, :], ALU.add)
                    dve.drain()
                    x = raw[:, 0:320].rearrange("p (h d) -> p h d", h=20)
                    r = rot[:, :].rearrange("p (h d) -> p h d", h=20)
                    nc.vector.tensor_tensor(r, x, x, ALU.mult)
                    dve.drain()
                    nc.vector.tensor_reduce(ss[:, :], r, AX.X, ALU.add)
                    dve.drain()
                    nc.vector.tensor_scalar(ss[:, :], ss[:, :], 1.0 / HD, 1.1920929e-07, ALU.mult, ALU.add
                                            ).then_inc(ss_ready, 1)
                    a = turnd[:, :].rearrange("p (h d) -> p h d", h=20)
                    nc.vector.tensor_tensor(a, x, consts["cos"][:, :].unsqueeze(1).to_broadcast([P, 20, HD]), ALU.mult)
                    for i in range(2):
                        lo, hi = 8 * i, 8 * i + 8
                        nc.vector.tensor_tensor(r[:, :, lo:hi], x[:, :, 8 - lo:16 - lo],
                                                consts["sin"][:, lo:hi].unsqueeze(1).to_broadcast([P, 20, 8]),
                                                ALU.mult)
                    dve.drain()
                    nc.vector.tensor_tensor(a, a, r, ALU.add)
                    dve.wait_ge(rr_ready, b + 1)
                    nc.vector.tensor_tensor(ss[:, :], rr[:, :], consts["gain"][:, :], ALU.mult)
                    dve.drain()
                    nc.vector.tensor_tensor(q_tok[:, :].rearrange("p (h d) -> p h d", h=16), a[:, 0:16, :],
                                            ss[:, 0:16].unsqueeze(2).to_broadcast([P, 16, HD]), ALU.mult)
                    k4 = k_tok[:, :].rearrange("p (h r d) -> p h r d", h=4, r=4)
                    for i in range(4):
                        nc.vector.tensor_tensor(k4[:, :, i, :], a[:, 16:20, :],
                                                ss[:, 16:20].unsqueeze(2).to_broadcast([P, 4, HD]), ALU.mult)
                    dve.drain().then_inc(qk_ready, 1)

                def layered(b, u):
                    dve.wait_ge(q_made, b + 1)
                    dve.wait_ge(kv_made, nth(b))
                    n = 2 * H
                    x = raw[:, 0:2 * D].rearrange("p (h d) -> p h d", h=n)
                    kv = b_kv[:, :].rearrange("p (h a d) -> p h a d", h=H, a=2)
                    bias = consts["bias"][:, D:].rearrange("p (h a d) -> p h a d", h=H, a=2)
                    nc.vector.tensor_tensor(raw[:, 0:D], b_q[:, 0:D], consts["bias"][:, 0:D], ALU.add)
                    nc.vector.tensor_tensor(x[:, H:, :], kv[:, :, 0, :], bias[:, :, 0, :], ALU.add)
                    nc.vector.tensor_tensor(v_raw[:, :].rearrange("p (h d) -> p h d", h=H), kv[:, :, 1, :],
                                            bias[:, :, 1, :], ALU.add)
                    dve.drain()
                    wide_h = [P, n, HD]
                    nc.vector.tensor_reduce(ss[:, :], x, AX.X, ALU.add)
                    dve.drain()
                    nc.vector.tensor_scalar(ss[:, :], ss[:, :], 1.0 / HD, None, ALU.mult)
                    dve.drain()
                    nc.vector.tensor_tensor(x, x, ss[:, :].unsqueeze(2).to_broadcast(wide_h), ALU.subtract)
                    dve.drain()
                    r = rot[:, :].rearrange("p (h d) -> p h d", h=n)
                    nc.vector.tensor_tensor(r, x, x, ALU.mult)
                    dve.drain()
                    nc.vector.tensor_reduce(ss[:, :], r, AX.X, ALU.add)
                    dve.drain()
                    nc.vector.tensor_scalar(ss[:, :], ss[:, :], 1.0 / HD, 1e-6, ALU.mult, ALU.add
                                            ).then_inc(ss_ready, 1)
                    dve.wait_ge(rr_ready, b + 1)
                    nc.vector.tensor_tensor(x, x, rr[:, :].unsqueeze(2).to_broadcast(wide_h), ALU.mult)
                    dve.drain()
                    dve.wait_ge(qk_turned, nth(b - 1))
                    for i, tok in enumerate((q_tok, k_tok)):
                        t = tok[:, :].rearrange("p (h d) -> p h d", h=H)
                        w, s = (consts[m][:, HD * i:HD * i + HD].unsqueeze(1).to_broadcast([P, H, HD])
                                for m in ("affine_w", "affine_b"))
                        nc.vector.tensor_tensor(t, x[:, H * i:H * i + H, :], w, ALU.mult)
                        dve.drain()
                        nc.vector.tensor_tensor(t, t, s, ALU.add)
                    dve.drain().then_inc(qk_ready, 1)

                def values_split(b, u):
                    held(dve, o_made, nth(NC * (b - 2) + NC - 1))
                    src = v_raw[:, :].rearrange("p (h d) -> p h d", h=H)
                    for i in range(2):
                        at = (HD + 1) * i
                        nc.vector.tensor_scalar(v[u][:, :, at:at + HD], src, consts["part"][:, i:i + 1], None, ALU.mult)
                    dve.drain().then_inc(v_kept, 1)

                PREPARE = {"axial": axial, "summed": summed, "grouped": grouped, "split": layered}
                VALUES = {"axial": values_axial, "summed": values_raw, "grouped": values_raw, "split": values_split}

                def keep_kX(b, u):
                    dve.wait_ge(qT_kept, nth(b))
                    held(dve, s_made, nth(NC * (b - 2) + NC - 1))
                    for j in range(HC):
                        nc.vector.tensor_scalar(kX[u][0:F, :, j, :], b_t2[0:F, D:D + P * NF].rearrange(
                            "p (k t) -> p k t", k=NF), masks[0:F, j:j + 1], None, ALU.mult)
                    dve.drain().then_inc(kX_kept, 1)

                def less_max(it):
                    b, u, c, f = it
                    i = c % 2 if NC > 1 else u
                    dve.wait_ge(s_made, nth(f))
                    s = b_s[i][:, :].rearrange("p (h k) -> p h k", h=HC)
                    for a, (lo, hi) in enumerate(((0, MAIN), (MAIN, P)) if split else ((0, P),)):
                        nc.vector.tensor_reduce(smax[:, a, :], s[:, :, lo:hi], AX.X, ALU.max)
                        dve.drain()
                        last = nc.vector.tensor_tensor(
                            dif[i][:, :, lo:hi], s[:, :, lo:hi],
                            smax[:, a, :].unsqueeze(2).to_broadcast([P, HC, hi - lo]), ALU.subtract)
                    dve.drain().then_inc(d_ready, 1)

                def keep_out(it):
                    b, u, c, f = it
                    i = c % 2 if NC > 1 else u
                    dve.wait_ge(o_made, nth(f))
                    if c == 0:
                        dve.wait_ge(o_turned, nth(b - 2))
                    o = b_o[:, 0:HC * W].rearrange("p (h w) -> p h w", h=HC)
                    out = o_tok[u][:, HC * c:HC * c + HC, :]
                    n = 2 if split else 1
                    for a in range(n):
                        nc.vector.reciprocal(orec[:, a, :], o[:, :, (HD + 1) * (a + 1) - 1])
                    dve.drain()
                    for a in range(n):
                        nc.vector.tensor_tensor(out if n == 1 else o_two[:, a, :, :],
                                                o[:, :, (HD + 1) * a:(HD + 1) * a + HD],
                                                orec[:, a, :].unsqueeze(2).to_broadcast([P, HC, HD]), ALU.mult)
                    if split:
                        dve.drain()
                        nc.vector.tensor_tensor(out, o_two[:, 0, :, :], o_two[:, 1, :, :], ALU.add)
                    dve.drain().then_inc(o_kept, 1)

                def residual(b, u):
                    dve.drain()
                    dve.wait_ge(y_made, nth(b))
                    xb = pick(core.x[:, :, :], b).rearrange("p a d -> p (a d)")
                    nc.vector.tensor_tensor(yb[:, :], b_t1[:, 0:D], consts["out_bias"][:, :], ALU.add
                                            ).then_inc(y_kept, 1)
                    dve.drain()
                    nc.vector.tensor_tensor(xb, xb, yb[:, :], ALU.add)

                def slot(b, u, c):
                    pj, sc, pr, ou, tn, fin = (behind(b, u, c, k, NC) for k in (K_PROJ, K_S, K_P, K_O, K_T, K_Y))
                    if sc:
                        less_max(sc)
                    if pj and c == 0:
                        prepare(pj[0], pj[1])
                    if fin and fin[2] == NC - 1:
                        residual(fin[0], fin[1])
                    if c == NC - 1 and behind(b, u, c, 0, NC):
                        norm.moments(dve, b)
                        norm.normalise(dve, b)
                    if ou:
                        keep_out(ou)
                    if pj and c == NC - 1:
                        VALUES[kind](pj[0], pj[1])
                        keep_kX(pj[0], pj[1])

                run_slots(dve, slot, NC, peeled, K_Y)

            @block.scalar
            def _(act):
                norm.prime_act(act)
                if kind == "axial":
                    act.wait_ge(angles_ready, 2)
                    for angle in (sin_t, cos_t):
                        nc.scalar.activation(angle[:, :, :], angle[:, :, :], ACT.Sin).then_inc(angles_ready, 1)
                for s in (qT_kept, pT_kept, oT_kept):
                    act.sem_inc(s, SPARE)

                def exponentials(it):
                    b, u, c, f = it
                    i = c % 2 if NC > 1 else u
                    act.wait_ge(d_ready, nth(f))
                    act.wait_ge(p_turned, nth(f - 2))
                    nc.scalar.activation(prob[i][:, :, :], dif[i][:, :, :], ACT.Exp, scale=scale).then_inc(e_ready, 1)

                def keep_probs(it):
                    b, u, c, f = it
                    i = c % 2 if NC > 1 else u
                    act.wait_ge(p_turned, nth(f))
                    act.wait_ge(o_made, nth(f - 2))
                    nc.scalar.copy(pT[i][:, :, :].rearrange("p h k -> p (h k)"), b_p[:, :]).then_inc(pT_kept, 1)

                def keep_oT(b, u):
                    act.wait_ge(o_turned, nth(b))
                    act.wait_ge(y_made, nth(b - 1))
                    nc.scalar.copy(oT[0:F, :, :].rearrange("p k t -> p (k t)"), b_t1[0:F, 0:NF * P]
                                   ).then_inc(oT_kept, 1)

                def keep_qT(b, u):
                    act.wait_ge(qk_turned, nth(b))
                    held(act, s_made, nth(NC * (b - 2) + NC - 1))
                    nc.scalar.copy(qT[u][0:F, :, :].rearrange("p k t -> p (k t)"), b_t2[0:F, 0:NF * P]
                                   ).then_inc(qT_kept, 1)

                def slot(b, u, c):
                    pj, sc, pr, ou, tn, fin = (behind(b, u, c, k, NC) for k in (K_PROJ, K_S, K_P, K_O, K_T, K_Y))
                    if sc:
                        exponentials(sc)
                    if pr:
                        keep_probs(pr)
                    if tn and tn[2] == NC - 1:
                        keep_oT(tn[0], tn[1])
                    if pj and c == NC - 1:
                        keep_qT(pj[0], pj[1])
                    if c == NC - 1 and behind(b, u, c, 0, NC):
                        norm.keep(act, b, u, ((kv_made, nth(b - 2)),) if not (isinstance(b, int) and b < 2) else ())

                run_slots(act, slot, NC, peeled, K_Y)

            @block.gpsimd
            def _(pool):
                def rsqrt(b):
                    pool.wait_ge(ss_ready, nth(b))
                    nc.gpsimd.tensor_tensor(rr[:, :], ss[:, :], core.minus_half[:, 0:n_rr], ALU.pow).then_inc(rr_ready, 1)

                def slot(b, u, c):
                    pj = behind(b, u, c, K_PROJ, NC)
                    if pj and c == 0 and kind in ("grouped", "split"):
                        rsqrt(pj[0])
                    if c == NC - 1 and behind(b, u, c, 0, NC):
                        norm.rsqrt(pool, b)

                run_slots(pool, slot, NC, peeled, K_Y)


def linear_attention_layer(nc, core, name, weights, loaded, tables, prefetch=()):
    H, HD, EPS = 16, 16, 1e-6
    HF = P // HD
    KVW = P + HF
    wqk, wv, wo = weights
    K_PROJ, K_KV, K_OUT, K_Y = 1, 2, 3, 4
    peeled = 3
    with Layer(nc, name) as L:
        sb, sem = L.sb, L.sem
        b_qk, b_v, b_x, b_t, b_kv, b_o, b_ot, b_y = core.bank
        norm = Norm(nc, core, L, b_x)
        raw, low, e = sb("raw", [P, 512]), sb("low", [P, 512]), sb("e", [P, 512])
        feat = [sb(f"feat{u}", [P, 512]) for u in range(2)]
        v = [sb(f"v{u}", [P, KD, KVW]) for u in range(2)]
        qT = [sb(f"qT{u}", [P, KD, P]) for u in range(2)]
        kv = sb("kv", [P, KD, KVW])
        den, o_tok, oT, yb = sb("den", [P, KD, HF]), sb("o_tok", [P, D]), sb("oT", [P, KD, P]), sb("yb", [P, D])
        consts = {n: sb(f"t_{n}", [P, w]) for n, (w, _) in tables.items()}
        tables_in, tables_done = sem("tables_in"), sem("tables_done")
        (qkv_made, low_ready, e_ready, feat_ready, turned, qT_kept, kv_made, kv_kept, o_made, o_kept,
         o_turned, oT_kept, y_made, y_kept) = (sem(n) for n in (
             "qkv_made", "low_ready", "e_ready", "feat_ready", "turned", "qT_kept", "kv_made", "kv_kept",
             "o_made", "o_kept", "o_turned", "oT_kept", "y_made", "y_kept"))

        with nc.Block() as block:
            @block.sync
            def _(sp):
                for n, (_, src) in tables.items():
                    sp.dma_start(consts[n][:, :], src).then_inc(tables_in, 16)
                for fetch in prefetch:
                    fetch(sp)

            @block.tensor
            def _(pe):
                norm.prime_pe(pe)
                for s in (turned, kv_made, o_made, o_turned, y_made):
                    pe.sem_inc(s, SPARE)
                pe.wait_ge(loaded[0], loaded[1])

                def project(b, u):
                    pe.wait_ge(norm.kept, nth(b))
                    pe.wait_ge(feat_ready, nth(b - 1))
                    for bank, w, n in ((b_qk, wqk, 512), (b_v, wv, D)):
                        for k in range(KD):
                            last = nc.tensor.matmul(bank[:, 0:n], norm.xnT[u][:, k, :], w[:, k, :],
                                                    start=(k == 0), stop=(k == KD - 1))
                    last.then_inc(qkv_made, 1)

                def key_value(b, u):
                    pe.wait_ge(feat_ready, nth(b))
                    pe.wait_ge(qT_kept, nth(b - 1))
                    for k in range(KD):
                        last = nc.tensor.transpose(b_t[:, P * k:P * k + P], feat[u][:, P * k:P * k + P],
                                                   core.ident[:, :])
                    last.then_inc(turned, 1)
                    pe.wait_ge(kv_kept, nth(b - 1))
                    for k in range(KD):
                        last = nc.tensor.matmul(b_kv[:, KVW * k:KVW * k + KVW], feat[u][:, D + P * k:D + P * k + P],
                                                v[u][:, k, :], start=True, stop=True)
                    last.then_inc(kv_made, 1)

                def outputs(b, u):
                    pe.wait_ge(kv_kept, nth(b))
                    pe.wait_ge(qT_kept, nth(b))
                    pe.wait_ge(o_kept, nth(b - 1))
                    for k in range(KD):
                        last = nc.tensor.matmul(b_o[:, KVW * k:KVW * k + KVW], qT[u][:, k, :], kv[:, k, :],
                                                start=True, stop=True)
                    last.then_inc(o_made, 1)

                def turn_out(b, u):
                    pe.wait_ge(o_kept, nth(b))
                    pe.wait_ge(oT_kept, nth(b - 1))
                    for k in range(KD):
                        last = nc.tensor.transpose(b_ot[:, P * k:P * k + P], o_tok[:, P * k:P * k + P], core.ident[:, :])
                    last.then_inc(o_turned, 1)

                def project_out(b, u):
                    pe.wait_ge(oT_kept, nth(b))
                    pe.wait_ge(y_kept, nth(b - 1))
                    for k in range(KD):
                        last = nc.tensor.matmul(b_y[:, 0:D], oT[:, k, :], wo[:, k, :],
                                                start=(k == 0), stop=(k == KD - 1))
                    last.then_inc(y_made, 1)

                def slot(b, u, c):
                    pj, kvs, out, fin = (behind(b, u, c, k, 1) for k in (K_PROJ, K_KV, K_OUT, K_Y))
                    if fin:
                        turn_out(fin[0], fin[1])
                    if kvs:
                        key_value(kvs[0], kvs[1])
                    if fin:
                        project_out(fin[0], fin[1])
                    if pj:
                        project(pj[0], pj[1])
                    if out:
                        outputs(out[0], out[1])
                    if behind(b, u, c, 0, 1):
                        norm.turn(pe, b)

                run_slots(pe, slot, 1, peeled, K_Y)

            @block.vector
            def _(dve):
                for s in (low_ready, feat_ready, kv_kept, o_kept, y_kept):
                    dve.sem_inc(s, SPARE)
                for u in range(2):
                    nc.vector.memset(v[u][:, :, :], 1.0)
                dve.wait_ge(tables_in, 16 * len(tables))

                def features(b, u):
                    dve.wait_ge(qkv_made, b + 1)
                    nc.vector.tensor_tensor(raw[:, :], b_qk[:, :], consts["qk_bias"][:, :], ALU.add)
                    dve.drain()
                    nc.vector.tensor_scalar(low[:, :], raw[:, :], 0.0, None, ALU.min).then_inc(low_ready, 1)
                    held(dve, kv_made, nth(b - 2))
                    nc.vector.tensor_tensor(v[u][:, :, 0:P], b_v[:, 0:D].rearrange("p (k e) -> p k e", k=KD),
                                            consts["v_bias"][:, :].rearrange("p (k e) -> p k e", k=KD), ALU.add)
                    dve.wait_ge(e_ready, b + 1)
                    nc.vector.scalar_tensor_tensor(feat[u][:, :], raw[:, :], 0.0, e[:, :], ALU.max, ALU.add
                                                   ).then_inc(feat_ready, 1)

                def keep_kv(b, u):
                    dve.wait_ge(kv_made, nth(b))
                    dve.wait_ge(o_made, nth(b - 1))
                    nc.vector.tensor_tensor(kv[:, :, :], b_kv[:, 0:KD * KVW].rearrange("p (k e) -> p k e", k=KD),
                                            consts["own_head"][:, :].unsqueeze(1).to_broadcast([P, KD, KVW]),
                                            ALU.mult).then_inc(kv_kept, 1)

                def keep_out(b, u):
                    dve.wait_ge(o_made, nth(b))
                    o = b_o[:, 0:KD * KVW].rearrange("p (k e) -> p k e", k=KD)
                    nc.vector.tensor_scalar(den[:, :, :], o[:, :, P:], EPS, None, ALU.add)
                    dve.drain()
                    nc.vector.reciprocal(den[:, :, :], den[:, :, :])
                    dve.drain()
                    dve.wait_ge(o_turned, nth(b - 1))
                    for k in range(KD):
                        last = nc.vector.tensor_tensor(
                            o_tok[:, P * k:P * k + P].rearrange("p (h d) -> p h d", h=HF),
                            o[:, k, 0:P].rearrange("p (h d) -> p h d", h=HF),
                            den[:, k, :].unsqueeze(2).to_broadcast([P, HF, HD]), ALU.mult)
                    last.then_inc(o_kept, 1)

                def residual(b, u):
                    dve.drain()
                    dve.wait_ge(y_made, nth(b))
                    xb = pick(core.x[:, :, :], b).rearrange("p a d -> p (a d)")
                    nc.vector.tensor_tensor(yb[:, :], b_y[:, 0:D], consts["out_bias"][:, :], ALU.add
                                            ).then_inc(y_kept, 1)
                    dve.drain()
                    nc.vector.tensor_tensor(xb, xb, yb[:, :], ALU.add)

                def slot(b, u, c):
                    pj, kvs, out, fin = (behind(b, u, c, k, 1) for k in (K_PROJ, K_KV, K_OUT, K_Y))
                    if kvs:
                        keep_kv(kvs[0], kvs[1])
                    if fin:
                        residual(fin[0], fin[1])
                    if pj:
                        features(pj[0], pj[1])
                    if out:
                        keep_out(out[0], out[1])
                    if behind(b, u, c, 0, 1):
                        norm.moments(dve, b)
                        norm.normalise(dve, b)

                run_slots(dve, slot, 1, peeled, K_Y)

            @block.scalar
            def _(act):
                norm.prime_act(act)
                for s in (qT_kept, oT_kept):
                    act.sem_inc(s, SPARE)

                def slot(b, u, c):
                    pj, kvs, out, fin = (behind(b, u, c, k, 1) for k in (K_PROJ, K_KV, K_OUT, K_Y))
                    if fin:
                        act.wait_ge(o_turned, nth(fin[0]))
                        held(act, y_made, nth(fin[0] - 1))
                        nc.scalar.copy(oT[:, :, :].rearrange("p k t -> p (k t)"), b_ot[:, 0:D]).then_inc(oT_kept, 1)
                    if kvs:
                        act.wait_ge(turned, nth(kvs[0]))
                        held(act, o_made, nth(kvs[0] - 2))
                        nc.scalar.copy(qT[kvs[1]][:, :, :].rearrange("p k t -> p (k t)"), b_t[:, 0:D]
                                       ).then_inc(qT_kept, 1)
                    if pj:
                        act.wait_ge(low_ready, nth(pj[0]))
                        act.wait_ge(feat_ready, nth(pj[0] - 1))
                        nc.scalar.activation(e[:, :], low[:, :], ACT.Exp).then_inc(e_ready, 1)
                    if behind(b, u, c, 0, 1):
                        norm.keep(act, b, u, ((feat_ready, nth(b - 2)),) if not (isinstance(b, int) and b < 2) else ())

                run_slots(act, slot, 1, peeled, K_Y)

            @block.gpsimd
            def _(pool):
                def slot(b, u, c):
                    if behind(b, u, c, 0, 1):
                        norm.rsqrt(pool, b)

                run_slots(pool, slot, 1, peeled, K_Y)


def look_up_layer(nc, core, name, idx_in, idx_down, lut, w_in, w_down):
    n_in, (width, n_down) = idx_in.shape[1], idx_down.shape
    with Layer(nc, name) as L:
        sb, sem = L.sb, L.sem
        parts = []
        for n, rows, cols in (("in", P, n_in), ("down", width, n_down)):
            parts.append((rows, cols, sb(f"i_{n}", [rows, cols], I32), sb(f"idx_{n}", [rows, cols], BF16),
                          sb(f"hit_{n}", [rows, cols], BF16), sb(f"w_{n}", [rows, cols])))
        table = sb("table", [P, 16])
        loaded, decoded, stored = sem("loaded"), sem("decoded"), sem("stored")
        with nc.Block() as block:
            @block.sync
            def _(sp):
                sp.dma_start(table[:, :], lut.partition_broadcast(P)).then_inc(loaded, 16)
                for (rows, cols, i, *_), src in zip(parts, (idx_in, idx_down)):
                    sp.dma_start(i[:, :], src).then_inc(loaded, 16)
                sp.wait_ge(decoded, 1)
                (_, _, _, _, _, w1), (_, _, _, _, _, w2) = parts
                slices = w_in.shape[0]
                sp.dma_start(w_in.rearrange("s p w -> p s w"),
                             w1[:, :].rearrange("p (s w) -> p s w", s=slices)).then_inc(stored, 16)
                sp.dma_start(w_down.rearrange("s p w -> p s w"),
                             w2[:, :].rearrange("p (s w) -> p s w", s=slices)).then_inc(stored, 16)
                sp.wait_ge(stored, 32)

            @block.vector
            def _(dve):
                dve.wait_ge(loaded, 48)
                for _, _, i, idx, _, w in parts:
                    nc.vector.tensor_copy(idx[:, :], i[:, :])
                    nc.vector.memset(w[:, :], 0.0)
                dve.drain()
                for j in range(16):
                    for rows, _, _, idx, hit, w in parts:
                        nc.vector.tensor_scalar(hit[:, :], idx[:, :], float(j), None, ALU.is_equal)
                        dve.drain()
                        nc.vector.scalar_tensor_tensor(w[:, :], hit[:, :], table[0:rows, j:j + 1], w[:, :],
                                                       ALU.mult, ALU.add)
                dve.drain().then_inc(decoded, 1)


def slices_in(*weights):
    a = np.stack([w.reshape(w.shape[0], KD, P, w.shape[2]) for w in weights], 1)
    n, g, k, p, w = a.shape
    return np.ascontiguousarray(a.transpose(0, 3, 1, 2, 4)).reshape(n, p, g * k * w)


def cut_columns(w, width):
    return w.reshape(w.shape[0], -1, width).transpose(1, 0, 2)


def falling(n):
    return np.ascontiguousarray(np.broadcast_to(np.arange(n, 0, -1, dtype=np.float32), (P, NB, n))
                                ).reshape(P, NB * n)


def rows_in(w):
    k = w.shape[0] // P
    return w.reshape(k, P, -1).transpose(1, 0, 2).reshape(P, -1)


def rope_angles(dim):
    f = np.float32
    freq = f(1.0) / np.power(f(10000.0), np.arange(0, dim, 2, dtype=f) / f(dim), dtype=f)
    angle = np.arange(P, dtype=f)[:, None] * freq[None, :]
    return np.cos(angle), np.sin(angle)


def lay_out(i):
    a = {"x": i["x"], "ident": np.eye(P, dtype=np.float32)}
    a["falling8"], a["falling4"], a["falling16"], a["falling32"] = (falling(n) for n in (8, 4, 16, 32))
    a["below"] = np.triu(np.ones((P, P), np.float32), 1)
    cat = np.concatenate
    a["l1f_in"] = slices_in(cat([i["L1_ffn_W_gate"], cut_columns(i["L1_ffn_shared_gate"].T, 128)]),
                            cat([i["L1_ffn_W_up"], cut_columns(i["L1_ffn_shared_up"].T, 128)]))
    a["l1f_down"] = cat([i["L1_ffn_W_down"], i["L1_ffn_shared_down"].T.reshape(2, 128, D)])
    a["l1f_router"] = i["L1_ffn_router_w"].T
    a["l1f_bias"] = i["L1_ffn_e_bias"]
    w1, w3 = ((w.reshape(8, D, 2, 88).transpose(0, 2, 1, 3).reshape(16, D, 88))
              for w in (i["L2_ffn_w1"], i["L2_ffn_w3"]))
    a["l2f_in"] = slices_in(cat([w1, cut_columns(i["L2_ffn_ws1"], 88)]),
                            cat([w3, cut_columns(i["L2_ffn_ws3"], 88)]))
    a["l2f_down"] = cat([i["L2_ffn_w2"].reshape(16, 88, D), i["L2_ffn_ws2"].reshape(4, 88, D)])
    a["l2f_router"] = i["L2_ffn_w_router"]
    a["l3f_in"] = slices_in(cat([i["L3_ffn_w_up"], cut_columns(i["L3_ffn_shared_up"], 128)]))
    a["l3f_down"] = cat([i["L3_ffn_w_down"], i["L3_ffn_shared_down"].reshape(4, 128, D)])
    a["l3f_router"] = i["L3_ffn_router_weight"].T
    a["l3f_bias"] = i["L3_ffn_e_bias"]
    a["ctxT"] = i["ctx_1024"].transpose(0, 2, 1)
    mask = i["mask_BxS2_bf1"].view(np.uint8)
    a["mask_row"], a["mask_col"] = mask.reshape(1, NB * P), mask.T
    col, row = np.arange(P)[None, :], np.arange(P)[:, None]
    a["causal"] = np.where(col <= row, 0.0, NEG).astype(np.float32)
    a["masks8"], a["masks16"] = ((row // n % 4 == np.arange(4)[None, :]).astype(np.float32) for n in (8, 16))
    a["part"] = np.concatenate([row < P - 16, row >= P - 16], 1).astype(np.float32)
    slots_ = lambda t, n: np.ascontiguousarray(t.transpose(1, 0, 2)).reshape(t.shape[1], n)
    a["l0f_idx_in"] = slots_(slices_in(cut_columns(i["L0_ffn_gate_idx"].T, 86),
                                       cut_columns(i["L0_ffn_up_idx"].T, 86)), 8 * 344)
    a["l0f_idx_down"] = slots_(i["L0_ffn_down_idx"].T.reshape(8, 86, D), 8 * D)
    a["l0f_lut"] = i["L0_ffn_lut"]
    a["l0a_qk"] = rows_in(cat([i["L0_attn_q_w"], i["L0_attn_k_w"]], 0).T)
    a["l0a_v"], a["l0a_o"] = rows_in(i["L0_attn_v_w"].T), rows_in(i["L0_attn_o_w"].T)
    a["l0a_bqk"] = cat([i["L0_attn_q_b"], i["L0_attn_k_b"]])
    a["l0a_bv"], a["l0a_bo"] = i["L0_attn_v_b"], i["L0_attn_o_b"]
    heads8 = row // 16
    a["own_head"] = cat([heads8 == col // 16, heads8 == np.arange(8)[None, :]], 1).astype(np.float32)
    a["pos"] = i["fside_BxSx2_0"].transpose(1, 0, 2)
    a["l0x_q"], a["l0x_kv"], a["l0x_o"] = (rows_in(i["L0_xattn_W" + n]) for n in ("q", "kv", "out"))
    a["l0x_bo"] = i["L0_xattn_bout"]
    cat1 = lambda names: cat([i[n] for n in names], -1)
    a["l1a_q"] = rows_in(cat1(["L1_attn_Wq", "L1_attn_Wk", "L1_attn_Wv"]))
    a["l1a_b"] = cat1(["L1_attn_bq", "L1_attn_bk", "L1_attn_bv"])
    a["l1a_o"], a["l1a_bo"] = i["L1_attn_Wo"], i["L1_attn_bo"]
    a["cos8"], a["sin8"] = rope_angles(16)
    c, s = a["cos8"], a["sin8"]
    a["cos16"], a["sin16"] = cat([c, c], 1), cat([s, -s], 1)
    a["l2a_q"] = rows_in(cat([i["L2_attn_Wq"], i["L2_attn_Wk"], i["L2_attn_Wv"]], 0).T)
    a["l2a_b"] = cat1(["L2_attn_bq", "L2_attn_bk", "L2_attn_bv"])
    a["l2a_o"], a["l2a_bo"] = rows_in(i["L2_attn_Wo"].T), i["L2_attn_bo"]
    a["l2a_gain"] = cat([i["L2_attn_q_gain"], np.ones(4, np.float32)])
    by_head = lambda w: w.reshape(-1, 2, 16, 16).transpose(0, 2, 1, 3).reshape(-1, 512)
    a["l2x_q"], a["l2x_o"], a["l2x_bo"] = rows_in(i["L2_xattn_Wq"]), rows_in(i["L2_xattn_Wo"]), i["L2_xattn_bo"]
    a["l2x_kv"] = cat([i["L2_xattn_Wk"], i["L2_xattn_Wv"], by_head(i["L2_xattn_Wkv_dca"])], 1)
    a["l2x_b"] = cat1(["L2_xattn_bq", "L2_xattn_bk", "L2_xattn_bv"])
    a["l2x_bd"] = cat([i["L2_xattn_bq"], by_head(i["L2_xattn_bkv_dca"])[0]])
    for n in "wb":
        a["l2x_" + n + "1"] = cat1(["L2_xattn_qn_" + n, "L2_xattn_kn_" + n])
        a["l2x_" + n + "2"] = cat1(["L2_xattn_qn_" + n, "L2_xattn_kn_dca_" + n])
    a["l1x_q"], a["l1x_k"], a["l1x_v"] = (rows_in(i["L1_xattn_W" + n]) for n in "qkv")
    a["l1x_o"] = rows_in(i["L1_xattn_Wo"])
    qkv = i["L3_attn_w_qkv"].T
    a["l3a_q"], a["l3a_k"], a["l3a_v"] = (rows_in(qkv[:, 2048 * n:2048 * (n + 1)]) for n in range(3))
    a["l3a_o"] = rows_in(i["L3_attn_w_out"].T)
    a["l3x_q"], a["l3x_k"], a["l3x_v"] = (rows_in(i["L3_xattn_W" + n]) for n in "qkv")
    a["l3x_o"] = rows_in(i["L3_xattn_Wo"])
    a["l3x_gq"], a["l3x_gk"] = i["L3_xattn_gq"], i["L3_xattn_gk"]
    c, s = rope_angles(P)
    a["l3a_cos"], a["l3a_sin"] = np.concatenate([c, c], 1), np.concatenate([-s, s], 1)
    return {k: np.ascontiguousarray(v) for k, v in a.items()}


def program(nc, a, out, layers):
    with ExitStack() as ctx:
        core = Core(nc, ctx, a)
        l1x_w, l1x_in, l1x_fetch = claim(nc, core, core.far, 0, "l1x", (
            (a["l1x_q"], P, (KD, 2048)), (a["l1x_k"], P, (1, 1024)), (a["l1x_v"], P, (1, 1024)),
            (a["l1x_o"], P, (16, D))))
        l3a_w, l3a_in, l3a_fetch = claim(nc, core, core.far, 0, "l3a", (
            (a["l3a_q"], P, (KD, 2048)), (a["l3a_k"], P, (KD, 2048)), (a["l3a_v"], P, (KD, 2048)),
            (a["l3a_o"], P, (16, D))))
        l3x_w, l3x_in, l3x_fetch = claim(nc, core, core.near, 0, "l3x", (
            (a["l3x_q"], P, (KD, 2048)), (a["l3x_k"], P, (1, 2048)), (a["l3x_v"], P, (1, 2048)),
            (a["l3x_o"], P, (16, D))))
        l0a_w, l0a_in, l0a_fetch = claim(nc, core, core.near, 0, "l0a", (
            (a["l0a_qk"], P, (KD, 512)), (a["l0a_v"], P, (KD, D)), (a["l0a_o"], P, (KD, D))))
        l0x_w, l0x_in, l0x_fetch = claim(nc, core, core.near, 2560, "l0x", (
            (a["l0x_q"], P, (KD, D)), (a["l0x_kv"], P, (1, 512)), (a["l0x_o"], P, (KD, D))))
        l1a_w, l1a_in, l1a_fetch = claim(nc, core, core.near, 4096, "l1a", (
            (a["l1a_q"], P, (KD, 384)), (a["l1a_o"], 64, (1, D))))
        l2a_w, l2a_in, l2a_fetch = claim(nc, core, core.near, 5120, "l2a", (
            (a["l2a_q"], P, (KD, 384)), (a["l2a_o"], P, (KD, D))))
        l2x_w, l2x_in, l2x_fetch = claim(nc, core, core.near, 6400, "l2x", (
            (a["l2x_q"], P, (KD, D)), (a["l2x_kv"], P, (2, 512)), (a["l2x_o"], P, (KD, D))))
        every, main, dca = slice(0, P), slice(0, P - 16), slice(P - 16, P)
        bc = lambda n, rows=P: a[n].partition_broadcast(rows)
        small = {
            "l0x": (dict(zip(("q", "kv", "o"), l0x_w)), l0x_in, "axial", 8 ** -0.5, {
                "masks": ([P, 4], F32, [(every, a["masks8"])]),
                "pos": ([P, NB, 2], F32, [(every, a["pos"].rearrange("p b q -> p (b q)"))]),
                "out_bias": ([P, D], F32, [(every, bc("l0x_bo"))])}, a["ctxT"]),
            "l1a": (dict(zip(("q", "o"), l1a_w)), l1a_in, "summed", 0.25, {
                "masks": ([P, 4], F32, [(every, a["masks16"])]),
                "causal": ([P, P], F32, [(every, a["causal"])]),
                "bias": ([P, 384], F32, [(every, bc("l1a_b"))]),
                "cos": ([P, 8], F32, [(every, a["cos8"])]), "sin": ([P, 8], F32, [(every, a["sin8"])]),
                "out_bias": ([P, D], F32, [(every, bc("l1a_bo"))])}),
            "l2a": (dict(zip(("q", "o"), l2a_w)), l2a_in, "grouped", 0.25, {
                "masks": ([P, 4], F32, [(every, a["masks16"])]),
                "causal": ([P, P], F32, [(every, a["causal"])]),
                "bias": ([P, 384], F32, [(every, bc("l2a_b"))]),
                "gain": ([P, 20], F32, [(every, bc("l2a_gain"))]),
                "cos": ([P, 16], F32, [(every, a["cos16"])]), "sin": ([P, 16], F32, [(every, a["sin16"])]),
                "out_bias": ([P, D], F32, [(every, bc("l2a_bo"))])}),
            "l2x": (dict(zip(("q", "kv", "o"), l2x_w)), l2x_in, "split", 0.25, {
                "masks": ([P, 4], F32, [(every, a["masks16"])]),
                "part": ([P, 2], F32, [(every, a["part"])]),
                "bias": ([P, 768], F32, [(main, bc("l2x_b", P - 16)), (dca, bc("l2x_bd", 16))]),
                "affine_w": ([P, 32], F32, [(main, bc("l2x_w1", P - 16)), (dca, bc("l2x_w2", 16))]),
                "affine_b": ([P, 32], F32, [(main, bc("l2x_b1", P - 16)), (dca, bc("l2x_b2", 16))]),
                "out_bias": ([P, D], F32, [(every, bc("l2x_bo"))])}, a["ctxT"]),
        }
        fetches = {"begin": [l0a_fetch, l0x_fetch, l1a_fetch, l2a_fetch, l2x_fetch, l1x_fetch], "l1f": [l3a_fetch], "l2f": [l3x_fetch]}
        first = layers[0]
        if first != LAYERS[0]:
            fetches = {"begin": [f for n, f in (("l0a", l0a_fetch), ("l0x", l0x_fetch), ("l1a", l1a_fetch), ("l2a", l2a_fetch), ("l2x", l2x_fetch),
                                                 ("l1x", l1x_fetch), ("l3a", l3a_fetch), ("l3x", l3x_fetch))
                                 if n in layers]}
        get = lambda n: fetches.get(n, ())
        load_constants(nc, core, a["x"], a["ident"], get("begin"))
        l0f_in = nc.dram_tensor("l0f_w_in", (8, P, 344), F32).ap()
        l0f_down = nc.dram_tensor("l0f_w_down", (8, 86, D), F32).ap()
        if "l0f" in layers:
            look_up_layer(nc, core, "lut", a["l0f_idx_in"], a["l0f_idx_down"], a["l0f_lut"], l0f_in, l0f_down)
        for name in layers:
            if name == "l0a":
                linear_attention_layer(nc, core, name, l0a_w, l0a_in, {
                    "qk_bias": (512, bc("l0a_bqk")), "v_bias": (D, bc("l0a_bv")), "out_bias": (D, bc("l0a_bo")),
                    "own_head": (136, a["own_head"])})
            if name == "l0f":
                ffn_layer(nc, core, name, l0f_in, l0f_down, 86, "silu")
            if name in small:
                small_attention_layer(nc, core, name, *small[name])
            elif name == "l1x":
                wide_attention_layer(nc, core, name, *l1x_w, l1x_in, 8, "direct", 128 ** -0.5, a["ctxT"],
                                     mask=(a["mask_row"], a["mask_col"]))
            elif name == "l3a":
                wide_attention_layer(nc, core, name, *l3a_w, l3a_in, 16, "rope", 128 ** -0.5,
                                     tables=(a["l3a_cos"], a["l3a_sin"]))
            elif name == "l3x":
                wide_attention_layer(nc, core, name, *l3x_w, l3x_in, 16, "rms", 128 ** -0.5, a["ctxT"],
                                     tables=(a["l3x_gq"], a["l3x_gk"]))
            elif name == "l1f":
                ffn_layer(nc, core, name, a["l1f_in"], a["l1f_down"], 128, "silu",
                          make_router(nc, core, a["l1f_router"], a["l1f_bias"], (a["falling32"], a["falling8"]),
                                      32, 8, 3, 4, 2.5, 1e-20, 80, a["below"]), prefetch=get(name))
            elif name == "l2f":
                ffn_layer(nc, core, name, a["l2f_in"], a["l2f_down"], 88, "silu",
                          make_router(nc, core, a["l2f_router"], None, (a["falling8"],),
                                      8, 0, 0, 2, 1.0, 0.0, per=2), per=2, prefetch=get(name))
            elif name == "l3f":
                ffn_layer(nc, core, name, a["l3f_in"], a["l3f_down"], 128, "relu2",
                          make_router(nc, core, a["l3f_router"], a["l3f_bias"], (a["falling16"], a["falling4"]),
                                      16, 4, 2, 2, 1.0, 1e-20), prefetch=get(name))
        store_result(nc, core, out)


LAYERS = ["l0a", "l0x", "l0f", "l1a", "l1x", "l1f", "l2a", "l2x", "l2f", "l3a", "l3x", "l3f"]


def kernel(**inputs):
    import concourse.bacc as bacc
    from concourse.bass_utils import run_bass_kernel_spmd

    nc = bacc.Bacc("TRN2", target_bir_lowering=False, num_devices=1)
    arrays = lay_out({k: np.asarray(v) for k, v in inputs.items()})
    aps = {k: nc.dram_tensor(f"in_{k}", v.shape, mybir.dt.from_np(v.dtype), kind="ExternalInput").ap()
           for k, v in arrays.items()}
    out = nc.dram_tensor("out", (NB, P, D), F32, kind="ExternalOutput").ap()
    program(nc, aps, out, LAYERS)
    result = run_bass_kernel_spmd(nc, [{f"in_{k}": v for k, v in arrays.items()}], core_ids=[0])
    return result.results[0]["out"]
```

```python
from contextlib import ExitStack

import numpy as np

import concourse.bass as bass
from concourse import mybir

ALU = mybir.AluOpType
ACT = mybir.ActivationFunctionType
AX = mybir.AxisListType
F32 = mybir.dt.float32
BF16 = mybir.dt.bfloat16
I32 = mybir.dt.int32

P = 128
NB = 16
D = 256
KD = D // P
DCTX = 128
GRP = 4
NG = NB // GRP
LN_EPS = 1e-5
PI = float(np.pi)
FREQ = (1.0, 0.01)
NEG = -1e30
SPARE = 2


def nth(k):
    return k + 1 + SPARE


def held(eng, sem, value):
    if not isinstance(value, int) or value > SPARE:
        eng.wait_ge(sem, value)


def pick(ap, i):
    return ap[:, bass.ds(i, 1)]


class Layer:

    def __init__(self, nc, name):
        self.nc, self.name, self.stack, self.sems = nc, name, ExitStack(), []

    def __enter__(self):
        return self

    def sb(self, name, shape, dtype=F32):
        return self.stack.enter_context(self.nc.sbuf_tensor(f"{self.name}_{name}", shape, dtype))

    def sem(self, name):
        s = self.nc.alloc_semaphore(f"{self.name}_{name}")
        self.sems.append(s)
        return s

    def __exit__(self, *exc):
        if exc[0] is None:
            self.nc.clear_and_free_semaphores(self.sems)
            self.nc.all_engine_barrier()
        self.stack.close()
        return False


class Core:

    def __init__(self, nc, ctx, consts):
        self.nc = nc
        sb = lambda n, s, d=F32: ctx.enter_context(nc.sbuf_tensor(n, s, d))
        self.x = sb("x_res", [P, NB, D])
        self.ident = sb("ident", [P, P])
        self.ones = sb("ones", [P, P])
        self.minus_half = sb("minus_half", [P, 32])
        self.far = sb("far", [P, 16384])
        self.near = sb("near", [P, 12288])
        self.arrived = {}
        self.bank = [ctx.enter_context(nc.psum_tensor(f"bank{i}", [P, 512], F32)) for i in range(8)]


def claim(nc, core, arena, at, name, parts):
    arrived = nc.alloc_semaphore(f"{name}_weights_in")
    views, todo = [], []
    for source, rows, shape in parts:
        n = int(np.prod(shape))
        flat = arena[0:rows, at:at + n]
        names = " ".join(f"d{i}" for i in range(len(shape)))
        sizes = {f"d{i}": s for i, s in enumerate(shape)}
        views.append(flat.rearrange(f"p ({names}) -> p {names}", **sizes))
        todo.append((flat, source))
        at += n

    def fetch(sp):
        for flat, source in todo:
            sp.dma_start(flat, source).then_inc(arrived, 16)

    return views, (arrived, 16 * len(parts)), fetch


def load_constants(nc, core, x_in, ident_in, prefetch=()):
    with Layer(nc, "begin") as L:
        loaded = L.sem("loaded")
        with nc.Block() as block:
            @block.sync
            def _(sp):
                sp.dma_start(core.x[:, :, :], x_in.rearrange("b p d -> p b d")).then_inc(loaded, 16)
                sp.dma_start(core.ident[:, :], ident_in).then_inc(loaded, 16)
                for fetch in prefetch:
                    fetch(sp)
                sp.wait_ge(loaded, 32)

            @block.vector
            def _(dve):
                nc.vector.memset(core.ones[:, :], 1.0)
                nc.vector.memset(core.minus_half[:, :], -0.5)


def store_result(nc, core, out):
    with Layer(nc, "end") as L:
        stored = L.sem("stored")
        with nc.Block() as block:
            @block.sync
            def _(sp):
                sp.dma_start(out.rearrange("b p d -> p b d"), core.x[:, :, :]).then_inc(stored, 16)
                sp.wait_ge(stored, 16)


def top_first(nc, dve, v, k, n, iota, work, sel):
    eq, top = work["eq"], work["top"]
    rows = v.shape[1]
    wide = [P, rows, n]
    for r in range(k):
        dve.drain()
        nc.vector.tensor_reduce(top, v, AX.X, ALU.max)
        dve.drain()
        nc.vector.tensor_tensor(eq, v, top.unsqueeze(2).to_broadcast(wide), ALU.is_equal)
        dve.drain()
        nc.vector.tensor_tensor(eq, eq, iota, ALU.mult)
        dve.drain()
        nc.vector.tensor_reduce(top, eq, AX.X, ALU.max)
        dve.drain()
        nc.vector.tensor_tensor(eq, eq, top.unsqueeze(2).to_broadcast(wide), ALU.is_equal)
        dve.drain()
        if r == 0:
            nc.vector.tensor_copy(sel, eq)
        else:
            nc.vector.tensor_tensor(sel, sel, eq, ALU.add)
        nc.vector.scalar_tensor_tensor(v, eq, NEG, v, ALU.mult, ALU.add)
    dve.drain()


def ffn_layer(nc, core, name, w_in, w_down, width, act, router=None, per=1, prefetch=()):
    gated = act == "silu"
    slices = w_in.shape[0]
    halves = 2 if gated else 1
    experts = router["experts"] if router else 0
    placed = router["placed"] if router else None
    with Layer(nc, name) as L:
        sb, sem = L.sb, L.sem
        stats = sb("stats", [P, GRP, 6])
        mv = sb("mv", [P, GRP, 2])
        var = sb("var", [P, GRP])
        rstd = sb("rstd", [P, GRP])
        xn = sb("xn", [P, GRP, D])
        if placed is None:
            xnT = sb("xnT", [P, KD, NB * P])
        else:
            xnT = core.far[:, 0:KD * NB * P].rearrange("p (k t) -> p k t", k=KD)
        wi = [sb(f"wi{u}", [P, halves, KD, width]) for u in range(2)]
        wd = [sb(f"wd{u}", [width, D]) for u in range(2)]
        s = [sb(f"s{u}", [width, 512]) for u in range(2)]
        h = [sb(f"h{u}", [width, 512]) for u in range(2)]
        combine = sb("combine", [P, NB, slices])
        if router:
            wr = sb("wr", [P, KD, experts])
            xg = sb("xg", [P, KD, 512])
            logits = sb("logits", [P, NB, experts])
        b_T, b_log = core.bank[0:2], core.bank[2]
        b_g, b_u, b_y = core.bank[0:2], core.bank[2:4], core.bank[4:8]

        var_ready, rstd_ready, xn_ready = sem("var_ready"), sem("rstd_ready"), sem("xn_ready")
        turned, xnT_ready, xg_ready = sem("turned"), sem("xnT_ready"), sem("xg_ready")
        logits_made, logits_kept, scored = sem("logits_made"), sem("logits_kept"), sem("scored")
        combined, router_in = sem("combined"), sem("router_in")
        wi_loaded = [sem(f"wi_loaded{u}") for u in range(2)]
        wd_loaded = [sem(f"wd_loaded{u}") for u in range(2)]
        gu_made, act_done, h_ready, y_made, y_added = (
            sem("gu_made"), sem("act_done"), sem("h_ready"), sem("y_made"), sem("y_added"))
        picked, counted, hi_made = sem("picked"), sem("counted"), sem("hi_made")

        with nc.Block() as block:
            @block.sync
            def _(sp):
                def load(n, u):
                    sp.dma_start(wi[u][:, :, :, :].rearrange("p a k w -> p (a k w)"),
                                 w_in[bass.ds(n, 1), :, :].rearrange("a p w -> (a p) w")
                                 ).then_inc(wi_loaded[u], 16)
                    sp.dma_start(wd[u][:, :], w_down[bass.ds(n, 1), :, :].rearrange("a p w -> (a p) w")
                                 ).then_inc(wd_loaded[u], 16)

                if router:
                    sp.dma_start(wr[:, :, :], router["w"].rearrange("(k p) e -> p k e", k=KD)
                                 ).then_inc(router_in, 16)
                    router["load"](sp, L, router_in)
                load(0, 0)
                load(1, 1)
                for fetch in prefetch:
                    fetch(sp)
                if slices > 2:
                    with sp.Fori(1, slices // 2) as i:
                        for u in range(2):
                            sp.wait_ge(y_made, nth(4 * (2 * i + u - 2) + 3))
                            load(2 * i + u, u)

            @block.vector
            def _(dve):
                dve.sem_inc(h_ready, SPARE)
                dve.sem_inc(y_added, SPARE)
                dve.sem_inc(logits_kept, SPARE)
                with dve.Fori(0, NG) as g:
                    for t in range(GRP):
                        nc.vector.bn_stats(stats[:, t, :], core.x[:, bass.ds(GRP * g + t, 1), :])
                    dve.drain()
                    for t in range(GRP):
                        nc.vector.bn_aggr(mv[:, t, :], stats[:, t, :])
                    dve.drain()
                    nc.vector.tensor_scalar(var[:, :], mv[:, :, 1], LN_EPS, None, ALU.add
                                            ).then_inc(var_ready, 1)
                    dve.wait_ge(rstd_ready, g + 1)
                    dve.wait_ge(turned, nth(g - 1))
                    for t in range(GRP):
                        last = nc.vector.tensor_scalar(
                            xn[:, t, :], core.x[:, bass.ds(GRP * g + t, 1), :],
                            mv[:, t, 0:1], rstd[:, t:t + 1], ALU.subtract, ALU.mult)
                    last.then_inc(xn_ready, 1)
                    if placed:
                        dve.wait_ge(hi_made, g + 1)
                        nc.vector.tensor_tensor(placed.x_lo[:, bass.ds(GRP * g, GRP), :], xn[:, :, :],
                                                placed.x_hi[:, bass.ds(GRP * g, GRP), :], ALU.subtract)
                        dve.drain()
                    if router:
                        dve.wait_ge(logits_made, nth(g))
                        nc.vector.tensor_copy(logits[:, bass.ds(GRP * g, GRP), :],
                                              b_log[:, 0:GRP * experts].rearrange("p (t e) -> p t e", t=GRP)
                                              ).then_inc(logits_kept, 1)
                nc.vector.memset(combine[:, :, 0 if placed else experts * per:], 1.0)
                if router:
                    router["choose"](dve, L, logits, combine, scored, picked, counted, router_in)
                dve.drain()

                def hidden(f, g):
                    dve.wait_ge(act_done, nth(f))
                    dve.wait_ge(y_made, nth(f - 2))
                    if gated:
                        nc.vector.tensor_tensor(h[g % 2][:, :], s[g % 2][:, :], b_u[g % 2][0:width, :],
                                                ALU.mult).then_inc(h_ready, 1)
                    else:
                        nc.vector.tensor_tensor(h[g % 2][:, :], s[g % 2][:, :], s[g % 2][:, :],
                                                ALU.mult).then_inc(h_ready, 1)

                def add(f, n, g):
                    dve.wait_ge(y_made, nth(f))
                    for t in range(GRP):
                        b = GRP * g + t
                        y = b_y[2 * (g % 2) + t // 2][:, 256 * (t % 2):256 * (t % 2) + 256]
                        last = nc.vector.scalar_tensor_tensor(
                            core.x[:, b, :], y, combine[:, b, bass.ds(n, 1)], core.x[:, b, :],
                            ALU.mult, ALU.add)
                    last.then_inc(y_added, 1)

                for u in range(2):
                    for g in range(NG):
                        hidden(4 * u + g, g)
                        if 4 * u + g:
                            add(4 * u + g - 1, u if g else 0, (g - 1) % NG)
                if slices > 2:
                    with dve.Fori(1, slices // 2) as i:
                        for u in range(2):
                            for g in range(NG):
                                hidden(8 * i + 4 * u + g, g)
                                add(8 * i + 4 * u + g - 1, 2 * i + u - (0 if g else 1), (g - 1) % NG)
                add(4 * slices - 1, slices - 1, NG - 1)

            @block.gpsimd
            def _(pool):
                with pool.Fori(0, NG) as g:
                    pool.wait_ge(var_ready, g + 1)
                    nc.gpsimd.tensor_tensor(rstd[:, :], var[:, :], core.minus_half[:, 0:GRP], ALU.pow
                                            ).then_inc(rstd_ready, 1)

            @block.scalar
            def _(act_):
                act_.sem_inc(act_done, SPARE)
                act_.sem_inc(xnT_ready, SPARE)
                with act_.Fori(0, NG) as g:
                    if placed:
                        act_.wait_ge(xn_ready, g + 1)
                        nc.scalar.copy(placed.x_hi[:, bass.ds(GRP * g, GRP), :], xn[:, :, :]).then_inc(hi_made, 1)
                    act_.wait_ge(turned, nth(g))
                    if router:
                        act_.wait_ge(logits_made, nth(g - 1))
                        for k in range(KD):
                            nc.scalar.copy(xg[:, k, :], b_T[k][:, :])
                    for k in range(KD):
                        last = nc.scalar.copy(xnT[:, k, bass.ds(512 * g, 512)], b_T[k][:, :])
                    act_.drain().then_inc(xnT_ready, 1)
                if router:
                    act_.wait_ge(logits_kept, nth(NG - 1))
                    nc.scalar.activation(logits[:, :, :], logits[:, :, :], ACT.Sigmoid
                                         ).then_inc(scored, 1)

                def activate(f, g):
                    act_.wait_ge(gu_made, nth(f))
                    if gated:
                        nc.scalar.activation(s[g % 2][:, :], b_g[g % 2][0:width, :], ACT.Silu
                                             ).then_inc(act_done, 1)
                    else:
                        nc.scalar.activation(s[g % 2][:, :], b_g[g % 2][0:width, :], ACT.Relu
                                             ).then_inc(act_done, 1)

                for f in range(8):
                    activate(f, f % NG)
                if slices > 2:
                    with act_.Fori(1, slices // 2) as i:
                        for f in range(8):
                            activate(8 * i + f, f % NG)

            @block.tensor
            def _(pe):
                pe.sem_inc(turned, SPARE)
                pe.sem_inc(logits_made, SPARE)
                pe.sem_inc(gu_made, SPARE)
                pe.sem_inc(y_made, SPARE)
                if router:
                    pe.wait_ge(router_in, router["loads"])
                with pe.Fori(0, NG) as g:
                    pe.wait_ge(xn_ready, g + 1)
                    pe.wait_ge(xnT_ready, nth(g - 1))
                    for k in range(KD):
                        for t in range(GRP):
                            last = nc.tensor.transpose(b_T[k][:, P * t:P * t + P],
                                                       xn[:, t, P * k:P * k + P], core.ident[:, :])
                    last.then_inc(turned, 1)
                    if router:
                        pe.wait_ge(xnT_ready, nth(g))
                        pe.wait_ge(logits_kept, nth(g - 1))
                        for t in range(GRP):
                            for k in range(KD):
                                last = nc.tensor.matmul(b_log[:, experts * t:experts * (t + 1)],
                                                        xg[:, k, P * t:P * t + P], wr[:, k, :],
                                                        start=(k == 0), stop=(k == KD - 1))
                        last.then_inc(logits_made, 1)
                pe.wait_ge(xnT_ready, nth(NG - 1))
                if router:
                    pe.wait_ge(logits_kept, nth(NG - 1))
                    router["count"](pe, L, picked, counted)

                def up(f, i, u, g):
                    if g == 0:
                        pe.wait_ge(wi_loaded[u], 16 * (i + 1))
                    pe.wait_ge(h_ready, nth(f - 2))
                    for a, bank in ((0, b_g), (1, b_u))[:halves]:
                        for k in range(KD):
                            last = nc.tensor.matmul(bank[g % 2][0:width, :], wi[u][:, a, k, :],
                                                    xnT[:, k, 512 * g:512 * g + 512],
                                                    start=(k == 0), stop=(k == KD - 1))
                    last.then_inc(gu_made, 1)

                def down(f, i, u, g):
                    if g == 0:
                        pe.wait_ge(wd_loaded[u], 16 * (i + 1))
                    pe.wait_ge(h_ready, nth(f))
                    pe.wait_ge(y_added, nth(f - 2))
                    for t in range(GRP):
                        last = nc.tensor.matmul(
                            b_y[2 * (g % 2) + t // 2][:, 256 * (t % 2):256 * (t % 2) + 256],
                            h[g % 2][:, P * t:P * t + P], wd[u][:, :], start=True, stop=True)
                    last.then_inc(y_made, 1)

                for u in range(2):
                    for g in range(NG):
                        up(4 * u + g, 0, u, g)
                        if 4 * u + g:
                            down(4 * u + g - 1, 0, u if g else 0, (g - 1) % NG)
                if slices > 2:
                    with pe.Fori(1, slices // 2) as i:
                        for u in range(2):
                            for g in range(NG):
                                up(8 * i + 4 * u + g, i, u, g)
                                if g:
                                    down(8 * i + 4 * u + g - 1, i, u, g - 1)
                                else:
                                    down(8 * i + 4 * u - 1, i - (1 - u), 1 - u, NG - 1)
                down(4 * slices - 1, slices // 2 - 1, 1, NG - 1)


def make_router(nc, core, w, bias, iotas, experts, groups, top_groups, top, scale, eps,
                placed=None, below=None, per=1):
    size = experts // groups if groups else 0
    capacity = placed is not None
    r = {"w": w, "experts": experts, "placed": placed}
    r["loads"] = 16 * (2 + (bias is not None) + (groups > 0) + (capacity > 0))
    wide = [P, NB, experts]

    def load(sp, L, router_in):
        r["iota"] = L.sb("iota", [P, NB, experts])
        sp.dma_start(r["iota"][:, :, :].rearrange("p b e -> p (b e)"), iotas[0]).then_inc(router_in, 16)
        if bias is not None:
            r["bias"] = L.sb("bias", [P, experts])
            sp.dma_start(r["bias"][:, :], bias.partition_broadcast(P)).then_inc(router_in, 16)
        if groups:
            r["giota"] = L.sb("giota", [P, NB, groups])
            sp.dma_start(r["giota"][:, :, :].rearrange("p b e -> p (b e)"), iotas[1]).then_inc(router_in, 16)
        if capacity:
            r["below"] = L.sb("below", [P, P])
            sp.dma_start(r["below"][:, :], below).then_inc(router_in, 16)

    def spread(combine):
        return combine[:, :, 0:experts * per].rearrange("p b (e r) -> p b e r", r=per)

    def choose(dve, L, scores, combine, scored, picked, counted, router_in):
        v = L.sb("v", wide)
        sel = L.sb("sel", wide)
        eq = L.sb("eq", wide)
        top_v = L.sb("top_v", [P, NB])
        dve.wait_ge(scored, 1)
        dve.wait_ge(router_in, r["loads"])
        if bias is not None:
            nc.vector.tensor_tensor(v[:, :, :], scores[:, :, :],
                                    r["bias"][:, :].unsqueeze(1).to_broadcast(wide), ALU.add)
        else:
            nc.vector.tensor_copy(v[:, :, :], scores[:, :, :])
        if groups:
            ab = L.sb("ab", [P, 4, NB * groups])
            gs = L.sb("gs", [P, NB, groups])
            gsel = L.sb("gsel", [P, NB, groups])
            geq = L.sb("geq", [P, NB, groups])
            m = v[:, :, :].rearrange("p b (g i) -> p (b g) i", i=size)
            dve.drain()
            for i in range(2):
                nc.vector.tensor_tensor(ab[:, 2 * i, :], m[:, :, 2 * i], m[:, :, 2 * i + 1], ALU.max)
                nc.vector.tensor_tensor(ab[:, 2 * i + 1, :], m[:, :, 2 * i], m[:, :, 2 * i + 1], ALU.min)
            dve.drain()
            g1 = gs[:, :, :].rearrange("p b g -> p (b g)")
            g2 = geq[:, :, :].rearrange("p b g -> p (b g)")
            g3 = gsel[:, :, :].rearrange("p b g -> p (b g)")
            nc.vector.tensor_tensor(g1, ab[:, 0, :], ab[:, 2, :], ALU.max)
            nc.vector.tensor_tensor(g2, ab[:, 0, :], ab[:, 2, :], ALU.min)
            nc.vector.tensor_tensor(g3, ab[:, 1, :], ab[:, 3, :], ALU.max)
            dve.drain()
            nc.vector.tensor_tensor(g2, g2, g3, ALU.max)
            dve.drain()
            nc.vector.tensor_tensor(g1, g1, g2, ALU.add)
            top_first(nc, dve, gs[:, :, :], top_groups, groups, r["giota"][:, :, :],
                      {"eq": geq[:, :, :], "top": top_v[:, :]}, gsel[:, :, :])
            nc.vector.tensor_tensor(m, m, g3.unsqueeze(2).to_broadcast([P, NB * groups, size]), ALU.mult)
        top_first(nc, dve, v[:, :, :], top, experts, r["iota"][:, :, :],
                  {"eq": eq[:, :, :], "top": top_v[:, :]}, sel[:, :, :])
        nc.vector.tensor_tensor(v[:, :, :], sel[:, :, :], scores[:, :, :], ALU.mult)
        dve.drain()
        nc.vector.tensor_reduce(top_v[:, :], v[:, :, :], AX.X, ALU.add)
        dve.drain()
        if eps:
            nc.vector.tensor_scalar(top_v[:, :], top_v[:, :], eps, None, ALU.add)
            dve.drain()
        nc.vector.reciprocal(top_v[:, :], top_v[:, :])
        dve.drain()
        nc.vector.tensor_tensor(v[:, :, :], v[:, :, :],
                                top_v[:, :].unsqueeze(2).to_broadcast(wide), ALU.mult)
        dve.drain()
        if not capacity:
            for r_ in range(per):
                nc.vector.tensor_scalar(spread(combine)[:, :, :, r_], v[:, :, :], scale, None, ALU.mult)
            return
        r["sel"] = sel
        nc.vector.tensor_scalar(placed.weights[:, :, :], v[:, :, :], scale, None, ALU.mult).then_inc(picked, 1)
        dve.wait_ge(counted, 1)
        total = [eq, L.sb("total", wide)]
        nc.vector.memset(total[0][:, 0, :], 0.0)
        nc.vector.tensor_copy(total[0][:, 1:, :], core.bank[1][:, 0:(NB - 1) * experts].rearrange(
            "p (b e) -> p b e", b=NB - 1))
        at, step = 0, 1
        while step < NB:
            dve.drain()
            a, b = total[at], total[1 - at]
            nc.vector.tensor_copy(b[:, 0:step, :], a[:, 0:step, :])
            nc.vector.tensor_tensor(b[:, step:, :], a[:, step:, :], a[:, 0:NB - step, :], ALU.add)
            at, step = 1 - at, 2 * step
        nc.vector.tensor_scalar(sel[:, :, :], sel[:, :, :], -float(NB * P), float(NB * P), ALU.mult, ALU.add)
        dve.drain()
        nc.vector.tensor_tensor(total[at][:, :, :], total[at][:, :, :],
                                core.bank[0][:, 0:NB * experts].rearrange("p (b e) -> p b e", b=NB), ALU.add)
        dve.drain()
        nc.vector.tensor_tensor(placed.places[:, :, :], total[at][:, :, :], sel[:, :, :],
                                ALU.add).then_inc(picked, 1)

    def count(pe, L, picked, counted):
        if not capacity:
            return
        pe.wait_ge(picked, 1)
        flat = r["sel"][:, :, :].rearrange("p b e -> p (b e)")
        nc.tensor.matmul(core.bank[0][:, 0:NB * experts], r["below"][:, :], flat, start=True, stop=True)
        nc.tensor.matmul(core.bank[1][:, 0:NB * experts], core.ones[:, :], flat, start=True, stop=True
                         ).then_inc(counted, 1)
        pe.wait_ge(picked, 2)

    r["load"], r["choose"], r["count"] = load, choose, count
    return r


F16 = mybir.dt.float16


class Placed:

    def __init__(self, L, experts):
        self.places = L.sb("places", [P, NB, experts])
        self.weights = L.sb("weights", [P, NB, experts])
        self.x_hi = L.sb("x_hi", [P, NB, D], F16)
        self.x_lo = L.sb("x_lo", [P, NB, D], F16)


def placed_experts_layer(nc, core, name, w_in, w_down, placed, experts, capacity, tables):
    G = 4
    K_UP, K_DOWN = 1, 2
    with Layer(nc, name) as L:
        sb, sem = L.sb, L.sem
        two = lambda n, shape, t=F32: [sb(f"{n}{u}", shape, t) for u in range(2)]
        w_at = lambda u: core.far[:, 1024 * u:1024 * u + 512].rearrange("p (a k w) -> p a k w", a=2, k=KD)
        wi = [w_at(u) for u in range(2)]
        wd = [core.far[:, 1024 * u + 512:1024 * u + 512 + D] for u in range(2)]
        place_iota = sb("place_iota", [P, capacity])
        token_iota = sb("token_iota", [P, NB * P], F16)
        w16 = sb("w16", [P, NB, experts, 2], F16)
        sel = two("sel", [P, NB, capacity], F16)
        facts = two("facts", [P, NB, 3], F16)
        xT = two("xT", [P, KD * capacity])
        found = two("found", [capacity, 3])
        weight = sb("weight", [capacity, 1])
        s, h = sb("s", [P, capacity]), two("h", [P, capacity])
        y = sb("y", [capacity, D])
        y_hi, y_lo = (sb(n, [capacity, G, D], F16) for n in ("y_hi", "y_lo"))
        back = sb("back", [capacity, G, NB * P], F16)
        b_x, b_h, b_y, b_out = core.bank[0:2], core.bank[2:4], core.bank[4:6], core.bank[6:8]
        tables_in, begun = sem("tables_in"), sem("begun")
        wi_loaded = [sem(f"wi_loaded{u}") for u in range(2)]
        wd_loaded = [sem(f"wd_loaded{u}") for u in range(2)]
        (sel_ready, fetched, xT_kept, gu_made, s_ready, h_ready, y_made, weight_ready, y_ready, hi_ready,
         back_ready, out_made, out_added) = (sem(n) for n in (
             "sel_ready", "fetched", "xT_kept", "gu_made", "s_ready", "h_ready", "y_made", "weight_ready",
             "y_ready", "hi_ready", "back_ready", "out_made", "out_added"))

        def done(eng, signal, k):
            if not (isinstance(k, int) and k < 0):
                eng.wait_ge(signal, k + 1)

        def item(e, k):
            return None if isinstance(e, int) and not 0 <= e - k < experts else e - k

        def run(eng, slot):
            for e in range(2 * G):
                slot(e, e % G, e // G)
            with eng.Fori(2, experts // G - 1) as i:
                for j in range(G):
                    slot(G * i + j, j, i)
            for e in range(experts - G, experts + K_DOWN + 1):
                slot(e, e % G, e // G)

        def returns(e, j):
            return j == K_DOWN and not (isinstance(e, int) and e < G)

        with nc.Block() as block:
            @block.sync
            def _(sp):
                sp.dma_start(place_iota[:, :], tables[0]).then_inc(tables_in, 16)
                sp.dma_start(token_iota[:, :], tables[1]).then_inc(tables_in, 16)
                for u in range(2):
                    sp.dma_start(facts[u][:, :, :].rearrange("p b i -> p (b i)"), tables[2]).then_inc(tables_in, 16)

                def load(e, u):
                    sp.dma_start(wi[u].rearrange("p a k w -> p (a k w)"),
                                 w_in[bass.ds(e, 1), :, :].rearrange("a p w -> (a p) w")
                                 ).then_inc(wi_loaded[u], 16)
                    sp.dma_start(wd[u], w_down[bass.ds(e, 1), :, :].rearrange("a p w -> (a p) w")
                                 ).then_inc(wd_loaded[u], 16)
                load(0, 0)
                load(1, 1)
                with sp.Fori(1, experts // 2) as i:
                    for u in range(2):
                        done(sp, y_made, 2 * i + u - 2)
                        load(2 * i + u, u)

            @block.tensor
            def _(pe):
                def fetch(e, u):
                    done(pe, sel_ready, e)
                    done(pe, xT_kept, e - 2)
                    for k in range(KD):
                        for b in range(NB):
                            for i, part in enumerate((placed.x_hi, placed.x_lo)):
                                nc.tensor.matmul(b_x[u][:, capacity * k:capacity * (k + 1)],
                                                 part[:, b, P * k:P * k + P], sel[u][:, b, :],
                                                 start=(b + i == 0), stop=(b == NB - 1 and i == 1))
                    at = KD * capacity
                    for b in range(NB):
                        last = nc.tensor.matmul(b_x[u][0:capacity, at:at + 3], sel[u][:, b, :],
                                                facts[u][:, b, :], start=(b == 0), stop=(b == NB - 1))
                    last.then_inc(fetched, 1)

                def up(e, u, i):
                    pe.wait_ge(wi_loaded[u], 16 * (i + 1))
                    done(pe, xT_kept, e)
                    done(pe, h_ready, e - 2)
                    for a in range(2):
                        for k in range(KD):
                            last = nc.tensor.matmul(b_h[u][:, capacity * a:capacity * (a + 1)], wi[u][:, a, k, :],
                                                    xT[u][:, capacity * k:capacity * (k + 1)],
                                                    start=(k == 0), stop=(k == KD - 1))
                    last.then_inc(gu_made, 1)

                def down(e, u, i):
                    pe.wait_ge(wd_loaded[u], 16 * (i + 1))
                    done(pe, h_ready, e)
                    done(pe, y_ready, e - 2)
                    nc.tensor.matmul(b_y[u][0:capacity, 0:D], h[u][:, :], wd[u], start=True, stop=True
                                     ).then_inc(y_made, 1)

                def give_back(e):
                    done(pe, back_ready, e - K_DOWN - 1)
                    n = NB // 2
                    g = (e - K_DOWN) // G - 1 if isinstance(e, int) else None
                    for t in range(n):
                        if g is not None:
                            done(pe, out_added, n * g + t - 2)
                        else:
                            done(pe, out_added, (e - K_DOWN - G) * (n // G) + t - 2)
                        for m in range(2):
                            for q in range(G):
                                for i, part in enumerate((y_hi, y_lo)):
                                    at = P * (2 * t + m)
                                    last = nc.tensor.matmul(b_out[t % 2][:, D * m:D * m + D],
                                                            back[:, q, at:at + P], part[:, q, :],
                                                            start=(q + i == 0), stop=(q == G - 1 and i == 1))
                        last.then_inc(out_made, 1)

                pe.wait_ge(begun, 1)

                def slot(e, j, i):
                    if returns(e, j):
                        give_back(e)
                    new, mid, end = (item(e, k) for k in (0, K_UP, K_DOWN))
                    if end is not None:
                        down(end, j % 2, turn(end, i, j - K_DOWN))
                    if mid is not None:
                        up(mid, (j - 1) % 2, turn(mid, i, j - K_UP))
                    if new is not None:
                        fetch(new, j % 2)

                def turn(e, i, j):
                    return (G * i + j) // 2 if isinstance(e, int) else (G // 2) * i + j // 2

                run(pe, slot)

            @block.vector
            def _(dve):
                nc.vector.tensor_copy(w16[:, :, :, 0], placed.weights[:, :, :])
                dve.drain()
                nc.vector.tensor_tensor(w16[:, :, :, 1], placed.weights[:, :, :], w16[:, :, :, 0], ALU.subtract)
                dve.drain().then_inc(begun, 1)
                dve.wait_ge(tables_in, 64)

                def choose(e, u):
                    if not (isinstance(e, int) and e < 2):
                        dve.wait_ge(fetched, e - 1)
                    here = placed.places[:, :, bass.ds(e, 1)].to_broadcast([P, NB, capacity])
                    nc.vector.tensor_tensor(sel[u][:, :, :], here,
                                            place_iota[:, :].unsqueeze(1).to_broadcast([P, NB, capacity]),
                                            ALU.is_equal)
                    nc.vector.tensor_copy(facts[u][:, :, 1:3],
                                          w16[:, :, bass.ds(e, 1), :].rearrange("p b a i -> p b (a i)"))
                    dve.drain().then_inc(sel_ready, 1)

                def hidden(e, u):
                    done(dve, s_ready, e)
                    done(dve, y_made, e - 2)
                    nc.vector.tensor_tensor(h[u][:, :], s[:, :], b_h[u][:, capacity:2 * capacity], ALU.mult
                                            ).then_inc(h_ready, 1)

                def way_back(e, u, j):
                    done(dve, y_ready, e - 1)
                    nc.vector.tensor_tensor(weight[:, :], found[u][:, 1:2], found[u][:, 2:3], ALU.add
                                            ).then_inc(weight_ready, 1)
                    nc.vector.tensor_scalar(back[:, j, :], token_iota[0:capacity, :], found[u][:, 0:1], None,
                                            ALU.is_equal)
                    done(dve, hi_ready, e)
                    nc.vector.tensor_tensor(y_lo[:, j, :], y[:, :], y_hi[:, j, :], ALU.subtract)
                    dve.drain().then_inc(back_ready, 1)

                def add(e):
                    n = NB // 2
                    g = (e - K_DOWN) // G - 1 if isinstance(e, int) else None
                    for t in range(n):
                        done(dve, out_made, n * g + t if g is not None else (e - K_DOWN - G) * (n // G) + t)
                        xb = core.x[:, 2 * t:2 * t + 2, :].rearrange("p b d -> p (b d)")
                        nc.vector.tensor_tensor(xb, b_out[t % 2][:, :], xb, ALU.add).then_inc(out_added, 1)

                choose(0, 0)

                def slot(e, j, i):
                    if returns(e, j):
                        add(e)
                    new, mid, end = (item(e, k) for k in (-1, K_UP, K_DOWN))
                    if mid is not None:
                        hidden(mid, (j - 1) % 2)
                    if end is not None:
                        way_back(end, j % 2, (j - K_DOWN) % G)
                    if new is not None:
                        choose(new, (j + 1) % 2)

                run(dve, slot)

            @block.scalar
            def _(act):
                def keep(e, u):
                    done(act, fetched, e)
                    done(act, gu_made, e - 2)
                    done(act, back_ready, e - 2)
                    nc.scalar.copy(xT[u][:, :], b_x[u][:, 0:KD * capacity])
                    nc.scalar.copy(found[u][:, :], b_x[u][0:capacity, KD * capacity:KD * capacity + 3])
                    act.drain().then_inc(xT_kept, 1)

                def silu(e, u):
                    done(act, gu_made, e)
                    done(act, h_ready, e - 1)
                    nc.scalar.activation(s[:, :], b_h[u][:, 0:capacity], ACT.Silu).then_inc(s_ready, 1)

                def weigh(e, u, j):
                    done(act, y_made, e)
                    done(act, weight_ready, e)
                    done(act, back_ready, e - 1)
                    nc.scalar.activation(y[:, :], b_y[u][0:capacity, 0:D], ACT.Copy, scale=weight[:, 0:1]
                                         ).then_inc(y_ready, 1)
                    act.drain()
                    nc.scalar.copy(y_hi[:, j, :], y[:, :]).then_inc(hi_ready, 1)

                def slot(e, j, i):
                    if returns(e, j):
                        n = NB // 2
                        g = (e - K_DOWN) // G - 1 if isinstance(e, int) else None
                        done(act, out_made, n * g + n - 1 if g is not None
                             else (e - K_DOWN - G) * (n // G) + n - 1)
                    new, mid, end = (item(e, k) for k in (0, K_UP, K_DOWN))
                    if mid is not None:
                        silu(mid, (j - 1) % 2)
                    if end is not None:
                        weigh(end, j % 2, (j - K_DOWN) % G)
                    if new is not None:
                        keep(new, j % 2)

                run(act, slot)


def behind(b, u, c, k, chunks):
    db, cc = divmod(c - k, chunks)
    if isinstance(b, int) and not 0 <= b + db < NB:
        return None
    return b + db, (u + db) % 2, cc, chunks * (b + db) + cc


def run_slots(eng, slot, chunks, peeled, extra):
    for b in range(2 * peeled):
        for c in range(chunks):
            slot(b, b % 2, c)
    with eng.Fori(peeled, NB // 2) as i:
        for u in range(2):
            for c in range(chunks):
                slot(2 * i + u, u, c)
    for f in range(NB * chunks, NB * chunks + extra):
        slot(f // chunks, (f // chunks) % 2, f % chunks)


class Norm:

    def __init__(self, nc, core, L, bank):
        self.nc, self.core, self.bank = nc, core, bank
        self.stats = L.sb("ln_stats", [P, 6])
        self.mv = [L.sb(f"ln_mv{u}", [P, 2]) for u in range(2)]
        self.var = L.sb("ln_var", [P, 1])
        self.rstd = L.sb("ln_rstd", [P, 1])
        self.xn = L.sb("ln_xn", [P, D])
        self.xnT = [L.sb(f"ln_xnT{u}", [P, KD, P]) for u in range(2)]
        self.var_ready, self.rstd_ready = L.sem("ln_var_ready"), L.sem("ln_rstd_ready")
        self.xn_ready, self.turned, self.kept = L.sem("xn_ready"), L.sem("xn_turned"), L.sem("xnT_kept")

    def prime_pe(self, pe):
        pe.sem_inc(self.turned, SPARE)

    def prime_act(self, act):
        act.sem_inc(self.kept, SPARE)

    def moments(self, dve, b):
        nc = self.nc
        nc.vector.bn_stats(self.stats[:, :], pick(self.core.x[:, :, :], b))
        dve.drain()
        mv = self.mv[0]
        nc.vector.bn_aggr(mv[:, :], self.stats[:, :])
        dve.drain()
        nc.vector.tensor_scalar(self.var[:, :], mv[:, 1:2], LN_EPS, None, ALU.add
                                ).then_inc(self.var_ready, 1)

    def rsqrt(self, pool, b):
        pool.wait_ge(self.var_ready, b + 1)
        self.nc.gpsimd.tensor_tensor(self.rstd[:, :], self.var[:, :], self.core.minus_half[:, 0:1],
                                     ALU.pow).then_inc(self.rstd_ready, 1)

    def normalise(self, dve, b):
        dve.wait_ge(self.rstd_ready, b + 1)
        dve.wait_ge(self.turned, nth(b - 1))
        self.nc.vector.tensor_scalar(self.xn[:, :], pick(self.core.x[:, :, :], b), self.mv[0][:, 0:1],
                                     self.rstd[:, 0:1], ALU.subtract, ALU.mult).then_inc(self.xn_ready, 1)

    def turn(self, pe, b):
        pe.wait_ge(self.xn_ready, b + 1)
        pe.wait_ge(self.kept, nth(b - 1))
        for k in range(KD):
            last = self.nc.tensor.transpose(self.bank[:, P * k:P * k + P], self.xn[:, P * k:P * k + P],
                                            self.core.ident[:, :])
        last.then_inc(self.turned, 1)

    def keep(self, act, b, u, users):
        act.wait_ge(self.turned, nth(b))
        for sem, value in users:
            act.wait_ge(sem, value)
        self.nc.scalar.copy(self.xnT[u][:, :, :].rearrange("p k t -> p (k t)"), self.bank[:, 0:D]
                            ).then_inc(self.kept, 1)


def wide_attention_layer(nc, core, name, wq, wk, wv, wo, loaded, kv_heads, prep, scale, ctxT=None,
                         tables=None, mask=None, prefetch=()):
    HC = 4
    NC = 4
    KC = kv_heads // NC
    K_PROJ, K_S, K_P, K_O = NC, NC + 1, NC + 3, NC + 4
    with Layer(nc, name) as L:
        sb, sem = L.sb, L.sem
        b_q, b_k, b_v, b_s, b_p, b_o, b_y, b_t = core.bank
        norm = Norm(nc, core, L, b_t)
        two = lambda n, w=512: [sb(f"{n}{i}", [P, w]) for i in range(2)]
        v = [sb(f"v{c}", [P, KC * P]) for c in range(NC)]
        qT, kT, dif, prob, oT = two("qT"), two("kT", KC * P), two("dif"), two("prob"), two("oT")
        pT = sb("pT", [P, 512])
        smax, ssum = sb("smax", [P, HC]), sb("ssum", [P, HC])
        srec = two("srec", HC)
        if prep != "direct":
            q_tok, k_tok = sb("q_tok", [P, 512]), sb("k_tok", [P, 512])
        if prep == "rope":
            qa, qb, ka, kb = (sb(n, [P, 512]) for n in ("qa", "qb", "ka", "kb"))
            cos, sin = sb("cos", [P, P]), sb("sin", [P, P])
        if prep == "rms":
            q_sq, k_sq = sb("q_sq", [P, 512]), sb("k_sq", [P, 512])
            ss, rr = sb("ss", [P, 2 * HC]), sb("rr", [P, 2 * HC])
            gains, gain = sb("gains", [P, 2]), sb("gain", [P, 1])
        if mask is not None:
            mrow_u8, mcol_u8 = sb("mrow_u8", [1, NB * P], mybir.dt.uint8), sb("mcol_u8", [P, NB], mybir.dt.uint8)
            mrow, mcol = sb("mrow", [1, NB * P], BF16), sb("mcol", [P, NB])
            one_row = sb("one_row", [1, P], BF16)
            mask_set = sem("mask_set")
            mrow_b = [sb(f"mrow_b{u}", [1, HC, P], BF16) for u in range(2)]
            mcol_b = [sb(f"mcol_b{u}", [P, 1]) for u in range(2)]
        if ctxT is not None:
            cT = two("cT", P)
            ctx_in = [sem(f"ctx_in{u}") for u in range(2)]
        tables_in, tables_done = sem("tables_in"), sem("tables_done")
        n_tables = 0
        (q_made, k_made, v_made, q_parts, k_parts, sq_ready, ss_ready, rr_ready, k_ready, q_turned, turned,
         qT_kept, kT_kept, v_kept, s_made, d_ready, e_ready, sum_ready, p_ready, p_turned, pT_kept,
         o_made, oT_kept, y_made, y_added) = (sem(n) for n in (
             "q_made", "k_made", "v_made", "q_parts", "k_parts", "sq_ready", "ss_ready", "rr_ready",
             "k_ready", "q_turned", "turned", "qT_kept", "kT_kept", "v_kept", "s_made", "d_ready", "e_ready",
             "sum_ready", "p_ready", "p_turned", "pT_kept", "o_made", "oT_kept", "y_made", "y_added"))
        heads = lambda ap, n=HC: ap.rearrange("p (h w) -> p h w", h=n)
        wide = [P, HC, P]

        with nc.Block() as block:
            @block.sync
            def _(sp):
                if prep == "rope":
                    sp.dma_start(cos[:, :], tables[0]).then_inc(tables_in, 16)
                    sp.dma_start(sin[:, :], tables[1]).then_inc(tables_in, 16)
                elif prep == "rms":
                    sp.dma_start(gains[:, 0:1], tables[0].rearrange("(p o) -> p o", o=1)).then_inc(tables_in, 16)
                    sp.dma_start(gains[:, 1:2], tables[1].rearrange("(p o) -> p o", o=1)).then_inc(tables_in, 16)
                else:
                    sp.dma_start(mrow_u8[:, :], mask[0]).then_inc(tables_in, 16)
                    sp.dma_start(mcol_u8[:, :], mask[1]).then_inc(tables_in, 16)
                if ctxT is not None:
                    def load(b, u):
                        sp.dma_start(cT[u][:, :], ctxT[bass.ds(b, 1), :, :].rearrange("a p t -> (a p) t")
                                     ).then_inc(ctx_in[u], 16)
                    load(0, 0)
                    load(1, 1)
                for fetch in prefetch:
                    fetch(sp)
                if ctxT is not None:
                    with sp.Fori(1, NB // 2) as i:
                        for u in range(2):
                            sp.wait_ge(v_made, nth(NC * (2 * i + u - 2) + NC - 1))
                            load(2 * i + u, u)

            @block.tensor
            def _(pe):
                norm.prime_pe(pe)
                for s in (v_made, k_made, turned, s_made, p_turned, o_made):
                    pe.sem_inc(s, SPARE)
                pe.wait_ge(loaded[0], loaded[1])
                pe.wait_ge(tables_done, 1)

                def turn_probs(it):
                    b, u, c, f = it
                    pe.wait_ge(p_ready, f + 1)
                    pe.wait_ge(pT_kept, nth(f - 1))
                    for j in range(HC):
                        last = nc.tensor.transpose(b_p[:, P * j:P * j + P], prob[c % 2][:, P * j:P * j + P],
                                                   core.ident[:, :])
                    last.then_inc(p_turned, 1)

                def project_out(it):
                    b, u, c, f = it
                    pe.wait_ge(oT_kept, nth(f))
                    if c == 0:
                        pe.wait_ge(y_added, nth(b - 1))
                    for j in range(HC):
                        last = nc.tensor.matmul(b_y[:, 0:D], oT[c % 2][:, P * j:P * j + P],
                                                wo[:, HC * c + j, :], start=(c == 0 and j == 0),
                                                stop=(c == NC - 1 and j == HC - 1))
                    if c == NC - 1:
                        last.then_inc(y_made, 1)

                def turn_q(it, after_norm):
                    b, u, c, f = it
                    pe.wait_ge(k_ready, f + 1)
                    pe.wait_ge(kT_kept, nth(f - 1))
                    if after_norm is not None:
                        pe.wait_ge(norm.kept, nth(after_norm))
                    for j in range(HC):
                        last = nc.tensor.transpose(b_t[:, P * j:P * j + P], q_tok[:, P * j:P * j + P],
                                                   core.ident[:, :])
                    last.then_inc(q_turned, 1)

                def turn_k(it):
                    b, u, c, f = it
                    pe.wait_ge(qT_kept, nth(f))
                    for j in range(HC):
                        last = nc.tensor.transpose(b_t[:, P * j:P * j + P], k_tok[:, P * j:P * j + P],
                                                   core.ident[:, :])
                    last.then_inc(turned, 1)

                def heads_out(it):
                    b, u, c, f = it
                    pe.wait_ge(pT_kept, nth(f))
                    pe.wait_ge(v_kept, nth(f))
                    pe.wait_ge(oT_kept, nth(f - 1))
                    for j in range(HC):
                        at = P * (j * KC // HC)
                        last = nc.tensor.matmul(b_o[:, P * j:P * j + P], v[c][:, at:at + P],
                                                pT[:, P * j:P * j + P], start=True, stop=True)
                    last.then_inc(o_made, 1)

                def scores(it):
                    b, u, c, f = it
                    pe.wait_ge(kT_kept, nth(f))
                    pe.wait_ge(qT_kept, nth(f))
                    pe.wait_ge(d_ready, nth(f - 1))
                    if mask is not None:
                        if c == 0:
                            pe.wait_ge(mask_set, b + 1)
                        nc.tensor.matmul(b_s[:, :], one_row[:, :], mrow_b[u][:, :, :].rearrange(
                            "p h k -> p (h k)"), start=True, stop=False)
                    for j in range(HC):
                        at = P * (j * KC // HC)
                        last = nc.tensor.matmul(b_s[:, P * j:P * j + P], qT[c % 2][:, P * j:P * j + P],
                                                kT[c % 2][:, at:at + P], start=mask is None,
                                                stop=mask is None or j == HC - 1)
                    last.then_inc(s_made, 1)

                def project_q(it):
                    b, u, c, f = it
                    if c == 0:
                        pe.wait_ge(norm.kept, nth(b))
                        if ctxT is not None:
                            pe.wait_ge(ctx_in[u], ctx_turn(b))
                    if prep == "direct":
                        pe.wait_ge(qT_kept, nth(f - 1))
                    else:
                        held(pe, k_ready, f)
                    if prep == "direct":
                        for j in range(HC):
                            for k in range(KD):
                                last = nc.tensor.matmul(b_q[:, P * j:P * j + P],
                                                        wq[:, k, 512 * c + P * j:512 * c + P * j + P],
                                                        norm.xnT[u][:, k, :], start=(k == 0), stop=(k == KD - 1))
                    else:
                        for k in range(KD):
                            last = nc.tensor.matmul(b_q[:, :], norm.xnT[u][:, k, :],
                                                    wq[:, k, 512 * c:512 * c + 512],
                                                    start=(k == 0), stop=(k == KD - 1))
                    last.then_inc(q_made, 1)

                def ctx_turn(b):
                    return 16 * (b // 2 + 1)

                def project_k(it):
                    b, u, c, f = it
                    w = KC * P
                    if prep == "direct":
                        pe.wait_ge(kT_kept, nth(f - 1))
                    else:
                        held(pe, k_ready, f)
                    if prep == "direct":
                        for j in range(KC):
                            last = nc.tensor.matmul(b_k[:, P * j:P * j + P],
                                                    wk[:, 0, w * c + P * j:w * c + P * j + P], cT[u][:, :],
                                                    start=True, stop=True)
                    elif ctxT is not None:
                        last = nc.tensor.matmul(b_k[:, 0:w], cT[u][:, :], wk[:, 0, w * c:w * c + w],
                                                start=True, stop=True)
                    else:
                        for k in range(KD):
                            last = nc.tensor.matmul(b_k[:, 0:w], norm.xnT[u][:, k, :],
                                                    wk[:, k, w * c:w * c + w], start=(k == 0), stop=(k == KD - 1))
                    last.then_inc(k_made, 1)

                def project_v(it):
                    b, u, c, f = it
                    w = KC * P
                    pe.wait_ge(v_kept, nth(f - 1))
                    if ctxT is not None:
                        last = nc.tensor.matmul(b_v[:, 0:w], cT[u][:, :], wv[:, 0, w * c:w * c + w],
                                                start=True, stop=True)
                    else:
                        for k in range(KD):
                            last = nc.tensor.matmul(b_v[:, 0:w], norm.xnT[u][:, k, :],
                                                    wv[:, k, w * c:w * c + w], start=(k == 0), stop=(k == KD - 1))
                    last.then_inc(v_made, 1)

                def slot(b, u, c):
                    proj, sc, pr, ou = (behind(b, u, c, k, NC) for k in (K_PROJ, K_S, K_P, K_O))
                    if pr:
                        turn_probs(pr)
                    if ou:
                        project_out(ou)
                    if sc and prep != "direct":
                        turn_q(sc, b if c == 3 and behind(b, u, c, 0, NC) else None)
                    if pr:
                        heads_out(pr)
                    if sc and prep != "direct":
                        turn_k(sc)
                    if proj:
                        project_q(proj)
                        project_k(proj)
                    if c == 2 and behind(b, u, c, 0, NC):
                        if sc and prep != "direct":
                            pe.wait_ge(kT_kept, nth(sc[3]))
                        norm.turn(pe, b)
                    if sc:
                        scores(sc)
                    if proj:
                        project_v(proj)

                run_slots(pe, slot, NC, 1, K_O)

            @block.vector
            def _(dve):
                for s in (d_ready, oT_kept, y_added, ss_ready):
                    dve.sem_inc(s, SPARE)
                dve.wait_ge(tables_in, 32)
                if prep == "rms":
                    nc.vector.tensor_tensor(gain[:, :], gains[:, 0:1], gains[:, 1:2], ALU.mult)
                if mask is not None:
                    nc.vector.memset(one_row[:, :], 1.0)
                    nc.vector.tensor_scalar(mrow[:, :], mrow_u8[:, :], -1.0, -NEG, ALU.add, ALU.mult)
                    nc.vector.tensor_copy(mcol[:, :], mcol_u8[:, :])
                dve.drain().then_inc(tables_done, 1)

                def residual(it):
                    b, u, c, f = it
                    dve.wait_ge(y_made, b + 1)
                    xb = pick(core.x[:, :, :], b).rearrange("p a d -> p (a d)")
                    nc.vector.tensor_tensor(xb, b_y[:, 0:D], xb, ALU.add).then_inc(y_added, 1)

                def keep_o(it):
                    b, u, c, f = it
                    dve.wait_ge(o_made, nth(f))
                    nc.vector.tensor_copy(oT[c % 2][:, :], b_o[:, :]).then_inc(oT_kept, 1)

                def less_max(it):
                    b, u, c, f = it
                    dve.wait_ge(s_made, nth(f))
                    nc.vector.tensor_reduce(smax[:, :], heads(b_s[:, :]), AX.X, ALU.max)
                    dve.drain()
                    nc.vector.tensor_tensor(heads(dif[c % 2][:, :]), heads(b_s[:, :]),
                                            smax[:, :].unsqueeze(2).to_broadcast(wide), ALU.subtract
                                            ).then_inc(d_ready, 1)

                def sums(it):
                    b, u, c, f = it
                    dve.wait_ge(e_ready, f + 1)
                    nc.vector.tensor_reduce(ssum[:, :], heads(prob[c % 2][:, :]), AX.X, ALU.add)
                    dve.drain()
                    nc.vector.reciprocal(srec[c % 2][:, :], ssum[:, :]).then_inc(sum_ready, 1)

                def rotate(made, bank, a, b_, parts, it):
                    b, u, c, f = it
                    dve.wait_ge(made, f + 1 if made is q_made else nth(f))
                    if not (isinstance(f, int) and f == 0):
                        dve.wait_ge(k_ready, f)
                    x, y = heads(bank[:, :]), heads(b_[:, :])
                    half = [P, HC, P // 2]
                    nc.vector.tensor_tensor(heads(a[:, :]), x, cos[:, :].unsqueeze(1).to_broadcast(wide), ALU.mult)
                    nc.vector.tensor_tensor(y[:, :, 0:64], x[:, :, 64:128],
                                            sin[:, 0:64].unsqueeze(1).to_broadcast(half), ALU.mult)
                    nc.vector.tensor_tensor(y[:, :, 64:128], x[:, :, 0:64],
                                            sin[:, 64:128].unsqueeze(1).to_broadcast(half), ALU.mult)
                    dve.drain().then_inc(parts, 1)

                def squares(it):
                    b, u, c, f = it
                    for i, sq in enumerate((q_sq, k_sq)):
                        dve.wait_ge(sq_ready, 2 * f + i + 1)
                        nc.vector.tensor_reduce(ss[:, HC * i:HC * i + HC], heads(sq[:, :]), AX.X, ALU.add)
                    dve.drain()
                    nc.vector.tensor_scalar(ss[:, :], ss[:, :], 1.0 / P, LN_EPS, ALU.mult, ALU.add
                                            ).then_inc(ss_ready, 1)

                def scale_qk(it):
                    b, u, c, f = it
                    dve.wait_ge(rr_ready, f + 1)
                    dve.wait_ge(turned, nth(f - 1))
                    for i, (bank, tok) in enumerate(((b_q, q_tok), (b_k, k_tok))):
                        nc.vector.tensor_tensor(heads(tok[:, :]), heads(bank[:, :]),
                                                rr[:, HC * i:HC * i + HC].unsqueeze(2).to_broadcast(wide),
                                                ALU.mult)
                    dve.drain().then_inc(k_ready, 1)

                def slot(b, u, c):
                    proj, sc, pr, ou = (behind(b, u, c, k, NC) for k in (K_PROJ, K_S, K_P, K_O))
                    ln = behind(b, u, c, 0, NC)
                    if ln and c == 0:
                        norm.moments(dve, b)
                    if ln and c == 1:
                        norm.normalise(dve, b)
                    if ln and c == 2 and mask is not None:
                        nc.vector.tensor_copy(mrow_b[u][:, :, :], mrow[:, bass.ds(P * b, P)].unsqueeze(1)
                                              .to_broadcast([1, HC, P]))
                        nc.vector.tensor_copy(mcol_b[u][:, :], mcol[:, bass.ds(b, 1)])
                        dve.drain().then_inc(mask_set, 1)
                    if ou and ou[2] == NC - 1:
                        residual(ou)
                    if pr:
                        keep_o(pr)
                    if proj and prep == "rope":
                        rotate(q_made, b_q, qa, qb, q_parts, proj)
                        rotate(k_made, b_k, ka, kb, k_parts, proj)
                    if proj and prep == "rms":
                        squares(proj)
                    if sc:
                        less_max(sc)
                    if proj and prep == "rms":
                        scale_qk(proj)
                    if sc:
                        sums(sc)

                run_slots(dve, slot, NC, 1, K_O)

            @block.scalar
            def _(act):
                norm.prime_act(act)
                for s in (pT_kept, qT_kept, kT_kept, v_kept):
                    act.sem_inc(s, SPARE)
                act.wait_ge(tables_done, 1)

                def keep_probs(it):
                    b, u, c, f = it
                    act.wait_ge(p_turned, nth(f))
                    act.wait_ge(o_made, nth(f - 1))
                    nc.scalar.copy(pT[:, :], b_p[:, :]).then_inc(pT_kept, 1)

                def keep_q(it, made, value):
                    b, u, c, f = it
                    act.wait_ge(made, value)
                    act.wait_ge(s_made, nth(f - 2))
                    bank = b_q if prep == "direct" else b_t
                    if prep == "rms":
                        nc.scalar.activation(qT[c % 2][:, :], bank[:, :], ACT.Copy, scale=gain[:, 0:1]
                                             ).then_inc(qT_kept, 1)
                    else:
                        nc.scalar.copy(qT[c % 2][:, :], bank[:, :]).then_inc(qT_kept, 1)

                def keep_k(it, made):
                    b, u, c, f = it
                    act.wait_ge(made, nth(f))
                    act.wait_ge(s_made, nth(f - 2))
                    bank = b_k if prep == "direct" else b_t
                    nc.scalar.copy(kT[c % 2][:, :], bank[:, 0:KC * P]).then_inc(kT_kept, 1)

                def keep_v(it):
                    b, u, c, f = it
                    act.wait_ge(v_made, nth(f))
                    held(act, o_made, nth(f - NC))
                    if mask is not None:
                        if c == 0:
                            act.wait_ge(mask_set, b + 1)
                        nc.scalar.activation(v[c][:, :], b_v[:, 0:KC * P], ACT.Copy,
                                             scale=mcol_b[u][:, 0:1]).then_inc(v_kept, 1)
                    else:
                        nc.scalar.copy(v[c][:, :], b_v[:, 0:KC * P]).then_inc(v_kept, 1)

                def exponentials(it):
                    b, u, c, f = it
                    act.wait_ge(d_ready, nth(f))
                    act.wait_ge(p_turned, nth(f - 2))
                    nc.scalar.activation(prob[c % 2][:, :], dif[c % 2][:, :], ACT.Exp, scale=scale
                                         ).then_inc(e_ready, 1)

                def square(it):
                    b, u, c, f = it
                    act.wait_ge(q_made, f + 1)
                    act.wait_ge(ss_ready, nth(f - 1))
                    nc.scalar.activation(q_sq[:, :], b_q[:, :], ACT.Square).then_inc(sq_ready, 1)
                    act.wait_ge(k_made, nth(f))
                    nc.scalar.activation(k_sq[:, :], b_k[:, :], ACT.Square).then_inc(sq_ready, 1)

                def slot(b, u, c):
                    proj, sc, pr, ou = (behind(b, u, c, k, NC) for k in (K_PROJ, K_S, K_P, K_O))
                    if pr:
                        keep_probs(pr)
                    if sc and prep != "direct":
                        keep_q(sc, q_turned, sc[3] + 1)
                        keep_k(sc, turned)
                    if proj and prep == "rms":
                        square(proj)
                    if proj and prep == "direct":
                        keep_q(proj, q_made, proj[3] + 1)
                        keep_k(proj, k_made)
                    if c == 2 and behind(b, u, c, 0, NC):
                        norm.keep(act, b, u, ((v_made, nth(NC * (b - 2) + NC - 1)),)
                                  if not (isinstance(b, int) and b < 2) else ())
                    if sc:
                        exponentials(sc)
                    if proj:
                        keep_v(proj)

                run_slots(act, slot, NC, 1, K_O)

            @block.gpsimd
            def _(pool):
                def add_parts(it):
                    b, u, c, f = it
                    pool.wait_ge(turned, nth(f - 1))
                    pool.wait_ge(q_parts, f + 1)
                    nc.gpsimd.tensor_tensor(q_tok[:, :], qa[:, :], qb[:, :], ALU.add)
                    pool.wait_ge(k_parts, f + 1)
                    nc.gpsimd.tensor_tensor(k_tok[:, :], ka[:, :], kb[:, :], ALU.add)
                    pool.drain().then_inc(k_ready, 1)

                def rsqrt(it):
                    b, u, c, f = it
                    pool.wait_ge(ss_ready, nth(f))
                    nc.gpsimd.tensor_tensor(rr[:, :], ss[:, :], core.minus_half[:, 0:2 * HC], ALU.pow
                                            ).then_inc(rr_ready, 1)

                def divide(it):
                    b, u, c, f = it
                    pool.wait_ge(sum_ready, f + 1)
                    nc.gpsimd.tensor_tensor(heads(prob[c % 2][:, :]), heads(prob[c % 2][:, :]),
                                            srec[c % 2][:, :].unsqueeze(2).to_broadcast(wide), ALU.mult
                                            ).then_inc(p_ready, 1)

                def slot(b, u, c):
                    proj, sc, pr, ou = (behind(b, u, c, k, NC) for k in (K_PROJ, K_S, K_P, K_O))
                    if c == 0 and behind(b, u, c, 0, NC):
                        norm.rsqrt(pool, b)
                    if proj and prep == "rope":
                        add_parts(proj)
                    if proj and prep == "rms":
                        rsqrt(proj)
                    if sc:
                        divide(sc)

                run_slots(pool, slot, NC, 1, K_O)


def small_attention_layer(nc, core, name, weights, loaded, kind, scale, tables, ctxT=None, prefetch=()):
    HC = 4
    HD = {"axial": 8}.get(kind, 16)
    H = {"axial": 32, "summed": 4}.get(kind, 16)
    NC = H // HC
    R = HC * HD
    NF = -(-H * HD // P)
    F = H * HD // NF
    causal = kind in ("summed", "grouped")
    split = kind == "split"
    W = (HD + 1) * (2 if split else 1)
    K_PROJ, K_S = NC, 2 * NC
    K_P, K_O = (K_S + 1, K_S + 1) if NC == 1 else (K_S + 2, K_S + 3)
    K_T, K_Y = K_O + 1, K_O + 2
    MID, TURN = (0, 0) if NC == 1 else (1, NC - 2)
    peeled = -(-(K_Y + 1) // (2 * NC))
    QW = 384 if kind in ("summed", "grouped") else D
    wq, wkv, wo = weights["q"], weights.get("kv"), weights["o"]
    with Layer(nc, name) as L:
        sb, sem = L.sb, L.sem
        b_s, b_p, b_q, b_kv, b_t1, b_t2, b_o = (core.bank[0:2], core.bank[2], core.bank[3], core.bank[4],
                                                core.bank[5], core.bank[6], core.bank[7])
        norm = Norm(nc, core, L, b_q)
        qT = [sb(f"qT{u}", [P, NF, P]) for u in range(2)]
        kX = [sb(f"kX{u}", [P, NF, HC, P]) for u in range(2)]
        v_all = [sb(f"v{u}", [P, H * W + P]) for u in range(2)]
        v = [t[:, 0:H * W].rearrange("p (h w) -> p h w", h=H) for t in v_all]
        bias = [sb(f"bias{i}", [P, 2, HC]) for i in range(2)]
        prob = [sb(f"prob{i}", [P, HC, P]) for i in range(2)]
        pT = [sb(f"pT{i}", [P, HC, P]) for i in range(2)]
        smax = sb("smax", [P, 2, HC])
        orec = sb("orec", [P, 2, HC])
        o_two = sb("o_two", [P, 2, HC, HD])
        o_tok = [sb(f"o_tok{u}", [P, NF * P // HD, HD]) for u in range(2)]
        oT = sb("oT", [P, NF, P])
        q_tok, k_tok = sb("q_tok", [P, NF * P]), sb("k_tok", [P, NF * P])
        yb = sb("yb", [P, D])
        if ctxT is not None:
            cT = [sb(f"cT{u}", [P, P]) for u in range(2)]
            ctx_in = [sem(f"ctx_in{u}") for u in range(2)]
            if split:
                cT2 = [sb(f"cT2{u}", [P, P]) for u in range(2)]
        consts = {n: sb(f"t_{n}", shape, dt) for n, (shape, dt, _) in tables.items()}
        masks = consts["masks"]
        if causal:
            ident_b, mask_b = sb("ident_b", [P, P], BF16), sb("mask_b", [P, HC, P], BF16)
        if kind == "axial":
            rot = sb("rot", [P, D])
            sin_t, cos_t, turns = (sb(n, [P, NB, HD]) for n in ("sin_t", "cos_t", "turns"))
            whole, angles_ready = sb("whole", [P, NB, HD], I32), sem("angles_ready")
        if kind == "summed":
            rot, raw, pair = sb("rot", [P, D]), sb("raw", [P, 384]), sb("pair", [P, 2, 4, 16])
        if kind == "grouped":
            rot, raw, turnd = sb("rot", [P, 320]), sb("raw", [P, 384]), sb("turnd", [P, 320])
        if kind == "split":
            rot, raw, v_raw = sb("rot", [P, 512]), sb("raw", [P, 512]), sb("v_raw", [P, D])

        if kind in ("grouped", "split"):
            n_rr = 20 if kind == "grouped" else 32
            ss, rr = sb("ss", [P, n_rr]), sb("rr", [P, n_rr])
        tables_in, tables_done, ctx_zeroed = sem("tables_in"), sem("tables_done"), sem("ctx_zeroed")
        (q_made, kv_made, qk_ready, qk_turned, qT_kept, kX_kept, v_kept, s_made, d_ready, e_ready, p_turned,
         pT_kept, o_made, o_kept, o_turned, oT_kept, y_made, y_kept, ss_ready, rr_ready) = (sem(n) for n in (
             "q_made", "kv_made", "qk_ready", "qk_turned", "qT_kept", "kX_kept", "v_kept", "s_made", "d_ready",
             "e_ready", "p_turned", "pT_kept", "o_made", "o_kept", "o_turned", "oT_kept", "y_made",
             "y_kept", "ss_ready", "rr_ready"))
        wide = [P, HC, P]
        MAIN = P - 16
        parts = ((0, MAIN), (MAIN, P)) if split else ((0, P),)

        with nc.Block() as block:
            @block.sync
            def _(sp):
                for n, (_, _, source) in tables.items():
                    ap = consts[n][tuple(slice(None) for _ in consts[n].shape)]
                    if len(consts[n].shape) == 3:
                        ap = ap.rearrange("p a b -> p (a b)")
                    for rows, src in source:
                        sp.dma_start(ap[rows, :], src).then_inc(tables_in, 16)
                if ctxT is not None:
                    if split:
                        sp.wait_ge(ctx_zeroed, 1)

                    def load(b, u):
                        src = ctxT[bass.ds(b, 1), :, :].rearrange("a p t -> (a p) t")
                        if split:
                            sp.dma_start(cT[u][:, 0:MAIN], src[:, 0:MAIN]).then_inc(ctx_in[u], 16)
                            sp.dma_start(cT2[u][:, MAIN:], src[:, MAIN:]).then_inc(ctx_in[u], 16)
                        else:
                            sp.dma_start(cT[u][:, :], src).then_inc(ctx_in[u], 16)
                    load(0, 0)
                    load(1, 1)
                for fetch in prefetch:
                    fetch(sp)
                if ctxT is not None:
                    with sp.Fori(1, NB // 2) as i:
                        for u in range(2):
                            sp.wait_ge(kv_made, nth(2 * i + u - 2))
                            load(2 * i + u, u)

            @block.tensor
            def _(pe):
                norm.prime_pe(pe)
                for s in (kv_made, qk_turned, s_made, p_turned, o_made, o_turned, y_made):
                    pe.sem_inc(s, SPARE)
                pe.wait_ge(loaded[0], loaded[1])
                pe.wait_ge(tables_done, 1)

                def project(b, u):
                    pe.wait_ge(norm.kept, nth(b))
                    pe.wait_ge(qk_ready, nth(b - 1))
                    for k in range(KD):
                        last = nc.tensor.matmul(b_q[:, 0:QW], norm.xnT[u][:, k, :], wq[:, k, :],
                                                start=(k == 0), stop=(k == KD - 1))
                    if ctxT is not None:
                        last.then_inc(q_made, 1)
                        pe.wait_ge(ctx_in[u], (32 if split else 16) * (b // 2 + 1))
                        pe.wait_ge(v_kept, nth(b - 1))
                        last = nc.tensor.matmul(b_kv[:, :], cT[u][:, :], wkv[:, 0, :], start=True, stop=not split)
                        if split:
                            last = nc.tensor.matmul(b_kv[:, :], cT2[u][:, :], wkv[:, 1, :], start=False, stop=True)
                    last.then_inc(kv_made, 1)

                def turn_qk(b, u):
                    pe.wait_ge(qk_ready, nth(b))
                    pe.wait_ge(kX_kept, nth(b - 1))
                    pe.wait_ge(qT_kept, nth(b - 1))
                    for i, src in enumerate((q_tok, k_tok)):
                        for k in range(NF):
                            at = 2 * P * i + P * k
                            last = nc.tensor.transpose(b_t2[:, at:at + P], src[:, P * k:P * k + P],
                                                       core.ident[:, :])
                    last.then_inc(qk_turned, 1)

                def scores(it):
                    b, u, c, f = it
                    if c == 0:
                        pe.wait_ge(qT_kept, nth(b))
                        pe.wait_ge(kX_kept, nth(b))
                    held(pe, e_ready, f - 1)
                    i = c % 2 if NC > 1 else u
                    if causal:
                        nc.tensor.matmul(b_s[i][:, :], ident_b[:, :], mask_b[:, :, :].rearrange(
                            "p h k -> p (h k)"), start=True, stop=False)
                    at, k = R * c % F, R * c // F
                    nc.tensor.matmul(b_s[i][:, :], qT[u][at:at + R, k, :],
                                     kX[u][at:at + R, k, :, :].rearrange("p h k -> p (h k)"),
                                     start=not causal, stop=True).then_inc(s_made, 1)

                def turn_probs(it):
                    b, u, c, f = it
                    i = c % 2 if NC > 1 else u
                    pe.wait_ge(e_ready, f + 1)
                    pe.wait_ge(pT_kept, nth(f - 1))
                    for j in range(HC):
                        last = nc.tensor.transpose(b_p[:, P * j:P * j + P], prob[i][:, j, :], core.ident[:, :])
                    last.then_inc(p_turned, 1)

                def heads_out(it):
                    b, u, c, f = it
                    i = c % 2 if NC > 1 else u
                    if c == 0:
                        pe.wait_ge(v_kept, nth(b))
                    pe.wait_ge(pT_kept, nth(f))
                    pe.wait_ge(o_kept, nth(f - 1))
                    for j in range(HC):
                        at = W * (HC * c + j)
                        last = nc.tensor.matmul(b_o[:, P * j:P * j + P], pT[i][:, j, :],
                                                v_all[u][:, at:at + P], start=True, stop=True)
                    last.then_inc(o_made, 1)

                def turn_out(b, u):
                    pe.wait_ge(o_kept, nth(NC * b + NC - 1))
                    pe.wait_ge(y_kept, nth(b - 1))
                    for k in range(NF):
                        last = nc.tensor.transpose(b_t1[:, P * k:P * k + P],
                                                   o_tok[u][:, :, :].rearrange("p h d -> p (h d)")[:, P * k:P * k + P],
                                                   core.ident[:, :])
                    last.then_inc(o_turned, 1)

                def project_out(b, u):
                    pe.wait_ge(oT_kept, nth(b))
                    for k in range(NF):
                        last = nc.tensor.matmul(b_t1[:, 0:D], oT[0:F, k, :], wo[0:F, k, :],
                                                start=(k == 0), stop=(k == NF - 1))
                    last.then_inc(y_made, 1)

                def slot(b, u, c):
                    pj, sc, pr, ou, tn, fin = (behind(b, u, c, k, NC) for k in (K_PROJ, K_S, K_P, K_O, K_T, K_Y))
                    if pr:
                        turn_probs(pr)
                    if pj and c == 0:
                        project(pj[0], pj[1])
                    if fin and fin[2] == NC - 1:
                        project_out(fin[0], fin[1])
                    if tn and tn[2] == NC - 1:
                        turn_out(tn[0], tn[1])
                    if ou:
                        heads_out(ou)
                    if sc:
                        scores(sc)
                    if pj and c == TURN:
                        turn_qk(pj[0], pj[1])
                    if c == NC - 1 and behind(b, u, c, 0, NC):
                        held(pe, qk_ready, nth(b - 1))
                        norm.turn(pe, b)

                run_slots(pe, slot, NC, peeled, K_Y)

            @block.vector
            def _(dve):
                for s in (d_ready, kX_kept, v_kept, o_kept, y_kept, qk_ready, ss_ready):
                    dve.sem_inc(s, SPARE)
                for u in range(2):
                    nc.vector.memset(v_all[u][:, :], 1.0)
                    if F < P:
                        nc.vector.memset(o_tok[u][:, :, :], 0.0)
                if F < P:
                    nc.vector.memset(q_tok[:, :], 0.0)
                    nc.vector.memset(k_tok[:, :], 0.0)
                if split:
                    for u in range(2):
                        nc.vector.memset(cT[u][:, :], 0.0)
                        nc.vector.memset(cT2[u][:, :], 0.0)
                dve.drain().then_inc(ctx_zeroed, 1)
                dve.wait_ge(tables_in, 16 * sum(len(t[2]) for t in tables.values()))
                if kind == "axial":
                    for i, angle in enumerate((sin_t, cos_t)):
                        a4 = angle[:, :, :].rearrange("p b (q h e) -> p b q h e", q=2, h=2)
                        for q in range(2):
                            for h in range(2):
                                for e in range(2):
                                    nc.vector.tensor_scalar(a4[:, :, q, h, e], consts["pos"][:, :, q],
                                                            FREQ[h], i * PI / 2, ALU.mult, ALU.add)
                        dve.drain()
                        nc.vector.tensor_scalar(turns[:, :, :], angle[:, :, :], 1 / (2 * PI), None, ALU.mult)
                        dve.drain()
                        nc.vector.tensor_copy(whole[:, :, :], turns[:, :, :])
                        dve.drain()
                        nc.vector.tensor_copy(turns[:, :, :], whole[:, :, :])
                        dve.drain()
                        nc.vector.scalar_tensor_tensor(angle[:, :, :], turns[:, :, :], -2 * PI, angle[:, :, :],
                                                       ALU.mult, ALU.add)
                        for op, bound, step in ((ALU.is_gt, PI, -2 * PI), (ALU.is_lt, -PI, 2 * PI)):
                            dve.drain()
                            nc.vector.tensor_scalar(turns[:, :, :], angle[:, :, :], bound, step, op, ALU.mult)
                            dve.drain()
                            nc.vector.tensor_tensor(angle[:, :, :], angle[:, :, :], turns[:, :, :], ALU.add)
                        dve.drain()
                        nc.vector.tensor_scalar(angle[:, :, :], angle[:, :, :], PI, -PI, ALU.min, ALU.max
                                                ).then_inc(angles_ready, 1)
                    dve.wait_ge(angles_ready, 4)
                    nc.vector.tensor_scalar(sin_t[:, :, 0::2], sin_t[:, :, 0::2], -1.0, None, ALU.mult)
                if causal:
                    nc.vector.tensor_copy(ident_b[:, :], core.ident[:, :])
                    nc.vector.tensor_copy(mask_b[:, :, :], consts["causal"][:, :].unsqueeze(1).to_broadcast(wide))
                if split:
                    for u in range(2):
                        for i in range(2):
                            at = (HD + 1) * (i + 1) - 1
                            nc.vector.tensor_copy(v[u][:, :, at], consts["part"][:, i:i + 1].to_broadcast([P, H]))
                dve.drain().then_inc(tables_done, 1)

                def axial(b, u, second):
                    if second:
                        dve.wait_ge(kv_made, nth(b))
                    else:
                        dve.wait_ge(q_made, b + 1)
                        dve.wait_ge(qk_turned, nth(b - 1))
                    cs = cos_t[:, bass.ds(b, 1), :].to_broadcast([P, H, HD])
                    src, tok = (b_kv[:, 0:D], k_tok) if second else (b_q[:, 0:D], q_tok)
                    x = src.rearrange("p (h d) -> p h d", h=H)
                    t = tok[:, :].rearrange("p (h d) -> p h d", h=H)
                    nc.vector.tensor_tensor(t, x, cs, ALU.mult)
                    r = rot[:, :].rearrange("p (h d) -> p h d", h=H)
                    for i in range(2):
                        sn = sin_t[:, bass.ds(b, 1), i::2].to_broadcast([P, H, HD // 2])
                        nc.vector.tensor_tensor(r[:, :, i::2], x[:, :, 1 - i::2], sn, ALU.mult)
                    dve.drain()
                    nc.vector.tensor_tensor(tok[:, :], tok[:, :], rot[:, :], ALU.add)
                    if second:
                        dve.drain().then_inc(qk_ready, 1)
                    else:
                        dve.drain()

                def values_axial(b, u):
                    dve.wait_ge(kv_made, nth(b))
                    held(dve, o_made, nth(NC * (b - 2) + NC - 1))
                    nc.vector.tensor_copy(v[u][:, :, 0:HD], b_kv[:, D:2 * D].rearrange("p (h d) -> p h d", h=H)
                                          ).then_inc(v_kept, 1)

                def summed(b, u, second):
                    if second:
                        return
                    dve.wait_ge(kv_made, nth(b))
                    dve.wait_ge(qk_turned, nth(b - 1))
                    nc.vector.tensor_tensor(raw[:, :], b_q[:, 0:384], consts["bias"][:, :], ALU.add)
                    dve.drain()
                    nc.vector.tensor_reduce(pair[:, 0, :, :], raw[:, 0:D].rearrange("p (h g d) -> p h d g", h=4, g=4),
                                            AX.X, ALU.add)
                    nc.vector.tensor_copy(pair[:, 1, :, :], raw[:, D:D + 64].rearrange("p (h d) -> p h d", h=4))
                    dve.drain()
                    x = pair[:, :, :, :].rearrange("p a h d -> p (a h) d")
                    cs = consts["cos"][:, :].unsqueeze(1).to_broadcast([P, 8, 8])
                    sn = consts["sin"][:, :].unsqueeze(1).to_broadcast([P, 8, 8])
                    turns_ = [rot[:, 64 * i:64 * i + 64].rearrange("p (h d) -> p h d", h=8) for i in range(4)]
                    nc.vector.tensor_tensor(turns_[0], x[:, :, 0::2], cs, ALU.mult)
                    nc.vector.tensor_tensor(turns_[1], x[:, :, 1::2], sn, ALU.mult)
                    nc.vector.tensor_tensor(turns_[2], x[:, :, 0::2], sn, ALU.mult)
                    nc.vector.tensor_tensor(turns_[3], x[:, :, 1::2], cs, ALU.mult)
                    dve.drain()
                    for i, tok in enumerate((q_tok, k_tok)):
                        t = tok[:, 0:64].rearrange("p (h d) -> p h d", h=4)
                        s = slice(4 * i, 4 * i + 4)
                        nc.vector.tensor_tensor(t[:, :, 0:8], turns_[0][:, s, :], turns_[1][:, s, :], ALU.subtract)
                        nc.vector.tensor_tensor(t[:, :, 8:16], turns_[2][:, s, :], turns_[3][:, s, :], ALU.add)
                    dve.drain().then_inc(qk_ready, 1)

                def values_raw(b, u):
                    held(dve, o_made, nth(NC * (b - 2) + NC - 1))
                    src = raw[:, D + 64:D + 128].rearrange("p (h d) -> p h d", h=4)
                    if kind == "grouped":
                        for r in range(4):
                            nc.vector.tensor_copy(v[u][:, r::4, 0:HD], src)
                    else:
                        nc.vector.tensor_copy(v[u][:, :, 0:HD], src)
                    dve.drain().then_inc(v_kept, 1)

                def grouped(b, u, second):
                    a = turnd[:, :].rearrange("p (h d) -> p h d", h=20)
                    if second:
                        return grouped_norm(b, a)
                    dve.wait_ge(kv_made, nth(b))
                    dve.wait_ge(qk_turned, nth(b - 1))
                    nc.vector.tensor_tensor(raw[:, :], b_q[:, 0:384], consts["bias"][:, :], ALU.add)
                    dve.drain()
                    x = raw[:, 0:320].rearrange("p (h d) -> p h d", h=20)
                    r = rot[:, :].rearrange("p (h d) -> p h d", h=20)
                    nc.vector.tensor_tensor(r, x, x, ALU.mult)
                    dve.drain()
                    nc.vector.tensor_reduce(ss[:, :], r, AX.X, ALU.add)
                    dve.drain()
                    nc.vector.tensor_scalar(ss[:, :], ss[:, :], 1.0 / HD, 1.1920929e-07, ALU.mult, ALU.add
                                            ).then_inc(ss_ready, 1)
                    nc.vector.tensor_tensor(a, x, consts["cos"][:, :].unsqueeze(1).to_broadcast([P, 20, HD]), ALU.mult)
                    for i in range(2):
                        lo, hi = 8 * i, 8 * i + 8
                        nc.vector.tensor_tensor(r[:, :, lo:hi], x[:, :, 8 - lo:16 - lo],
                                                consts["sin"][:, lo:hi].unsqueeze(1).to_broadcast([P, 20, 8]),
                                                ALU.mult)
                    dve.drain()
                    nc.vector.tensor_tensor(a, a, r, ALU.add)
                    dve.drain()

                def grouped_norm(b, a):
                    dve.wait_ge(rr_ready, b + 1)
                    nc.vector.tensor_tensor(ss[:, :], rr[:, :], consts["gain"][:, :], ALU.mult)
                    dve.drain()
                    nc.vector.tensor_tensor(q_tok[:, :].rearrange("p (h d) -> p h d", h=16), a[:, 0:16, :],
                                            ss[:, 0:16].unsqueeze(2).to_broadcast([P, 16, HD]), ALU.mult)
                    k4 = k_tok[:, :].rearrange("p (h r d) -> p h r d", h=4, r=4)
                    for i in range(4):
                        nc.vector.tensor_tensor(k4[:, :, i, :], a[:, 16:20, :],
                                                ss[:, 16:20].unsqueeze(2).to_broadcast([P, 4, HD]), ALU.mult)
                    dve.drain().then_inc(qk_ready, 1)

                def layered(b, u, second):
                    n = 2 * H
                    x = raw[:, 0:2 * D].rearrange("p (h d) -> p h d", h=n)
                    wide_h = [P, n, HD]
                    if second:
                        return layered_norm(b, x, wide_h)
                    dve.wait_ge(q_made, b + 1)
                    dve.wait_ge(kv_made, nth(b))
                    kv = b_kv[:, :].rearrange("p (h a d) -> p h a d", h=H, a=2)
                    bias = consts["bias"][:, D:].rearrange("p (h a d) -> p h a d", h=H, a=2)
                    nc.vector.tensor_tensor(raw[:, 0:D], b_q[:, 0:D], consts["bias"][:, 0:D], ALU.add)
                    nc.vector.tensor_tensor(x[:, H:, :], kv[:, :, 0, :], bias[:, :, 0, :], ALU.add)
                    nc.vector.tensor_tensor(v_raw[:, :].rearrange("p (h d) -> p h d", h=H), kv[:, :, 1, :],
                                            bias[:, :, 1, :], ALU.add)
                    dve.drain()
                    nc.vector.tensor_reduce(ss[:, :], x, AX.X, ALU.add)
                    dve.drain()
                    nc.vector.tensor_scalar(ss[:, :], ss[:, :], 1.0 / HD, None, ALU.mult)
                    dve.drain()
                    nc.vector.tensor_tensor(x, x, ss[:, :].unsqueeze(2).to_broadcast(wide_h), ALU.subtract)
                    dve.drain()
                    r = rot[:, :].rearrange("p (h d) -> p h d", h=n)
                    nc.vector.tensor_tensor(r, x, x, ALU.mult)
                    dve.drain()
                    nc.vector.tensor_reduce(ss[:, :], r, AX.X, ALU.add)
                    dve.drain()
                    nc.vector.tensor_scalar(ss[:, :], ss[:, :], 1.0 / HD, 1e-6, ALU.mult, ALU.add
                                            ).then_inc(ss_ready, 1)

                def layered_norm(b, x, wide_h):
                    dve.wait_ge(rr_ready, b + 1)
                    nc.vector.tensor_tensor(x, x, rr[:, :].unsqueeze(2).to_broadcast(wide_h), ALU.mult)
                    dve.drain()
                    dve.wait_ge(qk_turned, nth(b - 1))
                    for i, tok in enumerate((q_tok, k_tok)):
                        t = tok[:, :].rearrange("p (h d) -> p h d", h=H)
                        w, s = (consts[m][:, HD * i:HD * i + HD].unsqueeze(1).to_broadcast([P, H, HD])
                                for m in ("affine_w", "affine_b"))
                        nc.vector.tensor_tensor(t, x[:, H * i:H * i + H, :], w, ALU.mult)
                        dve.drain()
                        nc.vector.tensor_tensor(t, t, s, ALU.add)
                    dve.drain().then_inc(qk_ready, 1)

                def values_split(b, u):
                    held(dve, o_made, nth(NC * (b - 2) + NC - 1))
                    src = v_raw[:, :].rearrange("p (h d) -> p h d", h=H)
                    for i in range(2):
                        at = (HD + 1) * i
                        nc.vector.tensor_scalar(v[u][:, :, at:at + HD], src, consts["part"][:, i:i + 1], None, ALU.mult)
                    dve.drain().then_inc(v_kept, 1)

                PREPARE = {"axial": axial, "summed": summed, "grouped": grouped, "split": layered}
                VALUES = {"axial": values_axial, "summed": values_raw, "grouped": values_raw, "split": values_split}

                def keep_kX(b, u):
                    dve.wait_ge(qT_kept, nth(b))
                    held(dve, s_made, nth(NC * (b - 2) + NC - 1))
                    for j in range(HC):
                        nc.vector.tensor_scalar(kX[u][0:F, :, j, :], b_t2[0:F, D:D + P * NF].rearrange(
                            "p (k t) -> p k t", k=NF), masks[0:F, j:j + 1], None, ALU.mult)
                    dve.drain().then_inc(kX_kept, 1)

                def find_max(it):
                    b, u, c, f = it
                    i = c % 2 if NC > 1 else u
                    dve.wait_ge(s_made, nth(f))
                    s = b_s[i][:, :].rearrange("p (h k) -> p h k", h=HC)
                    for a, (lo, hi) in enumerate(parts):
                        nc.vector.tensor_reduce(smax[:, a, :], s[:, :, lo:hi], AX.X, ALU.max)
                    dve.drain()
                    n = len(parts)
                    nc.vector.tensor_scalar(bias[i][:, 0:n, :], smax[:, 0:n, :], -scale, None, ALU.mult
                                            ).then_inc(d_ready, 1)

                def keep_out(it):
                    b, u, c, f = it
                    i = c % 2 if NC > 1 else u
                    dve.wait_ge(o_made, nth(f))
                    if c == 0:
                        dve.wait_ge(o_turned, nth(b - 2))
                    o = b_o[:, :].rearrange("p (h w) -> p h w", h=HC)
                    out = o_tok[u][:, HC * c:HC * c + HC, :]
                    n = 2 if split else 1
                    for a in range(n):
                        nc.vector.reciprocal(orec[:, a, :], o[:, :, (HD + 1) * (a + 1) - 1])
                    dve.drain()
                    for a in range(n):
                        nc.vector.tensor_tensor(out if n == 1 else o_two[:, a, :, :],
                                                o[:, :, (HD + 1) * a:(HD + 1) * a + HD],
                                                orec[:, a, :].unsqueeze(2).to_broadcast([P, HC, HD]), ALU.mult)
                    if split:
                        dve.drain()
                        nc.vector.tensor_tensor(out, o_two[:, 0, :, :], o_two[:, 1, :, :], ALU.add)
                    dve.drain().then_inc(o_kept, 1)

                def residual(b, u):
                    dve.drain()
                    dve.wait_ge(y_made, nth(b))
                    xb = pick(core.x[:, :, :], b).rearrange("p a d -> p (a d)")
                    nc.vector.tensor_tensor(yb[:, :], b_t1[:, 0:D], consts["out_bias"][:, :], ALU.add
                                            ).then_inc(y_kept, 1)
                    dve.drain()
                    nc.vector.tensor_tensor(xb, xb, yb[:, :], ALU.add)

                def slot(b, u, c):
                    pj, sc, pr, ou, tn, fin = (behind(b, u, c, k, NC) for k in (K_PROJ, K_S, K_P, K_O, K_T, K_Y))
                    ln = behind(b, u, c, 0, NC)
                    if ln and c == 0:
                        norm.moments(dve, b)
                    if ln and c == NC - 1 and NC > 1:
                        norm.normalise(dve, b)
                    if fin and NC == 1:
                        residual(fin[0], fin[1])
                    if ou:
                        keep_out(ou)
                    if sc:
                        find_max(sc)
                    if fin and fin[2] == NC - 1 and NC > 1:
                        residual(fin[0], fin[1])
                    if pj and c == 0:
                        PREPARE[kind](pj[0], pj[1], False)
                    if pj and c == MID:
                        PREPARE[kind](pj[0], pj[1], True)
                    if ln and NC == 1:
                        norm.normalise(dve, b)
                    if pj and c == NC - 1:
                        VALUES[kind](pj[0], pj[1])
                        keep_kX(pj[0], pj[1])

                run_slots(dve, slot, NC, peeled, K_Y)

            @block.scalar
            def _(act):
                norm.prime_act(act)
                if kind == "axial":
                    act.wait_ge(angles_ready, 2)
                    for angle in (sin_t, cos_t):
                        nc.scalar.activation(angle[:, :, :], angle[:, :, :], ACT.Sin).then_inc(angles_ready, 1)
                for s in (qT_kept, pT_kept, oT_kept):
                    act.sem_inc(s, SPARE)

                def exponentials(it):
                    b, u, c, f = it
                    i = c % 2 if NC > 1 else u
                    act.wait_ge(d_ready, nth(f))
                    act.wait_ge(p_turned, nth(f - 2))
                    s = b_s[i][:, :].rearrange("p (h k) -> p h k", h=HC)
                    for j in range(HC):
                        for a, (lo, hi) in enumerate(parts):
                            last = nc.scalar.activation(prob[i][:, j, lo:hi], s[:, j, lo:hi], ACT.Exp,
                                                        bias=bias[i][:, a, j:j + 1], scale=scale)
                    last.then_inc(e_ready, 1)

                def keep_probs(it):
                    b, u, c, f = it
                    i = c % 2 if NC > 1 else u
                    act.wait_ge(p_turned, nth(f))
                    act.wait_ge(o_made, nth(f - 2))
                    nc.scalar.copy(pT[i][:, :, :].rearrange("p h k -> p (h k)"), b_p[:, :]).then_inc(pT_kept, 1)

                def keep_oT(b, u):
                    act.wait_ge(o_turned, nth(b))
                    act.wait_ge(y_made, nth(b - 1))
                    nc.scalar.copy(oT[0:F, :, :].rearrange("p k t -> p (k t)"), b_t1[0:F, 0:NF * P]
                                   ).then_inc(oT_kept, 1)

                def keep_qT(b, u):
                    act.wait_ge(qk_turned, nth(b))
                    held(act, s_made, nth(NC * (b - 2) + NC - 1))
                    nc.scalar.copy(qT[u][0:F, :, :].rearrange("p k t -> p (k t)"), b_t2[0:F, 0:NF * P]
                                   ).then_inc(qT_kept, 1)

                def slot(b, u, c):
                    pj, sc, pr, ou, tn, fin = (behind(b, u, c, k, NC) for k in (K_PROJ, K_S, K_P, K_O, K_T, K_Y))
                    if pr:
                        keep_probs(pr)
                    if tn and tn[2] == NC - 1:
                        keep_oT(tn[0], tn[1])
                    if sc:
                        exponentials(sc)
                    if pj and c == TURN:
                        keep_qT(pj[0], pj[1])
                    if c == NC - 1 and behind(b, u, c, 0, NC):
                        norm.keep(act, b, u, ((kv_made, nth(b - 2)),) if not (isinstance(b, int) and b < 2) else ())

                run_slots(act, slot, NC, peeled, K_Y)

            @block.gpsimd
            def _(pool):
                def rsqrt(b):
                    pool.wait_ge(ss_ready, nth(b))
                    nc.gpsimd.tensor_tensor(rr[:, :], ss[:, :], core.minus_half[:, 0:n_rr], ALU.pow).then_inc(rr_ready, 1)

                def slot(b, u, c):
                    pj = behind(b, u, c, K_PROJ, NC)
                    if pj and c == 0 and kind in ("grouped", "split"):
                        rsqrt(pj[0])
                    if c == 0 and behind(b, u, c, 0, NC):
                        norm.rsqrt(pool, b)

                run_slots(pool, slot, NC, peeled, K_Y)


def linear_attention_layer(nc, core, name, weights, loaded, tables, prefetch=()):
    H, HD, EPS = 16, 16, 1e-6
    HF = P // HD
    KVW = P + HF
    wqk, wv, wo = weights
    K_PROJ, K_KV, K_OUT, K_Y = 1, 2, 3, 4
    peeled = 3
    with Layer(nc, name) as L:
        sb, sem = L.sb, L.sem
        b_qk, b_v, b_x, b_t, b_kv, b_o, b_ot, b_y = core.bank
        norm = Norm(nc, core, L, b_x)
        raw, low, e = sb("raw", [P, 512]), sb("low", [P, 512]), sb("e", [P, 512])
        feat = [sb(f"feat{u}", [P, 512]) for u in range(2)]
        v = [sb(f"v{u}", [P, KD, KVW]) for u in range(2)]
        qT = [sb(f"qT{u}", [P, KD, P]) for u in range(2)]
        kv = sb("kv", [P, KD, KVW])
        den, o_tok, oT, yb = sb("den", [P, KD, HF]), sb("o_tok", [P, D]), sb("oT", [P, KD, P]), sb("yb", [P, D])
        consts = {n: sb(f"t_{n}", [P, w]) for n, (w, _) in tables.items()}
        tables_in, tables_done = sem("tables_in"), sem("tables_done")
        (qkv_made, low_ready, e_ready, feat_ready, turned, qT_kept, kv_made, kv_kept, o_made, o_kept,
         o_turned, oT_kept, y_made, y_kept) = (sem(n) for n in (
             "qkv_made", "low_ready", "e_ready", "feat_ready", "turned", "qT_kept", "kv_made", "kv_kept",
             "o_made", "o_kept", "o_turned", "oT_kept", "y_made", "y_kept"))

        with nc.Block() as block:
            @block.sync
            def _(sp):
                for n, (_, src) in tables.items():
                    sp.dma_start(consts[n][:, :], src).then_inc(tables_in, 16)
                for fetch in prefetch:
                    fetch(sp)

            @block.tensor
            def _(pe):
                norm.prime_pe(pe)
                for s in (turned, kv_made, o_made, o_turned, y_made):
                    pe.sem_inc(s, SPARE)
                pe.wait_ge(loaded[0], loaded[1])

                def project(b, u):
                    pe.wait_ge(norm.kept, nth(b))
                    pe.wait_ge(feat_ready, nth(b - 1))
                    for bank, w, n in ((b_qk, wqk, 512), (b_v, wv, D)):
                        for k in range(KD):
                            last = nc.tensor.matmul(bank[:, 0:n], norm.xnT[u][:, k, :], w[:, k, :],
                                                    start=(k == 0), stop=(k == KD - 1))
                    last.then_inc(qkv_made, 1)

                def key_value(b, u):
                    pe.wait_ge(feat_ready, nth(b))
                    pe.wait_ge(qT_kept, nth(b - 1))
                    for k in range(KD):
                        last = nc.tensor.transpose(b_t[:, P * k:P * k + P], feat[u][:, P * k:P * k + P],
                                                   core.ident[:, :])
                    last.then_inc(turned, 1)
                    pe.wait_ge(kv_kept, nth(b - 1))
                    for k in range(KD):
                        last = nc.tensor.matmul(b_kv[:, KVW * k:KVW * k + KVW], feat[u][:, D + P * k:D + P * k + P],
                                                v[u][:, k, :], start=True, stop=True)
                    last.then_inc(kv_made, 1)

                def outputs(b, u):
                    pe.wait_ge(kv_kept, nth(b))
                    pe.wait_ge(qT_kept, nth(b))
                    pe.wait_ge(o_kept, nth(b - 1))
                    for k in range(KD):
                        last = nc.tensor.matmul(b_o[:, KVW * k:KVW * k + KVW], qT[u][:, k, :], kv[:, k, :],
                                                start=True, stop=True)
                    last.then_inc(o_made, 1)

                def turn_out(b, u):
                    pe.wait_ge(o_kept, nth(b))
                    pe.wait_ge(oT_kept, nth(b - 1))
                    for k in range(KD):
                        last = nc.tensor.transpose(b_ot[:, P * k:P * k + P], o_tok[:, P * k:P * k + P], core.ident[:, :])
                    last.then_inc(o_turned, 1)

                def project_out(b, u):
                    pe.wait_ge(oT_kept, nth(b))
                    pe.wait_ge(y_kept, nth(b - 1))
                    for k in range(KD):
                        last = nc.tensor.matmul(b_y[:, 0:D], oT[:, k, :], wo[:, k, :],
                                                start=(k == 0), stop=(k == KD - 1))
                    last.then_inc(y_made, 1)

                def slot(b, u, c):
                    pj, kvs, out, fin = (behind(b, u, c, k, 1) for k in (K_PROJ, K_KV, K_OUT, K_Y))
                    if fin:
                        turn_out(fin[0], fin[1])
                    if kvs:
                        key_value(kvs[0], kvs[1])
                    if fin:
                        project_out(fin[0], fin[1])
                    if pj:
                        project(pj[0], pj[1])
                    if out:
                        outputs(out[0], out[1])
                    if behind(b, u, c, 0, 1):
                        norm.turn(pe, b)

                run_slots(pe, slot, 1, peeled, K_Y)

            @block.vector
            def _(dve):
                for s in (low_ready, feat_ready, kv_kept, o_kept, y_kept):
                    dve.sem_inc(s, SPARE)
                for u in range(2):
                    nc.vector.memset(v[u][:, :, :], 1.0)
                dve.wait_ge(tables_in, 16 * len(tables))

                def features(b, u):
                    dve.wait_ge(qkv_made, b + 1)
                    nc.vector.tensor_tensor(raw[:, :], b_qk[:, :], consts["qk_bias"][:, :], ALU.add)
                    dve.drain()
                    nc.vector.tensor_scalar(low[:, :], raw[:, :], 0.0, None, ALU.min).then_inc(low_ready, 1)
                    held(dve, kv_made, nth(b - 2))
                    nc.vector.tensor_tensor(v[u][:, :, 0:P], b_v[:, 0:D].rearrange("p (k e) -> p k e", k=KD),
                                            consts["v_bias"][:, :].rearrange("p (k e) -> p k e", k=KD), ALU.add)
                    dve.wait_ge(e_ready, b + 1)
                    nc.vector.scalar_tensor_tensor(feat[u][:, :], raw[:, :], 0.0, e[:, :], ALU.max, ALU.add
                                                   ).then_inc(feat_ready, 1)

                def keep_kv(b, u):
                    dve.wait_ge(kv_made, nth(b))
                    dve.wait_ge(o_made, nth(b - 1))
                    nc.vector.tensor_tensor(kv[:, :, :], b_kv[:, 0:KD * KVW].rearrange("p (k e) -> p k e", k=KD),
                                            consts["own_head"][:, :].unsqueeze(1).to_broadcast([P, KD, KVW]),
                                            ALU.mult).then_inc(kv_kept, 1)

                def keep_out(b, u):
                    dve.wait_ge(o_made, nth(b))
                    o = b_o[:, 0:KD * KVW].rearrange("p (k e) -> p k e", k=KD)
                    nc.vector.tensor_scalar(den[:, :, :], o[:, :, P:], EPS, None, ALU.add)
                    dve.drain()
                    nc.vector.reciprocal(den[:, :, :], den[:, :, :])
                    dve.drain()
                    dve.wait_ge(o_turned, nth(b - 1))
                    for k in range(KD):
                        last = nc.vector.tensor_tensor(
                            o_tok[:, P * k:P * k + P].rearrange("p (h d) -> p h d", h=HF),
                            o[:, k, 0:P].rearrange("p (h d) -> p h d", h=HF),
                            den[:, k, :].unsqueeze(2).to_broadcast([P, HF, HD]), ALU.mult)
                    last.then_inc(o_kept, 1)

                def residual(b, u):
                    dve.drain()
                    dve.wait_ge(y_made, nth(b))
                    xb = pick(core.x[:, :, :], b).rearrange("p a d -> p (a d)")
                    nc.vector.tensor_tensor(yb[:, :], b_y[:, 0:D], consts["out_bias"][:, :], ALU.add
                                            ).then_inc(y_kept, 1)
                    dve.drain()
                    nc.vector.tensor_tensor(xb, xb, yb[:, :], ALU.add)

                def slot(b, u, c):
                    pj, kvs, out, fin = (behind(b, u, c, k, 1) for k in (K_PROJ, K_KV, K_OUT, K_Y))
                    if kvs:
                        keep_kv(kvs[0], kvs[1])
                    if fin:
                        residual(fin[0], fin[1])
                    if pj:
                        features(pj[0], pj[1])
                    if out:
                        keep_out(out[0], out[1])
                    if behind(b, u, c, 0, 1):
                        norm.moments(dve, b)
                        norm.normalise(dve, b)

                run_slots(dve, slot, 1, peeled, K_Y)

            @block.scalar
            def _(act):
                norm.prime_act(act)
                for s in (qT_kept, oT_kept):
                    act.sem_inc(s, SPARE)

                def slot(b, u, c):
                    pj, kvs, out, fin = (behind(b, u, c, k, 1) for k in (K_PROJ, K_KV, K_OUT, K_Y))
                    if fin:
                        act.wait_ge(o_turned, nth(fin[0]))
                        held(act, y_made, nth(fin[0] - 1))
                        nc.scalar.copy(oT[:, :, :].rearrange("p k t -> p (k t)"), b_ot[:, 0:D]).then_inc(oT_kept, 1)
                    if kvs:
                        act.wait_ge(turned, nth(kvs[0]))
                        held(act, o_made, nth(kvs[0] - 2))
                        nc.scalar.copy(qT[kvs[1]][:, :, :].rearrange("p k t -> p (k t)"), b_t[:, 0:D]
                                       ).then_inc(qT_kept, 1)
                    if pj:
                        act.wait_ge(low_ready, nth(pj[0]))
                        act.wait_ge(feat_ready, nth(pj[0] - 1))
                        nc.scalar.activation(e[:, :], low[:, :], ACT.Exp).then_inc(e_ready, 1)
                    if behind(b, u, c, 0, 1):
                        norm.keep(act, b, u, ((feat_ready, nth(b - 2)),) if not (isinstance(b, int) and b < 2) else ())

                run_slots(act, slot, 1, peeled, K_Y)

            @block.gpsimd
            def _(pool):
                def slot(b, u, c):
                    if behind(b, u, c, 0, 1):
                        norm.rsqrt(pool, b)

                run_slots(pool, slot, 1, peeled, K_Y)


def look_up_layer(nc, core, name, idx_in, idx_down, lut, w_in, w_down):
    n_in, (width, n_down) = idx_in.shape[1], idx_down.shape
    with Layer(nc, name) as L:
        sb, sem = L.sb, L.sem
        parts = []
        for n, rows, cols in (("in", P, n_in), ("down", width, n_down)):
            parts.append((rows, cols, sb(f"i_{n}", [rows, cols], I32), sb(f"idx_{n}", [rows, cols], BF16),
                          sb(f"hit_{n}", [rows, cols], BF16), sb(f"w_{n}", [rows, cols])))
        table = sb("table", [P, 16])
        loaded, decoded, stored = sem("loaded"), sem("decoded"), sem("stored")
        with nc.Block() as block:
            @block.sync
            def _(sp):
                sp.dma_start(table[:, :], lut.partition_broadcast(P)).then_inc(loaded, 16)
                for (rows, cols, i, *_), src in zip(parts, (idx_in, idx_down)):
                    sp.dma_start(i[:, :], src).then_inc(loaded, 16)
                sp.wait_ge(decoded, 1)
                (_, _, _, _, _, w1), (_, _, _, _, _, w2) = parts
                slices = w_in.shape[0]
                sp.dma_start(w_in.rearrange("s p w -> p s w"),
                             w1[:, :].rearrange("p (s w) -> p s w", s=slices)).then_inc(stored, 16)
                sp.dma_start(w_down.rearrange("s p w -> p s w"),
                             w2[:, :].rearrange("p (s w) -> p s w", s=slices)).then_inc(stored, 16)
                sp.wait_ge(stored, 32)

            @block.vector
            def _(dve):
                dve.wait_ge(loaded, 48)
                for _, _, i, idx, _, w in parts:
                    nc.vector.tensor_copy(idx[:, :], i[:, :])
                    nc.vector.memset(w[:, :], 0.0)
                dve.drain()
                for j in range(16):
                    for rows, _, _, idx, hit, w in parts:
                        nc.vector.tensor_scalar(hit[:, :], idx[:, :], float(j), None, ALU.is_equal)
                        dve.drain()
                        nc.vector.scalar_tensor_tensor(w[:, :], hit[:, :], table[0:rows, j:j + 1], w[:, :],
                                                       ALU.mult, ALU.add)
                dve.drain().then_inc(decoded, 1)


def slices_in(*weights):
    a = np.stack([w.reshape(w.shape[0], KD, P, w.shape[2]) for w in weights], 1)
    n, g, k, p, w = a.shape
    return np.ascontiguousarray(a.transpose(0, 3, 1, 2, 4)).reshape(n, p, g * k * w)


def cut_columns(w, width):
    return w.reshape(w.shape[0], -1, width).transpose(1, 0, 2)


def falling(n):
    return np.ascontiguousarray(np.broadcast_to(np.arange(n, 0, -1, dtype=np.float32), (P, NB, n))
                                ).reshape(P, NB * n)


CAPACITY = 80


def rows_in(w):
    k = w.shape[0] // P
    return w.reshape(k, P, -1).transpose(1, 0, 2).reshape(P, -1)


def rope_angles(dim):
    f = np.float32
    freq = f(1.0) / np.power(f(10000.0), np.arange(0, dim, 2, dtype=f) / f(dim), dtype=f)
    angle = np.arange(P, dtype=f)[:, None] * freq[None, :]
    return np.cos(angle), np.sin(angle)


def lay_out(i):
    a = {"x": i["x"], "ident": np.eye(P, dtype=np.float32)}
    a["falling8"], a["falling4"], a["falling16"], a["falling32"] = (falling(n) for n in (8, 4, 16, 32))
    a["below"] = np.triu(np.ones((P, P), np.float32), 1)
    cat = np.concatenate
    a["l1f_in"] = slices_in(cat([i["L1_ffn_W_gate"], cut_columns(i["L1_ffn_shared_gate"].T, 128)]),
                            cat([i["L1_ffn_W_up"], cut_columns(i["L1_ffn_shared_up"].T, 128)]))
    a["l1f_down"] = cat([i["L1_ffn_W_down"], i["L1_ffn_shared_down"].T.reshape(2, 128, D)])
    a["l1f_router"] = i["L1_ffn_router_w"].T
    a["l1f_bias"] = i["L1_ffn_e_bias"]
    a["place_iota"] = np.tile(np.arange(CAPACITY, dtype=np.float32), (P, 1))
    a["token_iota"] = np.tile(np.arange(NB * P, dtype=np.float16), (P, 1))
    number = (np.arange(P)[:, None] + P * np.arange(NB)[None, :]).astype(np.float16)
    a["token_number"] = np.stack([number, 0 * number, 0 * number], 2).reshape(P, 3 * NB)
    w1, w3 = ((w.reshape(8, D, 2, 88).transpose(0, 2, 1, 3).reshape(16, D, 88))
              for w in (i["L2_ffn_w1"], i["L2_ffn_w3"]))
    a["l2f_in"] = slices_in(cat([w1, cut_columns(i["L2_ffn_ws1"], 88)]),
                            cat([w3, cut_columns(i["L2_ffn_ws3"], 88)]))
    a["l2f_down"] = cat([i["L2_ffn_w2"].reshape(16, 88, D), i["L2_ffn_ws2"].reshape(4, 88, D)])
    a["l2f_router"] = i["L2_ffn_w_router"]
    a["l3f_in"] = slices_in(cat([i["L3_ffn_w_up"], cut_columns(i["L3_ffn_shared_up"], 128)]))
    a["l3f_down"] = cat([i["L3_ffn_w_down"], i["L3_ffn_shared_down"].reshape(4, 128, D)])
    a["l3f_router"] = i["L3_ffn_router_weight"].T
    a["l3f_bias"] = i["L3_ffn_e_bias"]
    a["ctxT"] = i["ctx_1024"].transpose(0, 2, 1)
    mask = i["mask_BxS2_bf1"].view(np.uint8)
    a["mask_row"], a["mask_col"] = mask.reshape(1, NB * P), mask.T
    col, row = np.arange(P)[None, :], np.arange(P)[:, None]
    a["causal"] = np.where(col <= row, 0.0, NEG).astype(np.float32)
    a["masks8"], a["masks16"] = ((row // n % 4 == np.arange(4)[None, :]).astype(np.float32) for n in (8, 16))
    a["part"] = np.concatenate([row < P - 16, row >= P - 16], 1).astype(np.float32)
    slots_ = lambda t, n: np.ascontiguousarray(t.transpose(1, 0, 2)).reshape(t.shape[1], n)
    a["l0f_idx_in"] = slots_(slices_in(cut_columns(i["L0_ffn_gate_idx"].T, 86),
                                       cut_columns(i["L0_ffn_up_idx"].T, 86)), 8 * 344)
    a["l0f_idx_down"] = slots_(i["L0_ffn_down_idx"].T.reshape(8, 86, D), 8 * D)
    a["l0f_lut"] = i["L0_ffn_lut"]
    a["l0a_qk"] = rows_in(cat([i["L0_attn_q_w"], i["L0_attn_k_w"]], 0).T)
    a["l0a_v"], a["l0a_o"] = rows_in(i["L0_attn_v_w"].T), rows_in(i["L0_attn_o_w"].T)
    a["l0a_bqk"] = cat([i["L0_attn_q_b"], i["L0_attn_k_b"]])
    a["l0a_bv"], a["l0a_bo"] = i["L0_attn_v_b"], i["L0_attn_o_b"]
    heads8 = row // 16
    a["own_head"] = cat([heads8 == col // 16, heads8 == np.arange(8)[None, :]], 1).astype(np.float32)
    a["pos"] = i["fside_BxSx2_0"].transpose(1, 0, 2)
    a["l0x_q"], a["l0x_kv"], a["l0x_o"] = (rows_in(i["L0_xattn_W" + n]) for n in ("q", "kv", "out"))
    a["l0x_bo"] = i["L0_xattn_bout"]
    cat1 = lambda names: cat([i[n] for n in names], -1)
    a["l1a_q"] = rows_in(cat1(["L1_attn_Wq", "L1_attn_Wk", "L1_attn_Wv"]))
    a["l1a_b"] = cat1(["L1_attn_bq", "L1_attn_bk", "L1_attn_bv"])
    a["l1a_o"], a["l1a_bo"] = i["L1_attn_Wo"], i["L1_attn_bo"]
    a["cos8"], a["sin8"] = rope_angles(16)
    c, s = a["cos8"], a["sin8"]
    a["cos16"], a["sin16"] = cat([c, c], 1), cat([s, -s], 1)
    a["l2a_q"] = rows_in(cat([i["L2_attn_Wq"], i["L2_attn_Wk"], i["L2_attn_Wv"]], 0).T)
    a["l2a_b"] = cat1(["L2_attn_bq", "L2_attn_bk", "L2_attn_bv"])
    a["l2a_o"], a["l2a_bo"] = rows_in(i["L2_attn_Wo"].T), i["L2_attn_bo"]
    a["l2a_gain"] = cat([i["L2_attn_q_gain"], np.ones(4, np.float32)])
    by_head = lambda w: w.reshape(-1, 2, 16, 16).transpose(0, 2, 1, 3).reshape(-1, 512)
    a["l2x_q"], a["l2x_o"], a["l2x_bo"] = rows_in(i["L2_xattn_Wq"]), rows_in(i["L2_xattn_Wo"]), i["L2_xattn_bo"]
    a["l2x_kv"] = cat([i["L2_xattn_Wk"], i["L2_xattn_Wv"], by_head(i["L2_xattn_Wkv_dca"])], 1)
    a["l2x_b"] = cat1(["L2_xattn_bq", "L2_xattn_bk", "L2_xattn_bv"])
    a["l2x_bd"] = cat([i["L2_xattn_bq"], by_head(i["L2_xattn_bkv_dca"])[0]])
    for n in "wb":
        a["l2x_" + n + "1"] = cat1(["L2_xattn_qn_" + n, "L2_xattn_kn_" + n])
        a["l2x_" + n + "2"] = cat1(["L2_xattn_qn_" + n, "L2_xattn_kn_dca_" + n])
    a["l1x_q"], a["l1x_k"], a["l1x_v"] = (rows_in(i["L1_xattn_W" + n]) for n in "qkv")
    a["l1x_o"] = rows_in(i["L1_xattn_Wo"])
    qkv = i["L3_attn_w_qkv"].T
    a["l3a_q"], a["l3a_k"], a["l3a_v"] = (rows_in(qkv[:, 2048 * n:2048 * (n + 1)]) for n in range(3))
    a["l3a_o"] = rows_in(i["L3_attn_w_out"].T)
    a["l3x_q"], a["l3x_k"], a["l3x_v"] = (rows_in(i["L3_xattn_W" + n]) for n in "qkv")
    a["l3x_o"] = rows_in(i["L3_xattn_Wo"])
    a["l3x_gq"], a["l3x_gk"] = i["L3_xattn_gq"], i["L3_xattn_gk"]
    c, s = rope_angles(P)
    a["l3a_cos"], a["l3a_sin"] = np.concatenate([c, c], 1), np.concatenate([-s, s], 1)
    return {k: np.ascontiguousarray(v) for k, v in a.items()}


def program(nc, a, out, layers):
    with ExitStack() as ctx:
        core = Core(nc, ctx, a)
        l1x_w, l1x_in, l1x_fetch = claim(nc, core, core.far, 0, "l1x", (
            (a["l1x_q"], P, (KD, 2048)), (a["l1x_k"], P, (1, 1024)), (a["l1x_v"], P, (1, 1024)),
            (a["l1x_o"], P, (16, D))))
        l3a_w, l3a_in, l3a_fetch = claim(nc, core, core.far, 0, "l3a", (
            (a["l3a_q"], P, (KD, 2048)), (a["l3a_k"], P, (KD, 2048)), (a["l3a_v"], P, (KD, 2048)),
            (a["l3a_o"], P, (16, D))))
        l3x_w, l3x_in, l3x_fetch = claim(nc, core, core.near, 0, "l3x", (
            (a["l3x_q"], P, (KD, 2048)), (a["l3x_k"], P, (1, 2048)), (a["l3x_v"], P, (1, 2048)),
            (a["l3x_o"], P, (16, D))))
        l0a_w, l0a_in, l0a_fetch = claim(nc, core, core.near, 0, "l0a", (
            (a["l0a_qk"], P, (KD, 512)), (a["l0a_v"], P, (KD, D)), (a["l0a_o"], P, (KD, D))))
        l0x_w, l0x_in, l0x_fetch = claim(nc, core, core.near, 2560, "l0x", (
            (a["l0x_q"], P, (KD, D)), (a["l0x_kv"], P, (1, 512)), (a["l0x_o"], P, (KD, D))))
        l1a_w, l1a_in, l1a_fetch = claim(nc, core, core.near, 4096, "l1a", (
            (a["l1a_q"], P, (KD, 384)), (a["l1a_o"], 64, (1, D))))
        l2a_w, l2a_in, l2a_fetch = claim(nc, core, core.near, 5120, "l2a", (
            (a["l2a_q"], P, (KD, 384)), (a["l2a_o"], P, (KD, D))))
        l2x_w, l2x_in, l2x_fetch = claim(nc, core, core.near, 6400, "l2x", (
            (a["l2x_q"], P, (KD, D)), (a["l2x_kv"], P, (2, 512)), (a["l2x_o"], P, (KD, D))))
        every, main, dca = slice(0, P), slice(0, P - 16), slice(P - 16, P)
        bc = lambda n, rows=P: a[n].partition_broadcast(rows)
        small = {
            "l0x": (dict(zip(("q", "kv", "o"), l0x_w)), l0x_in, "axial", 8 ** -0.5, {
                "masks": ([P, 4], F32, [(every, a["masks8"])]),
                "pos": ([P, NB, 2], F32, [(every, a["pos"].rearrange("p b q -> p (b q)"))]),
                "out_bias": ([P, D], F32, [(every, bc("l0x_bo"))])}, a["ctxT"]),
            "l1a": (dict(zip(("q", "o"), l1a_w)), l1a_in, "summed", 0.25, {
                "masks": ([P, 4], F32, [(every, a["masks16"])]),
                "causal": ([P, P], F32, [(every, a["causal"])]),
                "bias": ([P, 384], F32, [(every, bc("l1a_b"))]),
                "cos": ([P, 8], F32, [(every, a["cos8"])]), "sin": ([P, 8], F32, [(every, a["sin8"])]),
                "out_bias": ([P, D], F32, [(every, bc("l1a_bo"))])}),
            "l2a": (dict(zip(("q", "o"), l2a_w)), l2a_in, "grouped", 0.25, {
                "masks": ([P, 4], F32, [(every, a["masks16"])]),
                "causal": ([P, P], F32, [(every, a["causal"])]),
                "bias": ([P, 384], F32, [(every, bc("l2a_b"))]),
                "gain": ([P, 20], F32, [(every, bc("l2a_gain"))]),
                "cos": ([P, 16], F32, [(every, a["cos16"])]), "sin": ([P, 16], F32, [(every, a["sin16"])]),
                "out_bias": ([P, D], F32, [(every, bc("l2a_bo"))])}),
            "l2x": (dict(zip(("q", "kv", "o"), l2x_w)), l2x_in, "split", 0.25, {
                "masks": ([P, 4], F32, [(every, a["masks16"])]),
                "part": ([P, 2], F32, [(every, a["part"])]),
                "bias": ([P, 768], F32, [(main, bc("l2x_b", P - 16)), (dca, bc("l2x_bd", 16))]),
                "affine_w": ([P, 32], F32, [(main, bc("l2x_w1", P - 16)), (dca, bc("l2x_w2", 16))]),
                "affine_b": ([P, 32], F32, [(main, bc("l2x_b1", P - 16)), (dca, bc("l2x_b2", 16))]),
                "out_bias": ([P, D], F32, [(every, bc("l2x_bo"))])}, a["ctxT"]),
        }
        fetches = {"begin": [l0a_fetch, l0x_fetch, l1a_fetch, l2a_fetch, l2x_fetch, l1x_fetch], "l2f": [l3a_fetch, l3x_fetch]}
        first = layers[0]
        if first != LAYERS[0]:
            fetches = {"begin": [f for n, f in (("l0a", l0a_fetch), ("l0x", l0x_fetch), ("l1a", l1a_fetch), ("l2a", l2a_fetch), ("l2x", l2x_fetch),
                                                 ("l1x", l1x_fetch), ("l3a", l3a_fetch), ("l3x", l3x_fetch))
                                 if n in layers]}
        get = lambda n: fetches.get(n, ())
        load_constants(nc, core, a["x"], a["ident"], get("begin"))
        l0f_in = nc.dram_tensor("l0f_w_in", (8, P, 344), F32).ap()
        l0f_down = nc.dram_tensor("l0f_w_down", (8, 86, D), F32).ap()
        if "l0f" in layers:
            look_up_layer(nc, core, "lut", a["l0f_idx_in"], a["l0f_idx_down"], a["l0f_lut"], l0f_in, l0f_down)
        for name in layers:
            if name == "l0a":
                linear_attention_layer(nc, core, name, l0a_w, l0a_in, {
                    "qk_bias": (512, bc("l0a_bqk")), "v_bias": (D, bc("l0a_bv")), "out_bias": (D, bc("l0a_bo")),
                    "own_head": (136, a["own_head"])})
            if name == "l0f":
                ffn_layer(nc, core, name, l0f_in, l0f_down, 86, "silu")
            if name in small:
                small_attention_layer(nc, core, name, *small[name])
            elif name == "l1x":
                wide_attention_layer(nc, core, name, *l1x_w, l1x_in, 8, "direct", 128 ** -0.5, a["ctxT"],
                                     mask=(a["mask_row"], a["mask_col"]))
            elif name == "l3a":
                wide_attention_layer(nc, core, name, *l3a_w, l3a_in, 16, "rope", 128 ** -0.5,
                                     tables=(a["l3a_cos"], a["l3a_sin"]))
            elif name == "l3x":
                wide_attention_layer(nc, core, name, *l3x_w, l3x_in, 16, "rms", 128 ** -0.5, a["ctxT"],
                                     tables=(a["l3x_gq"], a["l3x_gk"]))
            elif name == "l1f":
                with Layer(nc, "l1p") as between:
                    placed = Placed(between, 32)
                    ffn_layer(nc, core, name, a["l1f_in"][32:, :, :], a["l1f_down"][32:, :, :], 128, "silu",
                              make_router(nc, core, a["l1f_router"], a["l1f_bias"], (a["falling32"], a["falling8"]),
                                          32, 8, 3, 4, 2.5, 1e-20, placed, a["below"]))
                    placed_experts_layer(nc, core, "l1e", a["l1f_in"], a["l1f_down"], placed, 32, CAPACITY,
                                         (a["place_iota"], a["token_iota"], a["token_number"]))
            elif name == "l2f":
                ffn_layer(nc, core, name, a["l2f_in"], a["l2f_down"], 88, "silu",
                          make_router(nc, core, a["l2f_router"], None, (a["falling8"],),
                                      8, 0, 0, 2, 1.0, 0.0, per=2), per=2, prefetch=get(name))
            elif name == "l3f":
                ffn_layer(nc, core, name, a["l3f_in"], a["l3f_down"], 128, "relu2",
                          make_router(nc, core, a["l3f_router"], a["l3f_bias"], (a["falling16"], a["falling4"]),
                                      16, 4, 2, 2, 1.0, 1e-20), prefetch=get(name))
        store_result(nc, core, out)


LAYERS = ["l0a", "l0x", "l0f", "l1a", "l1x", "l1f", "l2a", "l2x", "l2f", "l3a", "l3x", "l3f"]


def kernel(**inputs):
    import concourse.bacc as bacc
    from concourse.bass_utils import run_bass_kernel_spmd

    nc = bacc.Bacc("TRN2", target_bir_lowering=False, num_devices=1)
    arrays = lay_out({k: np.asarray(v) for k, v in inputs.items()})
    aps = {k: nc.dram_tensor(f"in_{k}", v.shape, mybir.dt.from_np(v.dtype), kind="ExternalInput").ap()
           for k, v in arrays.items()}
    out = nc.dram_tensor("out", (NB, P, D), F32, kind="ExternalOutput").ap()
    program(nc, aps, out, LAYERS)
    result = run_bass_kernel_spmd(nc, [{f"in_{k}": v for k, v in arrays.items()}], core_ids=[0])
    return result.results[0]["out"]
```
